# Optimizing a Trainium2 kernel written in Bass

```python
import numpy as np
import jax
import jax.numpy as jnp

def _softmax(x, axis=-1):
    return jax.nn.softmax(x, axis=axis)

def _gelu(x):
    return jax.nn.gelu(x, approximate=True)

def _silu(x):
    return jax.nn.silu(x)

def _sigmoid(x):
    return jax.nn.sigmoid(x)

def _layernorm(x, axis=-1, eps=1e-05):
    m = jnp.mean(x, axis=axis, keepdims=True)
    v = jnp.var(x, axis=axis, keepdims=True)
    return (x - m) / jnp.sqrt(v + eps)

def _scatter_add(tgt, idx, src, axis=0):
    return tgt.at[idx].add(src)

def _segment_sum(src, seg, n):
    return jax.ops.segment_sum(src, seg, n)
kernel_name = 'mk_flamingo_gated_d2_seqx_r8_0d72a5'

def setup_inputs(seed: int=0):
    np.random.seed(seed)
    _w = jnp.asarray

    def _rec_inputs():
        import jax
        import jax.numpy as jnp
        _rk = jax.random.key(seed)
        x = 4.136e-05 + 0.9999 * jax.random.normal(jax.random.fold_in(_rk, 1), (4, 256, 256), jnp.float32)
        _lenS = 256 - jax.random.randint(jax.random.fold_in(_rk, 7), (4,), 0, max(1, 256 // 4) + 1, jnp.int32)
        _lenS2 = 256 - jax.random.randint(jax.random.fold_in(_rk, 8), (4,), 0, max(1, 256 // 4) + 1, jnp.int32)
        _ctx_1024P = jax.random.normal(jax.random.fold_in(_rk, 11), (4, 16, 128), jnp.float32)
        _ctx_1024c = jax.random.dirichlet(jax.random.fold_in(_rk, 511), 0.3 * jnp.ones((16,), jnp.float32), (4, 256))
        _ctx_1024t = jnp.einsum('bsk,bkd->bsd', _ctx_1024c, _ctx_1024P)
        _ctx_1024t = _ctx_1024t * jax.lax.rsqrt(jnp.mean(jnp.square(_ctx_1024t)) + 1e-12) * 0.953939
        ctx_1024 = -0.000292821 + 1.00034 * (_ctx_1024t + 0.3 * jax.random.normal(jax.random.fold_in(_rk, 611), (4, 256, 128), jnp.float32))
        _g = jax.random.normal(jax.random.fold_in(_rk, 9001), (2, 2), jnp.float32)
        _g = jnp.sign(_g) * jnp.maximum(jnp.abs(_g), 1.0) + (_g == 0) * 1.0
        g_xattn = _g[0]
        g_ffn = _g[1]
        return (x, ctx_1024, g_xattn, g_ffn)
    x, ctx_1024, g_xattn, g_ffn = _rec_inputs()

    def _L0_xattn_setup():
        import jax, jax.numpy as jnp
        import numpy as np
        import math
        B, L, DM = (2, 256, 128)
        DS, DC, EXP = (16, 4, 2)
        DI = EXP * DM
        DR = math.ceil(DM / 16)
        DT_MIN, DT_MAX, DT_FLOOR = (0.001, 0.1, 0.0001)

        def _ssm_forward(hidden_states, z, in_proj_w, conv_w, conv_b, x_proj_w, dt_proj_w, dt_proj_b, A_log, D):
            b = hidden_states.shape[0]
            x = jnp.einsum('ed,bld->bel', in_proj_w, hidden_states)
            xp = jnp.pad(x, ((0, 0), (0, 0), (DC - 1, 0)))
            xc = jax.lax.conv_general_dilated(xp, conv_w[:, None, :], window_strides=(1,), padding='VALID', dimension_numbers=('NCH', 'OIH', 'NCH'), feature_group_count=DI)
            u = jax.nn.silu(xc + conv_b[None, :, None])
            x_dbl = jnp.einsum('ke,bel->bkl', x_proj_w, u)
            dt_lo = x_dbl[:, :DR]
            Bm = x_dbl[:, DR:DR + DS]
            Cm = x_dbl[:, DR + DS:]
            delta = jax.nn.softplus(jnp.einsum('er,brl->bel', dt_proj_w, dt_lo) + dt_proj_b[None, :, None])
            A = -jnp.exp(A_log)

            def step(state, xs):
                d_t, B_t, C_t, u_t = xs
                dA = jnp.exp(d_t[..., None] * A)
                state = state * dA + (d_t * u_t)[..., None] * B_t[:, None, :]
                y_t = jnp.einsum('ben,bn->be', state, C_t)
                return (state, y_t)
            xs = (jnp.moveaxis(delta, -1, 0), jnp.moveaxis(Bm, -1, 0), jnp.moveaxis(Cm, -1, 0), jnp.moveaxis(u, -1, 0))
            state0 = jnp.zeros((b, DI, DS), delta.dtype)
            _, ys = jax.lax.scan(step, state0, xs)
            y = jnp.moveaxis(ys, 0, -1)
            y = y + D[None, :, None] * u
            y = y * jax.nn.silu(z)
            return jnp.swapaxes(y, 1, 2)
        key = jax.random.key(seed)
        ks = jax.random.split(key, 8)
        hidden_states = jax.random.normal(ks[0], (B, L, DM), jnp.float32)
        z = jax.random.normal(ks[1], (B, DI, L), jnp.float32)
        in_proj_w = jax.random.normal(ks[2], (DI, DM), jnp.float32) * DM ** (-0.5)
        conv_w = jax.random.normal(ks[3], (DI, DC), jnp.float32) * DC ** (-0.5)
        conv_b = jnp.zeros((DI,), jnp.float32)
        x_proj_w = jax.random.normal(ks[4], (DR + 2 * DS, DI), jnp.float32) * DI ** (-0.5)
        dt_std = DR ** (-0.5)
        dt_proj_w = jax.random.uniform(ks[5], (DI, DR), jnp.float32, -dt_std, dt_std)
        dt = jnp.exp(jax.random.uniform(ks[6], (DI,), jnp.float32) * (math.log(DT_MAX) - math.log(DT_MIN)) + math.log(DT_MIN))
        dt = jnp.clip(dt, DT_FLOOR)
        dt_proj_b = dt + jnp.log(-jnp.expm1(-dt))
        A_log = jnp.log(jnp.broadcast_to(jnp.arange(1, DS + 1, dtype=jnp.float32), (DI, DS)))
        D = jnp.ones((DI,), jnp.float32)
        return dict(hidden_states=hidden_states, z=z, in_proj_w=in_proj_w, conv_w=conv_w, conv_b=conv_b, x_proj_w=x_proj_w, dt_proj_w=dt_proj_w, dt_proj_b=dt_proj_b, A_log=A_log, D=D)
    _L0_xattn_all = _L0_xattn_setup()
    _L0_xattn_in = {k: v for k, v in _L0_xattn_all.items() if k in ('in_proj_w', 'conv_w', 'conv_b', 'x_proj_w', 'dt_proj_w', 'dt_proj_b', 'A_log', 'D')}
    del _L0_xattn_all

    def _L0_ffn_setup():
        import jax, jax.numpy as jnp
        import numpy as np
        DIM = 256
        INNER = 4 * DIM
        EPS = 1e-05

        def simple_rms_norm(x):
            d = x.shape[-1]
            n = jnp.linalg.norm(x, axis=-1, keepdims=True)
            return x / jnp.maximum(n, 1e-12) * jnp.sqrt(jnp.asarray(d, x.dtype))

        def activation_quant(x):
            scale = 127.0 / jnp.clip(jnp.max(jnp.abs(x), axis=-1, keepdims=True), EPS)
            return jnp.clip(jnp.round(x * scale), -128, 127) / scale

        def weight_quant(w):
            scale = 1.0 / jnp.clip(jnp.mean(jnp.abs(w)), EPS)
            return jnp.clip(jnp.round(w * scale), -1, 1) / scale

        def ste(x, q):
            return x + jax.lax.stop_gradient(q - x)

        def bitlinear158(x, w):
            xn = simple_rms_norm(x)
            xq = ste(xn, activation_quant(xn))
            wq = ste(w, weight_quant(w))
            return jnp.einsum('bsi,oi->bso', xq, wq)
        key = jax.random.key(seed)
        k1, k2, k3 = jax.random.split(key, 3)
        x = jax.random.normal(k1, (4, 256, DIM), dtype=jnp.float32)
        w1 = jax.random.normal(k2, (INNER, DIM), dtype=jnp.float32) * DIM ** (-0.5)
        w2 = jax.random.normal(k3, (DIM, INNER), dtype=jnp.float32) * INNER ** (-0.5)
        return {'x': x, 'w1': w1, 'w2': w2}
    _L0_ffn_all = _L0_ffn_setup()
    _L0_ffn_in = {k: v for k, v in _L0_ffn_all.items() if k in ('w1', 'w2')}
    del _L0_ffn_all

    def _L1_xattn_setup():
        import jax, jax.numpy as jnp
        import numpy as np
        EPS = 1e-05

        def rmsnorm(x, g, eps=EPS):
            var = jnp.mean(jnp.square(x), axis=-1, keepdims=True)
            return x * jax.lax.rsqrt(var + eps) * g
        key = jax.random.key(seed)
        ks = jax.random.split(key, 8)
        B, Sq, Skv = (2, 512, 64)
        dim, cdim, H, D = (256, 128, 16, 128)
        inner = H * D
        s = lambda f: 1.0 / np.sqrt(f)
        return {'hidden_states': jax.random.normal(ks[0], (B, Sq, dim), jnp.float32), 'encoder_hidden_states': jax.random.normal(ks[1], (B, Skv, cdim), jnp.float32), 'Wq': jax.random.normal(ks[2], (dim, inner), jnp.float32) * s(dim), 'Wk': jax.random.normal(ks[3], (cdim, inner), jnp.float32) * s(cdim), 'Wv': jax.random.normal(ks[4], (cdim, inner), jnp.float32) * s(cdim), 'Wo': jax.random.normal(ks[5], (inner, dim), jnp.float32) * s(inner), 'gq': jnp.ones((D,), jnp.float32), 'gk': jnp.ones((D,), jnp.float32)}
    _L1_xattn_all = _L1_xattn_setup()
    _L1_xattn_in = {k: v for k, v in _L1_xattn_all.items() if k in ('Wq', 'Wk', 'Wv', 'Wo', 'gq', 'gk')}
    del _L1_xattn_all

    def _L1_ffn_setup():
        import jax, jax.numpy as jnp
        import numpy as np
        B, S, H = (2, 128, 256)
        E, K, F = (8, 2, 176)
        N_SHARED = 2
        FS = F * N_SHARED
        ROUTED_SCALE = 1.0

        def _swiglu_mlp(x, wg, wu, wd):
            return jax.nn.silu(x @ wg.T) * (x @ wu.T) @ wd.T
        key = jax.random.key(seed)
        ks = jax.random.split(key, 8)

        def w(k, shape, fan_in):
            return jax.random.normal(k, shape, jnp.float32) * (1.0 / np.sqrt(fan_in))
        return {'hidden_states': jax.random.normal(ks[0], (B, S, H), jnp.float32), 'gate_weight': w(ks[1], (E, H), H), 'w_gate': w(ks[2], (E, F, H), H), 'w_up': w(ks[3], (E, F, H), H), 'w_down': w(ks[4], (E, H, F), F), 'sw_gate': w(ks[5], (FS, H), H), 'sw_up': w(ks[6], (FS, H), H), 'sw_down': w(ks[7], (H, FS), FS)}
    _L1_ffn_all = _L1_ffn_setup()
    _L1_ffn_in = {k: v for k, v in _L1_ffn_all.items() if k in ('gate_weight', 'w_gate', 'w_up', 'w_down', 'sw_gate', 'sw_up', 'sw_down')}
    del _L1_ffn_all
    return {'x': x, 'ctx_1024': ctx_1024, 'g_xattn': g_xattn, 'g_ffn': g_ffn, 'L0_xattn_in_proj_w': _L0_xattn_in['in_proj_w'], 'L0_xattn_conv_w': _L0_xattn_in['conv_w'], 'L0_xattn_conv_b': _L0_xattn_in['conv_b'], 'L0_xattn_x_proj_w': _L0_xattn_in['x_proj_w'], 'L0_xattn_dt_proj_w': _L0_xattn_in['dt_proj_w'], 'L0_xattn_dt_proj_b': _L0_xattn_in['dt_proj_b'], 'L0_xattn_A_log': _L0_xattn_in['A_log'], 'L0_xattn_D': _L0_xattn_in['D'], 'L0_ffn_w1': _L0_ffn_in['w1'], 'L0_ffn_w2': _L0_ffn_in['w2'], 'L1_xattn_Wq': _L1_xattn_in['Wq'], 'L1_xattn_Wk': _L1_xattn_in['Wk'], 'L1_xattn_Wv': _L1_xattn_in['Wv'], 'L1_xattn_Wo': _L1_xattn_in['Wo'], 'L1_xattn_gq': _L1_xattn_in['gq'], 'L1_xattn_gk': _L1_xattn_in['gk'], 'L1_ffn_gate_weight': _L1_ffn_in['gate_weight'], 'L1_ffn_w_gate': _L1_ffn_in['w_gate'], 'L1_ffn_w_up': _L1_ffn_in['w_up'], 'L1_ffn_w_down': _L1_ffn_in['w_down'], 'L1_ffn_sw_gate': _L1_ffn_in['sw_gate'], 'L1_ffn_sw_up': _L1_ffn_in['sw_up'], 'L1_ffn_sw_down': _L1_ffn_in['sw_down']}

def reference(x, ctx_1024, g_xattn, g_ffn, L0_xattn_in_proj_w, L0_xattn_conv_w, L0_xattn_conv_b, L0_xattn_x_proj_w, L0_xattn_dt_proj_w, L0_xattn_dt_proj_b, L0_xattn_A_log, L0_xattn_D, L0_ffn_w1, L0_ffn_w2, L1_xattn_Wq, L1_xattn_Wk, L1_xattn_Wv, L1_xattn_Wo, L1_xattn_gq, L1_xattn_gk, L1_ffn_gate_weight, L1_ffn_w_gate, L1_ffn_w_up, L1_ffn_w_down, L1_ffn_sw_gate, L1_ffn_sw_up, L1_ffn_sw_down):
    import jax
    import jax.numpy as jnp

    def _L0_xattn_ref(hidden_states, z, in_proj_w, conv_w, conv_b, x_proj_w, dt_proj_w, dt_proj_b, A_log, D):
        import jax, jax.numpy as jnp
        import numpy as np
        import math
        B, L, DM = (2, 256, 128)
        DS, DC, EXP = (16, 4, 2)
        DI = EXP * DM
        DR = math.ceil(DM / 16)
        DT_MIN, DT_MAX, DT_FLOOR = (0.001, 0.1, 0.0001)

        def _ssm_forward(hidden_states, z, in_proj_w, conv_w, conv_b, x_proj_w, dt_proj_w, dt_proj_b, A_log, D):
            b = hidden_states.shape[0]
            x = jnp.einsum('ed,bld->bel', in_proj_w, hidden_states)
            xp = jnp.pad(x, ((0, 0), (0, 0), (DC - 1, 0)))
            xc = jax.lax.conv_general_dilated(xp, conv_w[:, None, :], window_strides=(1,), padding='VALID', dimension_numbers=('NCH', 'OIH', 'NCH'), feature_group_count=DI)
            u = jax.nn.silu(xc + conv_b[None, :, None])
            x_dbl = jnp.einsum('ke,bel->bkl', x_proj_w, u)
            dt_lo = x_dbl[:, :DR]
            Bm = x_dbl[:, DR:DR + DS]
            Cm = x_dbl[:, DR + DS:]
            delta = jax.nn.softplus(jnp.einsum('er,brl->bel', dt_proj_w, dt_lo) + dt_proj_b[None, :, None])
            A = -jnp.exp(A_log)

            def step(state, xs):
                d_t, B_t, C_t, u_t = xs
                dA = jnp.exp(d_t[..., None] * A)
                state = state * dA + (d_t * u_t)[..., None] * B_t[:, None, :]
                y_t = jnp.einsum('ben,bn->be', state, C_t)
                return (state, y_t)
            xs = (jnp.moveaxis(delta, -1, 0), jnp.moveaxis(Bm, -1, 0), jnp.moveaxis(Cm, -1, 0), jnp.moveaxis(u, -1, 0))
            state0 = jnp.zeros((b, DI, DS), delta.dtype)
            _, ys = jax.lax.scan(step, state0, xs)
            y = jnp.moveaxis(ys, 0, -1)
            y = y + D[None, :, None] * u
            y = y * jax.nn.silu(z)
            return jnp.swapaxes(y, 1, 2)
        return _ssm_forward(hidden_states, z, in_proj_w, conv_w, conv_b, x_proj_w, dt_proj_w, dt_proj_b, A_log, D)

    def _L0_ffn_ref(x, w1, w2):
        import jax, jax.numpy as jnp
        import numpy as np
        DIM = 256
        INNER = 4 * DIM
        EPS = 1e-05

        def simple_rms_norm(x):
            d = x.shape[-1]
            n = jnp.linalg.norm(x, axis=-1, keepdims=True)
            return x / jnp.maximum(n, 1e-12) * jnp.sqrt(jnp.asarray(d, x.dtype))

        def activation_quant(x):
            scale = 127.0 / jnp.clip(jnp.max(jnp.abs(x), axis=-1, keepdims=True), EPS)
            return jnp.clip(jnp.round(x * scale), -128, 127) / scale

        def weight_quant(w):
            scale = 1.0 / jnp.clip(jnp.mean(jnp.abs(w)), EPS)
            return jnp.clip(jnp.round(w * scale), -1, 1) / scale

        def ste(x, q):
            return x + jax.lax.stop_gradient(q - x)

        def bitlinear158(x, w):
            xn = simple_rms_norm(x)
            xq = ste(xn, activation_quant(xn))
            wq = ste(w, weight_quant(w))
            return jnp.einsum('bsi,oi->bso', xq, wq)
        h = jax.nn.gelu(bitlinear158(x, w1), approximate=False)
        h = jax.nn.gelu(h, approximate=False)
        return bitlinear158(h, w2)

    def _L1_xattn_ref(hidden_states, encoder_hidden_states, Wq, Wk, Wv, Wo, gq, gk):
        import jax, jax.numpy as jnp
        import numpy as np
        EPS = 1e-05

        def rmsnorm(x, g, eps=EPS):
            var = jnp.mean(jnp.square(x), axis=-1, keepdims=True)
            return x * jax.lax.rsqrt(var + eps) * g
        B, Sq, _ = hidden_states.shape
        Skv = encoder_hidden_states.shape[1]
        D = gq.shape[0]
        H = Wq.shape[1] // D
        scale = 1.0 / np.sqrt(D)
        q = (hidden_states @ Wq).reshape(B, Sq, H, D)
        k = (encoder_hidden_states @ Wk).reshape(B, Skv, H, D)
        v = (encoder_hidden_states @ Wv).reshape(B, Skv, H, D)
        q = rmsnorm(q, gq)
        k = rmsnorm(k, gk)
        scores = jnp.einsum('bqhd,bkhd->bhqk', q, k) * scale
        attn = jax.nn.softmax(scores, axis=-1)
        out = jnp.einsum('bhqk,bkhd->bqhd', attn, v)
        out = out.reshape(B, Sq, H * D)
        return out @ Wo

    def _L1_ffn_ref(hidden_states, gate_weight, w_gate, w_up, w_down, sw_gate, sw_up, sw_down):
        import jax, jax.numpy as jnp
        import numpy as np
        B, S, H = (2, 128, 256)
        E, K, F = (8, 2, 176)
        N_SHARED = 2
        FS = F * N_SHARED
        ROUTED_SCALE = 1.0

        def _swiglu_mlp(x, wg, wu, wd):
            return jax.nn.silu(x @ wg.T) * (x @ wu.T) @ wd.T
        b, s, h = hidden_states.shape
        x = hidden_states.reshape(-1, h)
        T = x.shape[0]
        logits = x.astype(jnp.float32) @ gate_weight.astype(jnp.float32).T
        scores = jax.nn.softmax(logits, axis=-1)
        topk_w, topk_idx = jax.lax.top_k(scores, K)
        topk_w = topk_w / (jnp.sum(topk_w, axis=-1, keepdims=True) + 1e-20)
        topk_w = topk_w * ROUTED_SCALE
        cw = jnp.zeros((T, E), jnp.float32).at[jnp.arange(T)[:, None], topk_idx].add(topk_w)
        g = jax.nn.silu(jnp.einsum('th,efh->tef', x, w_gate)) * jnp.einsum('th,efh->tef', x, w_up)
        expert_out = jnp.einsum('tef,ehf->teh', g, w_down)
        y = jnp.einsum('te,teh->th', cw, expert_out).reshape(b, s, h)
        y = y + _swiglu_mlp(x, sw_gate, sw_up, sw_down).reshape(b, s, h)
        return y
    x = x + jnp.tanh(g_xattn[0]) * _L0_xattn_ref(ctx_1024, _layernorm(x, axis=-1), L0_xattn_in_proj_w, L0_xattn_conv_w, L0_xattn_conv_b, L0_xattn_x_proj_w, L0_xattn_dt_proj_w, L0_xattn_dt_proj_b, L0_xattn_A_log, L0_xattn_D)
    x = x + jnp.tanh(g_ffn[0]) * _L0_ffn_ref(_layernorm(x, axis=-1), L0_ffn_w1, L0_ffn_w2)
    x = x + jnp.tanh(g_xattn[1]) * _L1_xattn_ref(_layernorm(x, axis=-1), ctx_1024, L1_xattn_Wq, L1_xattn_Wk, L1_xattn_Wv, L1_xattn_Wo, L1_xattn_gq, L1_xattn_gk)
    x = x + jnp.tanh(g_ffn[1]) * _L1_ffn_ref(_layernorm(x, axis=-1), L1_ffn_gate_weight, L1_ffn_w_gate, L1_ffn_w_up, L1_ffn_w_down, L1_ffn_sw_gate, L1_ffn_sw_up, L1_ffn_sw_down)
    return x

_drawn_inputs = setup_inputs


def setup_inputs(seed=0):
    import zlib

    import numpy as np

    out = dict(_drawn_inputs(seed))
    spreads = {'g_ffn': (-1.0, 0.2),
     'L0_xattn_conv_b': (0.0, 0.1),
     'L0_xattn_D': (1.0, 0.2),
     'L1_xattn_gq': (1.0, 0.2),
     'L1_xattn_gk': (1.0, 0.2)}
    factors = {'L0_xattn_dt_proj_w': 2.787}
    for name, (base, spread) in spreads.items():
        noise = np.random.default_rng([zlib.crc32(name.encode()), seed]).standard_normal(out[name].shape)
        drawn = base * np.exp(spread * noise) if base else spread * noise
        out[name] = jnp.asarray(drawn.astype(out[name].dtype))
    for name, factor in factors.items():
        out[name] = (out[name] * factor).astype(out[name].dtype)
    return out
```

```python
from contextlib import ExitStack

import numpy as np

import concourse.bass as bass
from concourse import mybir

F32 = mybir.dt.float32
F32R = mybir.dt.float32r
BF16 = mybir.dt.bfloat16
U32 = mybir.dt.uint32
ALU = mybir.AluOpType
ACT = mybir.ActivationFunctionType
AX = mybir.AxisListType

P = 128
B, S, DM = 4, 256, 256
DC = 128
T = B * S
NT = T // P
DI, NS, TAPS, DR = 256, 16, 4, 8
PAD = 4
CH = P // NS
ST = DI // CH
JT = P // CH
INNER = 1024
FT0 = INNER // P
H = 16
E, F, FS = 8, 176, 352
FALL = E * F + FS
FT = -(-FALL // P)
FTR = E * F // P
EPS = 1e-5
MAGIC = 12582912.0
NSUM_LAG = 3
PIECE_LAG = 2
FIRST_HEAD = 6
PT_LAG, U_LAG = 2, 3
GRP = 4
RING = 3


def build(nc, d):
    with ExitStack() as ctx:
        def sb(name, shape, dt=F32):
            return ctx.enter_context(nc.sbuf_tensor(name, shape, dt))

        def sem(name):
            return ctx.enter_context(nc.semaphore(name))

        ps = ctx.enter_context(nc.psum_tensor("ps", [P, 8, 512], F32))

        x = sb("x", [P, NT, DM])
        ctxn = sb("ctxn", [P, NT, DC])
        ctxH = sb("ctxH", [P, B, PAD + S], F32R)
        ctxL = sb("ctxL", [P, B, PAD + S], F32R)
        inT = sb("inT", [P, DI])
        cstage = sb("cstage", [P, 2048])
        u = sb("u", [P, 2, T])
        xp = sb("xp", [P, 2, 2 * P + DR])
        bcz = sb("bcz", [P, 4096])
        rA = sb("rA", [P, 8192], F32R)
        rK = sb("rK", [P, 4096], F32R)
        sel = sb("sel", [P, 8, P], F32R)
        nwin = sb("nwin", [P, 2 * P - CH])
        work = sb("work", [P, 9216])
        stage = sb("stage", [P, 6144])
        w12q = sb("w12q", [P, 2, 2048], BF16)
        G = sb("G", [P, H, DM])
        xT = sb("xT", [P, 2, 2, 2, S], F32R)
        ident = sb("ident", [P, P])
        identb = sb("identb", [P, P], BF16)
        ones = sb("ones", [P, P])
        small = sb("small", [P, 64])
        acol = sb("acol", [P, ST])
        nacol = sb("nacol", [P, ST])
        dtw = sb("dtw", [DR, DI])
        ec = sb("ec", [P, 2, 3])
        gates = sb("gates", [P, 4])
        tg = sb("tg", [P, 4])
        gqk = sb("gqk", [P, 2])
        gkq = sb("gkq", [P, 1])
        st6 = sb("st6", [P, NT, 6])
        mv = sb("mv", [P, NT, 2])
        ve = sb("ve", [P, NT])
        rstd = sb("rstd", [P, NT])
        nb8 = sb("nb8", [P, NT])
        phalf = sb("phalf", [P, 32])
        nhalf = sb("nhalf", [P, 32])
        q8 = sb("q8", [P, 10, NT])
        wsum = sb("wsum", [P, 2])
        mw = sb("mw", [P, 2])
        iw = sb("iw", [P, 2])
        k2 = sb("k2", [P, 1])
        rr = sb("rr", [P, 4, GRP])
        rv = sb("rv", [P, 4, GRP])
        rq = sb("rq", [P, RING, GRP, 2])
        hs = sb("hs", [P, 4, 8])
        gw = sb("gw", [P, 2, E])
        gwH = sb("gwH", [P, 2, E], F32R)
        gwL = sb("gwL", [P, 2, E], F32R)
        iota8 = sb("iota8", [P, E])
        cwR = sb("cwR", [P, NT, E], F32R)
        rti = sb("rti", [P, NT, E], U32)

        cwb = cstage[:, 0:TAPS * DI].rearrange("p (j e) -> p j e", j=TAPS)
        wc = cstage[:, 1024:2048].rearrange("p (j e) -> p j e", j=TAPS)
        wcH = rK[:, 0:1024].rearrange("p (j e) -> p j e", j=TAPS)
        wcL = rK[:, 2048:3072].rearrange("p (j e) -> p j e", j=TAPS)
        Bs, Cs = bcz[:, 0:T], bcz[:, T:2 * T]
        sz = bcz[:, 2 * T:4 * T].rearrange("p (i l) -> p i l", i=NT)
        XD = rA[:, 0:4096].rearrange("p (s t) -> p s t", s=4)
        XU = rA[:, 4096:8192].rearrange("p (s t) -> p s t", s=4)
        ctxTr = work[:, 0:T]
        selr = work[:, T:2 * T].rearrange("p (j m) -> p j m", j=8)
        dlt = work[:, 2048:4096].rearrange("p (t n) -> p t n", t=2)
        dab = work[:, 4096:6144].rearrange("p (t n) -> p t n", t=2)
        dex = work[:, 6144:8192].rearrange("p (t n) -> p t n", t=2)
        dtl = work[0:DR, 8192:9216]
        dA = [work[:, i * T:(i + 1) * T] for i in (0, 1)]
        dBu = [work[:, i * T:(i + 1) * T] for i in (2, 3)]
        hb = [work[:, i * T:(i + 1) * T] for i in (4, 5)]
        hC = [work[:, i * T:(i + 1) * T] for i in (6, 7, 8)]
        wraw = [stage[:, 0:2048], stage[:, 2048:4096]]
        yg = stage[:, 4096:6144].rearrange("p (t n) -> p t n", t=2)
        xl = stage[:, 4096:6144].rearrange("p (i c) -> p i c", i=NT)
        g1 = [work[:, 0:1024], work[:, 1024:2048]]
        g2 = [work[:, 2048:3072], work[:, 3072:4096]]
        hq = [work[:, 4096 + 512 * i:4608 + 512 * i].bitcast(BF16) for i in (0, 1)]
        hT = [work[:, 5120 + 512 * i:5632 + 512 * i].bitcast(BF16).rearrange("p (k t) -> p k t", k=FT0) for i in (0, 1)]
        xq = work[:, 6144:7168].bitcast(BF16).rearrange("p (i c) -> p i c", i=NT)
        xqT = work[:, 7168:8192].bitcast(BF16).rearrange("p (k t) -> p k t", k=2)
        sqj = work[:, 8192:9216]
        w1q = w12q[:, 0, :].rearrange("p (k f) -> p k f", k=2)
        w2q = w12q[:, 1, :].rearrange("p (k o) -> p k o", k=FT0)
        Wqr = stage[:, 0:4096]
        Wkr = cstage[:, 0:2048]
        WqH = rA[:, 0:4096].rearrange("p (k n) -> p k n", k=2)
        WqL = rA[:, 4096:8192].rearrange("p (k n) -> p k n", k=2)
        WkH, WkL = rK[:, 0:2048], rK[:, 2048:4096]
        WvT = u[:, :, :].rearrange("p a (h c) -> p (a h) c", c=DC)
        Wo = bcz[:, :].rearrange("p (h o) -> p h o", h=H)
        kT = stage[:, 0:3072].rearrange("p (g h t) -> p g h t", g=RING, h=GRP)
        qT = stage[:, 3072:6144].rearrange("p (g h t) -> p g h t", g=RING, h=GRP)
        praw = [work[:, 512 * i:512 * i + 512] for i in range(4)]
        psq = [work[:, 2048 + 512 * i:2560 + 512 * i] for i in range(2)]
        Pb = [work[:, 3072 + 512 * i:3584 + 512 * i].rearrange("p (q k) -> p q k", q=2) for i in range(4)]
        PT = [work[:, 5120 + 512 * i:5632 + 512 * i].rearrange("p (k q) -> p k q", k=2) for i in range(3)]
        Us = [work[:, 6656 + 256 * i:6912 + 256 * i] for i in range(3)]
        xn = work[:, 7424:7936].rearrange("p (i c) -> p i c", i=2)
        xmH = rA[:, 0:2048].rearrange("p (k t) -> p k t", k=2)
        xmL = rA[:, 2048:4096].rearrange("p (k t) -> p k t", k=2)
        esel = xT[0:64].rearrange("p a b k t -> p (a b k t)")[:, 0:FTR * P]
        rt = work[:, 7168:7552].rearrange("p (i a e) -> p i a e", i=NT, a=6)
        cwHL = work[:, 7936:8448].rearrange("p (i m) -> p i m", i=NT)
        cwT = rA[0:64, 7168:8192]
        wr = [bcz[:, 768 * i:768 * i + 768] for i in range(4)]
        wH = [rA[:, 4096 + 1536 * i:4864 + 1536 * i] for i in range(2)]
        wL = [rA[:, 4864 + 1536 * i:5632 + 1536 * i] for i in range(2)]
        hH = [rK[:, 1024 * i:1024 * i + 512] for i in range(3)]
        hL = [rK[:, 1024 * i + 512:1024 * i + 1024] for i in range(3)]
        sg = [work[:, 512 * i:512 * i + 512] for i in range(2)]
        hm = [work[:, 1024 + 512 * i:1536 + 512 * i] for i in range(2)]
        xm = work[:, 4096:4608].rearrange("p (i c) -> p i c", i=2)
        yo = [work[:, 5120 + 512 * i:5632 + 512 * i].rearrange("p (i c) -> p i c", i=2) for i in range(4)]

        s = {}
        for name in ("ld_ctxT ld_wc ld_x ld_sel ld_xp ld_small ld_w ld_ctxn ld_wq ld_wk ld_wo ld_moe0 ld_moe1 ld_moe2 "
                     "ld_moe3 ld_esel ld_out "
                     "pool_init ctx_split conv_w sel_ready conv_done u_done zstat zpow znb sz_done xproj_done "
                     "bcd_evac dpre_done dact ddve dhi_done dlo_done "
                     "wabs wsum_done wq_stat wq_done nacol_done gate_done "
                     "dbc_done ubc_done exp_done dbu_done scan_done hc_done nsum_done yevac yg_done yT_done x1_done "
                     "fst fpow fxl fsc fq fqT_done fqT_evac mm1_done fact famax fpow2 fch fhq fT_done fT_evac mm2_done x2_done "
                     "G_done G_evac wk_split wqh wql "
                     "aln apow axn axT_done axTH axTL piece_done raw_done psq_done prs prv_done pnorm pT_done pT_evac gkq_done "
                     "sc_done hmax exps hrec pnorm_done PT_done PT_evac U_done U_evac y_done x3_done "
                     "mln mpow mxn mxT_done mxTH mxTL wsplit wsplitL gws rl_done rexp rdve cwT_done cwT_evac "
                     "gate_mm up_mm cw_mm silu_done m1_done m2_done hH_done hL_done down_done out_done").split():
            s[name] = sem(name)
        block = ctx.enter_context(nc.Block())

        @block.sync
        def _(sp):
            sp.dma_start(ctxTr, d["ctxT"]).then_inc(s["ld_ctxT"], 16)
            sp.dma_start(inT[:, :], d["inT"]).then_inc(s["ld_wc"], 16)
            sp.dma_start(cstage[:, 0:1024], d["cw"].partition_broadcast(P)).then_inc(s["ld_wc"], 16)
            sp.dma_start(ec[:, :, :], d["ec"]).then_inc(s["ld_small"], 16)
            sp.dma_start(gates[:, :], d["gates"].partition_broadcast(P)).then_inc(s["ld_small"], 16)
            sp.dma_start(x[:, :, :], d["x"].rearrange("b (h p) c -> p (b h) c", p=P)).then_inc(s["ld_x"], 16)
            sp.dma_start(xp[:, :, :], d["xp"]).then_inc(s["ld_xp"], 16)
            sp.dma_start(dtw[:, :], d["dtw"]).then_inc(s["ld_small"], 16)
            sp.dma_start(acol[:, :], d["acol"]).then_inc(s["ld_small"], 16)
            sp.dma_start(gqk[:, :], d["gqk"]).then_inc(s["ld_small"], 16)
            sp.dma_start(selr, d["sel"]).then_inc(s["ld_sel"], 16)
            sp.dma_start(nwin[:, :], d["nwin"]).then_inc(s["ld_sel"], 16)
            sp.dma_start(ident[:, :], d["ident"]).then_inc(s["ld_sel"], 16)
            sp.dma_start(wraw[0], d["w1"]).then_inc(s["ld_w"], 16)
            sp.dma_start(wraw[1], d["w2"]).then_inc(s["ld_w"], 16)
            sp.dma_start(ctxn[:, :, :], d["ctx"].rearrange("b (h p) c -> p (b h) c", p=P)).then_inc(s["ld_ctxn"], 16)
            sp.dma_start(gw[:, :, :], d["gw"]).then_inc(s["ld_ctxn"], 16)
            sp.dma_start(iota8[:, :], d["iota8"]).then_inc(s["ld_ctxn"], 16)
            sp.wait_ge(s["conv_w"], 3)
            sp.dma_start(Wkr, d["Wk"]).then_inc(s["ld_wk"], 16)
            sp.wait_ge(s["wq_done"], 6)
            sp.dma_start(Wqr, d["Wq"]).then_inc(s["ld_wq"], 16)
            sp.wait_ge(s["yg_done"], 2)
            sp.dma_start(u[:, :, :], d["WvT"].rearrange("p (a n) -> p a n", a=2)).then_inc(s["ld_wo"], 16)
            sp.dma_start(bcz[:, :], d["Wo"]).then_inc(s["ld_wo"], 16)
            sp.wait_ge(s["G_done"], H // 2)
            for i in range(FT):
                if i >= 4:
                    sp.wait_ge(s["wsplitL"], i - 3)
                sp.dma_start(wr[i % 4], d["moe"][i]).then_inc(s[f"ld_moe{i % 4}"], 16)
            for b in range(B):
                sp.wait_ge(s["out_done"], 2 * b + 2)
                sp.dma_start(d["out"][b].rearrange("(h p) c -> p h c", p=P), yo[b]).then_inc(s["ld_out"], 16)
            sp.wait_ge(s["ld_out"], 16 * B)

        def three(pe, out, pairs):
            terms = [(a, r) for aH, aL, rH, rL in pairs for a, r in ((aH, rH), (aH, rL), (aL, rH))]
            for n, (a, r) in enumerate(terms):
                last = pe.matmul(out, a, r, start=(n == 0), stop=(n == len(terms) - 1))
            return last

        @block.tensor
        def _(pe):
            pe.wait_ge(s["ctx_split"], 2)
            pe.wait_ge(s["pool_init"], 5)
            pe.wait_ge(s["conv_w"], 3)
            for et in range(2):
                for hf in range(2):
                    pairs = []
                    for j in range(TAPS):
                        c0 = PAD - (TAPS - 1) + j
                        w_ = slice(et * P, et * P + P)
                        pairs.append((wcH[:, j, w_], wcL[:, j, w_], ctxH[:, 2 * hf:2 * hf + 2, c0:c0 + S],
                                      ctxL[:, 2 * hf:2 * hf + 2, c0:c0 + S]))
                    three(pe, ps[:, 2 * et + hf, :], pairs).then_inc(s["conv_done"], 1)
            pe.wait_ge(s["ld_xp"], 16)
            pe.wait_ge(s["u_done"], 4)
            for n, (c0, m) in enumerate(((0, P), (P, P), (2 * P, DR))):
                for hf in range(2):
                    bank = (4, 6, 0)[n] + hf
                    for k in range(2):
                        last = pe.matmul(ps[0:m, bank, :], xp[:, k, c0:c0 + m], u[:, k, 512 * hf:512 * hf + 512],
                                         start=(k == 0), stop=(k == 1))
                    last.then_inc(s["xproj_done"], 1)
            pe.wait_ge(s["ld_small"], 80)
            for et in range(2):
                for hf in range(2):
                    pe.wait_ge(s["bcd_evac"], (2 if et == 0 else 6))
                    if et == 0 and hf == 0:
                        pe.wait_ge(s["bcd_evac"], 2)
                    pe.matmul(ps[:, 2 + 2 * et + hf, :], dtw[:, et * P:et * P + P], dtl[:, 512 * hf:512 * hf + 512],
                              start=True, stop=True).then_inc(s["dpre_done"], 1)
            pe.wait_ge(s["wabs"], 2)
            pe.matmul(ps[:, 7, 0:2], ones[:, :], wsum[:, :], start=True, stop=True).then_inc(s["wsum_done"], 1)

            def nsum(t):
                et, jj = divmod(t, JT)
                pe.wait_ge(s["hc_done"], t + 1)
                if t == JT:
                    pe.wait_ge(s["yevac"], 1)
                for hf in range(2):
                    last = pe.matmul(ps[:, 6 + hf, :], nwin[:, P - CH - CH * jj:2 * P - CH - CH * jj],
                                     hC[t % 3][:, 512 * hf:512 * hf + 512], start=(jj == 0), stop=(jj == JT - 1))
                last.then_inc(s["nsum_done"], 1)

            pe.wait_ge(s["dlo_done"], 8)
            pe.wait_ge(s["sel_ready"], 1)
            pe.wait_ge(s["wq_stat"], 1)
            for t in range(ST):
                g, j = divmod(t, 8)
                if t >= 1:
                    pe.wait_ge(s["exp_done"], t)
                for hf in range(2):
                    last = pe.matmul(ps[:, hf, :], sel[:, j, :], XD[:, g, 512 * hf:512 * hf + 512], start=True, stop=True)
                last.then_inc(s["dbc_done"], 1)
                if t >= 2:
                    pe.wait_ge(s["dbu_done"], t - 1)
                for hf in range(2):
                    last = pe.matmul(ps[:, 2 + 2 * (t % 2) + hf, :], sel[:, j, :], XU[:, g, 512 * hf:512 * hf + 512],
                                     start=True, stop=True)
                last.then_inc(s["ubc_done"], 1)
                if t >= NSUM_LAG:
                    nsum(t - NSUM_LAG)
            for t in range(ST - NSUM_LAG, ST):
                nsum(t)
            pe.wait_ge(s["exp_done"], ST)
            pe.wait_ge(s["dbu_done"], ST)
            for et in range(2):
                pe.wait_ge(s["yg_done"], et + 1)
                for b in range(B):
                    for lh in range(2):
                        last = pe.transpose(ps[:, b, lh * DM + et * P:lh * DM + et * P + P],
                                            yg[:, et, b * S + lh * P:b * S + lh * P + P], ident[:, :])
                    last.then_inc(s["yT_done"], 1)
            pe.wait_ge(s["fq"], NT + 1)
            pe.wait_ge(s["x1_done"], B)
            for k in range(2):
                for i in range(NT):
                    last = pe.transpose(ps[:, k, :].bitcast(BF16)[:, i * P:i * P + P], xq[:, i, k * P:k * P + P], identb[:, :])
                last.then_inc(s["fqT_done"], 1)

            def mm1(i):
                if i == 0:
                    pe.wait_ge(s["fqT_evac"], 2)
                    pe.wait_ge(s["wq_done"], 6)
                    pe.wait_ge(s["yevac"], 2)
                if i >= 2:
                    pe.wait_ge(s["fact"], 3 * (i - 2) + 1)
                for n in range(2):
                    for k in range(2):
                        last = pe.matmul(ps[:, 4 + 2 * (i % 2) + n, :], xqT[:, k, i * P:i * P + P],
                                         w1q[:, k, 512 * n:512 * n + 512], start=(k == 0), stop=(k == 1))
                last.then_inc(s["mm1_done"], 1)

            mm1(0)
            for i in range(NT):
                if i + 1 < NT:
                    mm1(i + 1)
                pe.wait_ge(s["fhq"], 2 * i + 2)
                if i >= 2:
                    pe.wait_ge(s["fT_evac"], i - 1)
                for k in range(FT0):
                    last = pe.transpose(ps[:, 2 + i % 2, :].bitcast(BF16)[:, k * P:k * P + P], hq[i % 2][:, k * P:k * P + P],
                                        identb[:, :])
                last.then_inc(s["fT_done"], 1)
                pe.wait_ge(s["fT_evac"], i + 1)
                if i >= 2:
                    pe.wait_ge(s["x2_done"], i - 1)
                for k in range(FT0):
                    last = pe.matmul(ps[:, i % 2, 0:DM], hT[i % 2][:, k, :], w2q[:, k, :], start=(k == 0), stop=(k == FT0 - 1))
                last.then_inc(s["mm2_done"], 1)
            pe.wait_ge(s["ld_wo"], 32)
            pe.wait_ge(s["fact"], 3 * NT)
            for n in range(H // 2):
                if n >= 4:
                    pe.wait_ge(s["G_evac"], n - 3)
                for a in range(2):
                    last = pe.matmul(ps[:, 4 + n % 4, a * DM:(a + 1) * DM], WvT[:, 2 * n + a, :], Wo[:, 2 * n + a, :],
                                     start=True, stop=True)
                last.then_inc(s["G_done"], 1)

            def ln_transposes(b):
                pe.wait_ge(s["axn"], 2 * b + 2)
                if b == 0:
                    pe.wait_ge(s["G_evac"], H // 2)
                    pe.wait_ge(s["x2_done"], NT)
                else:
                    pe.wait_ge(s["pT_evac"], 16 * b - PIECE_LAG)
                for k in range(2):
                    for i in range(2):
                        last = pe.transpose(ps[:, 7, k * S + i * P:k * S + i * P + P], xn[:, i, k * P:k * P + P], ident[:, :])
                last.then_inc(s["axT_done"], 1)

            def piece(p):
                b, r = divmod(p, 16)
                g, kind = divmod(r, 4)
                tt = kind % 2
                if r == 0:
                    ln_transposes(b)
                if p >= 1:
                    pe.wait_ge(s["raw_done"], p)
                n_ = slice(g * 512, g * 512 + 512)
                if kind < 2:
                    if p == 0:
                        pe.wait_ge(s["wk_split"], 2)
                    a_ = slice(PAD + tt * P, PAD + tt * P + P)
                    pairs = [(ctxH[:, b, a_], ctxL[:, b, a_], WkH[:, n_], WkL[:, n_])]
                else:
                    pe.wait_ge(s["axTH"], b + 1)
                    pe.wait_ge(s["axTL"], b + 1)
                    pe.wait_ge(s["wqh"], 4)
                    pe.wait_ge(s["wql"], 4)
                    a_ = slice(tt * P, tt * P + P)
                    pairs = [(xT[:, b % 2, 0, k, a_], xT[:, b % 2, 1, k, a_], WqH[:, k, n_], WqL[:, k, n_]) for k in range(2)]
                three(pe, ps[:, 6, :], pairs).then_inc(s["piece_done"], 1)

            def piece_T(p):
                if p % 4 < 2:
                    pe.wait_ge(s["pnorm"], 2 * (p // 4) + p % 4 + 1)
                else:
                    pe.wait_ge(s["raw_done"], p + 1)
                if p >= 1:
                    pe.wait_ge(s["pT_evac"], p)
                if p // 16 < B - 1 or True:
                    bb = (p + PIECE_LAG) // 16
                    if (p + PIECE_LAG) % 16 < PIECE_LAG + 1 and bb < B:
                        pe.wait_ge(s["axTL"], bb + 1)
                for a in range(GRP):
                    last = pe.transpose(ps[:, 7, a * P:a * P + P], praw[p % 4][:, a * P:a * P + P], ident[:, :])
                last.then_inc(s["pT_done"], 1)

            def scores(n):
                G_, a = divmod(n, GRP)
                if a == 0:
                    pe.wait_ge(s["pT_evac"], 4 * G_ + 4)
                if n >= 2:
                    pe.wait_ge(s["exps"], 2 * (n - 1))
                for qt in range(2):
                    last = pe.matmul(ps[:, n % 2, qt * S:qt * S + S], qT[:, G_ % RING, a, qt * P:qt * P + P],
                                     kT[:, G_ % RING, a, :], start=True, stop=True)
                last.then_inc(s["sc_done"], 1)

            def probs_T(n):
                pe.wait_ge(s["pnorm_done"], n + 1)
                if n >= 2:
                    pe.wait_ge(s["PT_evac"], n - 1)
                for kt in range(2):
                    for qt in range(2):
                        last = pe.transpose(ps[:, 2 + n % 2, kt * S + qt * P:kt * S + qt * P + P],
                                            Pb[n % 4][:, qt, kt * P:kt * P + P], ident[:, :])
                last.then_inc(s["PT_done"], 1)

            def values(n):
                b = n // H
                pe.wait_ge(s["PT_evac"], n + 1)
                if n >= 1:
                    pe.wait_ge(s["U_evac"], n)
                for kt in range(2):
                    last = pe.matmul(ps[:, 4, 0:S], ctxn[:, 2 * b + kt, :], PT[n % 3][:, kt, :], start=(kt == 0), stop=(kt == 1))
                last.then_inc(s["U_done"], 1)

            def project_out(n):
                b, h = divmod(n, H)
                pe.wait_ge(s["U_evac"], n + 1)
                if h == 0 and b >= 1:
                    pe.wait_ge(s["x3_done"], b)
                for qt in range(2):
                    last = pe.matmul(ps[:, 5, qt * DM:qt * DM + DM], Us[n % 3][:, qt * P:qt * P + P], G[:, h, :],
                                     start=(h == 0 and qt == 0), stop=(h == H - 1), skip_group_check=True)
                last.then_inc(s["y_done"], 1)

            pe.wait_ge(s["ld_ctxn"], 48)
            for step in range(16 * B + FIRST_HEAD + U_LAG + 1):
                n = step - FIRST_HEAD
                if step < 16 * B:
                    piece(step)
                if 0 <= n < 16 * B:
                    scores(n)
                if 0 <= step - PIECE_LAG < 16 * B:
                    piece_T(step - PIECE_LAG)
                if 0 <= n - PT_LAG < 16 * B:
                    probs_T(n - PT_LAG)
                if 0 <= n - U_LAG - 1 < 16 * B:
                    project_out(n - U_LAG - 1)
                if 0 <= n - U_LAG < 16 * B:
                    values(n - U_LAG)

            pe.wait_ge(s["exps"], 2 * 16 * B)
            pe.wait_ge(s["pT_evac"], 16 * B)
            for b in range(B):
                pe.wait_ge(s["mxn"], 2 * b + 2)
                if b >= 1:
                    pe.wait_ge(s["mxTL"], b)
                for k in range(2):
                    for i in range(2):
                        last = pe.transpose(ps[:, 7, k * S + i * P:k * S + i * P + P], xm[:, i, k * P:k * P + P], ident[:, :])
                last.then_inc(s["mxT_done"], 1)
            pe.wait_ge(s["mxTL"], B)
            pe.wait_ge(s["mxTH"], B)
            pe.wait_ge(s["gws"], 3)
            for i in range(NT):
                three(pe, ps[:, 7, i * E:i * E + E],
                      [(xmH[:, k, i * P:i * P + P], xmL[:, k, i * P:i * P + P], gwH[:, k, :], gwL[:, k, :]) for k in range(2)]
                      ).then_inc(s["rl_done"], 1)

            def cw_transposes():
                pe.wait_ge(s["rdve"], RD_ALL)
                for i in range(NT):
                    if i == 4:
                        pe.wait_ge(s["cwT_evac"], 1)
                    last = pe.transpose(ps[0:64, 7, (i % 4) * P:(i % 4) * P + P], cwHL[:, i, :], ident[:, :])
                    if i % 4 == 3:
                        last.then_inc(s["cwT_done"], 1)
                pe.wait_ge(s["cwT_evac"], 2)

            def down(m):
                ft, c = divmod(m, 2)
                rows = min(P, FALL - ft * P)
                pe.wait_ge(s["hL_done"], m + 1)
                for tt in range(4):
                    i = 4 * c + tt
                    a_ = slice(tt * P, tt * P + P)
                    terms = ((hH[m % 3], wH[ft % 2]), (hH[m % 3], wL[ft % 2]), (hL[m % 3], wH[ft % 2]))
                    for z, (a, w) in enumerate(terms):
                        last = pe.matmul(ps[:, i // 2, (i % 2) * DM:(i % 2) * DM + DM], a[0:rows, a_], w[0:rows, 512:768],
                                         start=(ft == 0 and z == 0 and i % 2 == 0), stop=(ft == FT - 1 and z == 2),
                                         skip_group_check=True)
                last.then_inc(s["down_done"], 1)

            for m in range(2 * FT):
                ft, c = divmod(m, 2)
                rows = min(P, FALL - ft * P)
                t_ = slice(c * 512, c * 512 + 512)
                if c == 0:
                    pe.wait_ge(s["wsplit"], ft + 1)
                    pe.wait_ge(s["wsplitL"], ft + 1)
                if m >= 1:
                    pe.wait_ge(s["silu_done"], m)
                if m == 0:
                    pe.wait_ge(s["U_evac"], 16 * B)
                    pe.wait_ge(s["x3_done"], B)
                for which, bank, done, free in ((0, 4, "gate_mm", None), (1, 5, "up_mm", "m1_done")):
                    if free and m >= 1:
                        pe.wait_ge(s[free], m)
                    three(pe, ps[0:rows, bank, :],
                          [(wH[ft % 2][:, 256 * which + k * P:256 * which + k * P + rows],
                            wL[ft % 2][:, 256 * which + k * P:256 * which + k * P + rows],
                            xmH[:, k, t_], xmL[:, k, t_]) for k in range(2)]).then_inc(s[done], 1)
                if m == 0:
                    cw_transposes()
                    pe.wait_ge(s["ld_esel"], 16)
                if ft < FTR:
                    if m >= 1:
                        pe.wait_ge(s["m2_done"], m)
                    pe.matmul(ps[:, 6, :], esel[:, ft * P:ft * P + P], cwT[:, t_], start=True, stop=True).then_inc(s["cw_mm"], 1)
                if m >= 1:
                    down(m - 1)
            down(2 * FT - 1)

        @block.scalar
        def _(act):
            act.wait_ge(s["ld_small"], 80)
            act.activation(tg[:, :], gates[:, :], ACT.Tanh).then_inc(s["gate_done"], 1)
            act.wait_ge(s["ld_sel"], 48)
            act.copy(identb[:, :], ident[:, :]).then_inc(s["gate_done"], 1)
            for et in range(2):
                for hf in range(2):
                    act.wait_ge(s["conv_done"], 2 * et + hf + 1)
                    act.activation(u[:, et, 512 * hf:512 * hf + 512], ps[:, 2 * et + hf, :], ACT.Silu,
                                   bias=ec[:, et, 0:1]).then_inc(s["u_done"], 1)
            act.wait_ge(s["znb"], 1)
            for i in range(NT):
                act.activation(sz[:, i, :], x[:, i, :], ACT.Silu, bias=nb8[:, i:i + 1], scale=rstd[:, i:i + 1]
                               ).then_inc(s["sz_done"], 1)
            for n, (hf, bank, dst) in enumerate(((0, 0, dtl[:, 0:512]), (1, 1, dtl[:, 512:1024]), (0, 4, Bs[:, 0:512]),
                                                 (1, 5, Bs[:, 512:1024]), (0, 6, Cs[:, 0:512]), (1, 7, Cs[:, 512:1024]))):
                act.wait_ge(s["xproj_done"], 6)
                m = DR if n < 2 else P
                act.copy(dst, ps[0:m, bank, :]).then_inc(s["bcd_evac"], 1)
            act.activation(nacol[:, :], acol[:, :], ACT.Exp).then_inc(s["nacol_done"], 1)
            for et in range(2):
                act.wait_ge(s["dpre_done"], 2 * et + 2)
                act.activation(dab[:, et, :], ps[:, 2 + 2 * et:4 + 2 * et, :].rearrange("p a n -> p (a n)"), ACT.Abs,
                               bias=ec[:, et, 1:2]).then_inc(s["dact"], 1)
            for et in range(2):
                act.wait_ge(s["dact"], et + 1)
                act.activation(dex[:, et, :], dab[:, et, :], ACT.Exp, scale=-1.0).then_inc(s["dact"], 1)
            for et in range(2):
                act.wait_ge(s["ddve"], et + 1)
                act.activation(dlt[:, et, :], dab[:, et, :], ACT.Ln).then_inc(s["dact"], 1)
            for et in range(2):
                for half in range(2):
                    r_ = slice(64 * half, 64 * half + 64)
                    act.wait_ge(s["ddve"], 6 + 4 * et + 3)
                    act.copy(XD[r_, 2 * et + half, :], dlt[r_, et, :]).then_inc(s["dhi_done"], 1)
                    act.wait_ge(s["ddve"], 6 + 4 * et + 4)
                    act.copy(XU[r_, 2 * et + half, :], dab[r_, et, :]).then_inc(s["dhi_done"], 1)
            act.wait_ge(s["ld_w"], 32)
            for w in range(2):
                act.wait_ge(s["dlo_done"], 8)
                act.activation(work[:, 7168:9216], wraw[w], ACT.Abs, accum_out=wsum[:, w:w + 1]).then_inc(s["wabs"], 1)
                act.wait_ge(s["wabs"], w + 1)
            act.wait_ge(s["nacol_done"], 2)
            act.wait_ge(s["pool_init"], 7)
            for t in range(ST):
                act.wait_ge(s["dbc_done"], t + 1)
                if t >= 2:
                    act.wait_ge(s["scan_done"], t - 1)
                act.activation(dA[t % 2].rearrange("p (b l) -> p b l", b=B)[:, :, 1:S],
                               ps[:, 0:2, :].rearrange("p a (b l) -> p (a b) l", b=2)[:, :, 1:S], ACT.Exp,
                               scale=nacol[:, t:t + 1]).then_inc(s["exp_done"], 1)
            for i in range(NT):
                act.wait_ge(s["mm1_done"], i + 1)
                act.wait_ge(s["fsc"], 7)
                if i == 0:
                    act.wait_ge(s["hc_done"], ST)
                if i >= 2:
                    act.wait_ge(s["fact"], 3 * (i - 2) + 2)
                act.activation(g1[i % 2], ps[:, 4 + 2 * (i % 2):6 + 2 * (i % 2), :].rearrange("p a n -> p (a n)"), ACT.Gelu,
                               scale=q8[:, 6, i:i + 1]).then_inc(s["fact"], 1)
                act.wait_ge(s["fact"], 3 * i + 1)
                if i >= 2:
                    act.wait_ge(s["fhq"], 2 * (i - 2) + 2)
                act.activation(g2[i % 2], g1[i % 2], ACT.Gelu).then_inc(s["fact"], 1)
                act.wait_ge(s["fact"], 3 * i + 2)
                act.activation(sqj, g2[i % 2], ACT.Square, accum_out=q8[:, 7, i:i + 1]).then_inc(s["fact"], 1)
            for n in range(H // 2):
                act.wait_ge(s["G_done"], n + 1)
                act.copy(G[:, 2 * n:2 * n + 2, :].rearrange("p a n -> p (a n)"), ps[:, 4 + n % 4, :]).then_inc(s["G_evac"], 1)
            act.wait_ge(s["ld_wq"], 16)
            for n in range(4):
                k, c = divmod(n, 2)
                act.copy(WqH[:, k, 1024 * c:1024 * c + 1024], Wqr[:, 1024 * n:1024 * n + 1024]).then_inc(s["wqh"], 1)

            def piece(p):
                b, r = divmod(p, 16)
                g, kind = divmod(r, 4)
                if r == 0:
                    act.wait_ge(s["axT_done"], b + 1)
                    if b >= 2:
                        act.wait_ge(s["piece_done"], 16 * (b - 1))
                    act.copy(xT[:, b % 2, 0, :, :].rearrange("p k t -> p (k t)"), ps[:, 7, :]).then_inc(s["axTH"], 1)
                act.wait_ge(s["piece_done"], p + 1)
                if p == 0:
                    act.wait_ge(s["x2_done"], NT)
                if p >= 4:
                    act.wait_ge(s["pT_done"], p - 3)
                    act.wait_ge(s["psq_done"], p - 3)
                act.copy(praw[p % 4], ps[:, 6, :]).then_inc(s["raw_done"], 1)

            def softmax(n):
                act.wait_ge(s["hmax"], 2 * n + 2)
                if n >= 4:
                    act.wait_ge(s["PT_done"], n - 3)
                for qt in range(2):
                    act.activation(Pb[n % 4][:, qt, :], ps[:, n % 2, qt * S:qt * S + S], ACT.Exp,
                                   bias=hs[:, n % 4, 2 + qt:3 + qt], scale=rq[:, (n // GRP) % RING, n % GRP, qt:qt + 1],
                                   accum_out=hs[:, n % 4, 4 + qt:5 + qt]).then_inc(s["exps"], 1)

            def PT_half(n):
                act.wait_ge(s["PT_done"], n + 1)
                if n >= 3:
                    act.wait_ge(s["U_done"], n - 2)
                act.copy(PT[n % 3].rearrange("p k q -> p (k q)"), ps[:, 2 + n % 2, :]).then_inc(s["PT_evac"], 1)

            for step in range(16 * B + FIRST_HEAD + U_LAG + 1):
                n = step - FIRST_HEAD
                if step < 16 * B:
                    piece(step)
                if 0 <= n < 16 * B:
                    softmax(n)
                if 0 <= n - PT_LAG < 16 * B:
                    PT_half(n - PT_LAG)
            for b in range(B):
                act.wait_ge(s["mxT_done"], b + 1)
                if b == 0:
                    act.wait_ge(s["piece_done"], 16 * B)
                act.copy(xmH[:, :, b * S:b * S + S], ps[:, 7, :].rearrange("p (k t) -> p k t", k=2)).then_inc(s["mxTH"], 1)
            for i in range(NT):
                act.wait_ge(s["rdve"], NT)
                act.activation(rt[:, i, 0, :], ps[:, 7, i * E:i * E + E], ACT.Exp, bias=rt[:, i, 4, 0:1],
                               accum_out=rt[:, i, 4, 1:2]).then_inc(s["rexp"], 1)

            def split(ft):
                act.wait_ge(s[f"ld_moe{ft % 4}"], 16 * (ft // 4 + 1))
                if ft >= 2:
                    act.wait_ge(s["down_done"], 2 * (ft - 2) + 2)
                act.copy(wH[ft % 2], wr[ft % 4]).then_inc(s["wsplit"], 1)

            split(0)
            for m in range(2 * FT):
                ft, c = divmod(m, 2)
                rows = min(P, FALL - ft * P)
                if c == 0 and ft + 1 < FT:
                    if ft == 0:
                        split(1)
                act.wait_ge(s["gate_mm"], m + 1)
                if m >= 2:
                    act.wait_ge(s["m1_done"], m - 1)
                act.activation(sg[m % 2][0:rows, :], ps[0:rows, 4, :], ACT.Silu).then_inc(s["silu_done"], 1)
                act.wait_ge(s["m2_done"], m + 1)
                if m >= 3:
                    act.wait_ge(s["down_done"], m - 2)
                act.copy(hH[m % 3][0:rows, :], hm[m % 2][0:rows, :]).then_inc(s["hH_done"], 1)
                if c == 0 and 1 <= ft < FT - 1:
                    split(ft + 1)

        def layer_stats(eng, src, tiles, name):
            n = len(tiles)
            for a, i in enumerate(tiles):
                eng.bn_stats(st6[:, i, :], src[:, i, :]).then_inc(s[name], 1)
            return n

        @block.vector
        def _(dve):
            dve.wait_ge(s["ld_ctxT"], 16)
            src = ctxTr.rearrange("p (b l) -> p b l", b=B)
            dve.tensor_copy(ctxH[:, :, PAD:], src).then_inc(s["ctx_split"], 1)
            dve.wait_ge(s["ld_wc"], 32)
            dve.tensor_tensor(wc, cwb, inT[:, :].unsqueeze(1).to_broadcast([P, TAPS, DI]), ALU.mult).then_inc(s["conv_w"], 1)
            dve.wait_ge(s["ctx_split"], 1)
            dve.tensor_tensor(ctxL[:, :, PAD:], src, ctxH[:, :, PAD:].bitcast(F32), ALU.subtract).then_inc(s["ctx_split"], 1)
            dve.wait_ge(s["conv_w"], 1)
            dve.tensor_copy(wcH, wc).then_inc(s["conv_w"], 1)
            dve.wait_ge(s["conv_w"], 2)
            dve.tensor_tensor(wcL, wc, wcH.bitcast(F32), ALU.subtract).then_inc(s["conv_w"], 1)
            dve.wait_ge(s["ld_x"], 16)
            dve.wait_ge(s["pool_init"], 5)

            def stats(tiles, name, base):
                for i in tiles:
                    dve.bn_stats(st6[:, i, :], x[:, i, :]).then_inc(s[name], 1)
                dve.wait_ge(s[name], base + len(tiles))
                for i in tiles:
                    dve.bn_aggr(mv[:, i, :], st6[:, i, :]).then_inc(s[name], 1)
                dve.wait_ge(s[name], base + 2 * len(tiles))
                a, z = tiles[0], tiles[-1] + 1
                dve.tensor_scalar(ve[:, a:z], mv[:, a:z, 1], EPS, None, ALU.add).then_inc(s[name], 1)

            stats(range(NT), "zstat", 0)
            dve.wait_ge(s["zpow"], 1)
            dve.scalar_tensor_tensor(nb8[:, :], mv[:, :, 0], -1.0, rstd[:, :], ALU.mult, ALU.mult).then_inc(s["znb"], 1)
            dve.wait_ge(s["ld_sel"], 48)
            dve.tensor_copy(sel[:, :, :], selr).then_inc(s["sel_ready"], 1)
            dve.wait_ge(s["nacol_done"], 1)
            dve.tensor_scalar(nacol[:, :], nacol[:, :], -1.0, None, ALU.mult).then_inc(s["nacol_done"], 1)
            for et in range(2):
                dve.wait_ge(s["dact"], 3 + et)
                dve.tensor_scalar(dab[:, et, :], dex[:, et, :], 1.0, None, ALU.add).then_inc(s["ddve"], 1)
            for et in range(2):
                dve.wait_ge(s["ddve"], 1 + et)
                dve.scalar_tensor_tensor(dex[:, et, :], dab[:, et, :], 1.0, dex[:, et, :], ALU.subtract, ALU.subtract
                                         ).then_inc(s["ddve"], 1)
            for et in range(2):
                dve.wait_ge(s["dact"], 5 + et)
                dve.wait_ge(s["ddve"], 3 + et)
                dve.tensor_tensor(dlt[:, et, :], dlt[:, et, :], dex[:, et, :], ALU.subtract).then_inc(s["ddve"], 1)
            base = 6
            for et in range(2):
                dve.wait_ge(s["ddve"], 6)
                pw = ps[:, 2 + 2 * et:4 + 2 * et, :].rearrange("p a n -> p (a n)")
                dve.tensor_scalar(dex[:, et, :], pw, ec[:, et, 1:2], 0.0, ALU.add, ALU.max).then_inc(s["ddve"], 1)
                dve.wait_ge(s["ddve"], base + 1)
                dve.tensor_tensor(dlt[:, et, :], dlt[:, et, :], dex[:, et, :], ALU.add).then_inc(s["ddve"], 1)
                dve.wait_ge(s["ddve"], base + 2)
                dve.tensor_tensor(dab[:, et, :], dlt[:, et, :], u[:, et, :], ALU.mult).then_inc(s["ddve"], 1)
                dve.wait_ge(s["ddve"], base + 3)
                dve.engine_nop().then_inc(s["ddve"], 1) if False else dve.tensor_copy(small[:, 0:1], dlt[:, et, 0:1]).then_inc(s["ddve"], 1)
                base += 4
            for et in range(2):
                for half in range(2):
                    r_ = slice(64 * half, 64 * half + 64)
                    o_ = slice(64 - 64 * half, 128 - 64 * half)
                    dve.wait_ge(s["dhi_done"], 4 * et + 2 * half + 1)
                    dve.tensor_tensor(XD[o_, 2 * et + half, :], dlt[r_, et, :], XD[r_, 2 * et + half, :].bitcast(F32), ALU.subtract
                                      ).then_inc(s["dlo_done"], 1)
                    dve.wait_ge(s["dhi_done"], 4 * et + 2 * half + 2)
                    dve.tensor_tensor(XU[o_, 2 * et + half, :], dab[r_, et, :], XU[r_, 2 * et + half, :].bitcast(F32), ALU.subtract
                                      ).then_inc(s["dlo_done"], 1)
            dve.wait_ge(s["wsum_done"], 1)
            dve.tensor_scalar(mw[:, :], ps[:, 7, 0:2], 1.0 / (INNER * DM), EPS, ALU.mult, ALU.max).then_inc(s["wq_stat"], 1)
            dve.wait_ge(s["wq_stat"], 1)
            dve.reciprocal(iw[:, :], mw[:, :]).then_inc(s["wq_stat"], 1)
            dve.wait_ge(s["wq_stat"], 2)
            for w in range(2):
                dve.tensor_scalar(wraw[w], wraw[w], iw[:, w:w + 1], 1.0, ALU.mult, ALU.min).then_inc(s["wq_done"], 1)
            for w in range(2):
                dve.wait_ge(s["wq_done"], 1 + w)
                dve.tensor_scalar(wraw[w], wraw[w], -1.0, MAGIC, ALU.max, ALU.add).then_inc(s["wq_done"], 1)
            for w in range(2):
                dve.wait_ge(s["wq_done"], 3 + w)
                dve.tensor_scalar(w12q[:, w, :], wraw[w], MAGIC, None, ALU.subtract).then_inc(s["wq_done"], 1)

            def dbu(t):
                dve.wait_ge(s["ubc_done"], t + 1)
                if t >= 2:
                    dve.wait_ge(s["scan_done"], t - 1)
                if t == 0:
                    dve.wait_ge(s["dlo_done"], 8)
                    dve.wait_ge(s["bcd_evac"], 6)
                pu = ps[:, 2 + 2 * (t % 2):4 + 2 * (t % 2), :].rearrange("p a n -> p (a n)")
                dve.tensor_tensor(dBu[t % 2], pu, Bs, ALU.mult).then_inc(s["dbu_done"], 1)

            def y_out(et):
                dve.wait_ge(s["nsum_done"], JT * (et + 1))
                py = ps[:, 6:8, :].rearrange("p a n -> p (a n)")
                dve.scalar_tensor_tensor(yg[:, et, :], u[:, et, :], ec[:, et, 2:3], py, ALU.mult, ALU.add).then_inc(s["yevac"], 1)
                dve.wait_ge(s["yevac"], et + 1)
                dve.wait_ge(s["sz_done"], NT)
                ygv = yg[:, et, :].rearrange("p (b l) -> p b l", b=B)
                dve.tensor_tensor(ygv, ygv, sz.rearrange("p (b h) l -> p h b l", h=2)[:, et], ALU.mult).then_inc(s["yg_done"], 1)

            dbu(0)
            for t in range(ST):
                if t == JT + NSUM_LAG:
                    y_out(0)
                if t + 1 < ST:
                    dbu(t + 1)
                dve.wait_ge(s["exp_done"], t + 1)
                dve.wait_ge(s["dbu_done"], t + 1)
                if t >= 2:
                    dve.wait_ge(s["hc_done"], t - 1)
                dve.tensor_tensor_scan(hb[t % 2], dA[t % 2], dBu[t % 2], 0.0, ALU.mult, ALU.add).then_inc(s["scan_done"], 1)
            y_out(1)
            dve.wait_ge(s["gate_done"], 1)
            for b in range(B):
                dve.wait_ge(s["yT_done"], B + b + 1)
                x_ = x[:, 2 * b:2 * b + 2, :].rearrange("p i c -> p (i c)")
                dve.scalar_tensor_tensor(x_, ps[:, b, :], tg[:, 0:1], x_, ALU.mult, ALU.add).then_inc(s["x1_done"], 1)
            dve.wait_ge(s["x1_done"], B)
            dve.wait_ge(s["znb"], 1)
            stats(range(NT), "fst", 0)
            dve.wait_ge(s["fpow"], 1)
            dve.scalar_tensor_tensor(q8[:, 0, :], mv[:, :, 1], float(DM), rstd[:, :], ALU.mult, ALU.mult).then_inc(s["fsc"], 1)
            dve.wait_ge(s["fsc"], 1)
            dve.tensor_tensor(q8[:, 0, :], q8[:, 0, :], rstd[:, :], ALU.mult).then_inc(s["fsc"], 1)
            dve.wait_ge(s["yT_done"], 2 * B)
            for i in range(NT):
                dve.tensor_scalar(xl[:, i, :], x[:, i, :], mv[:, i, 0:1], rstd[:, i:i + 1], ALU.subtract, ALU.mult
                                  ).then_inc(s["fxl"], 1)
            dve.wait_ge(s["fxl"], NT)
            dve.tensor_reduce(q8[:, 2, :], xl, AX.X, ALU.max, apply_absolute_value=True).then_inc(s["fxl"], 1)
            dve.wait_ge(s["fpow"], 2)
            dve.tensor_scalar(q8[:, 1, :], q8[:, 1, :], 1e-12, None, ALU.max).then_inc(s["fch"], 1)
            dve.wait_ge(s["fch"], 1)
            dve.reciprocal(q8[:, 1, :], q8[:, 1, :]).then_inc(s["fch"], 1)
            dve.wait_ge(s["fch"], 2)
            dve.wait_ge(s["fxl"], NT + 1)
            dve.scalar_tensor_tensor(q8[:, 3, :], q8[:, 2, :], float(DM) ** 0.5, q8[:, 1, :], ALU.mult, ALU.mult).then_inc(s["fsc"], 1)
            dve.wait_ge(s["fsc"], 3)
            dve.tensor_scalar(q8[:, 3, :], q8[:, 3, :], EPS, None, ALU.max).then_inc(s["fsc"], 1)
            dve.wait_ge(s["fsc"], 4)
            dve.reciprocal(q8[:, 4, :], q8[:, 3, :]).then_inc(s["fsc"], 1)
            dve.wait_ge(s["fsc"], 5)
            dve.scalar_tensor_tensor(q8[:, 5, :], q8[:, 1, :], 127.0 * float(DM) ** 0.5, q8[:, 4, :], ALU.mult, ALU.mult
                                     ).then_inc(s["fsc"], 1)
            dve.tensor_scalar(q8[:, 6, :], q8[:, 3, :], mw[:, 0:1], 1.0 / 127.0, ALU.mult, ALU.mult).then_inc(s["fsc"], 1)
            dve.tensor_scalar(k2[:, :], mw[:, 1:2], tg[:, 1:2], 1.0 / 127.0, ALU.mult, ALU.mult).then_inc(s["fsc"], 1)
            dve.wait_ge(s["fsc"], 8)
            for i in range(NT):
                dve.tensor_scalar(xl[:, i, :], xl[:, i, :], q8[:, 5, i:i + 1], MAGIC, ALU.mult, ALU.add).then_inc(s["fq"], 1)
            dve.wait_ge(s["fq"], NT)
            dve.wait_ge(s["hc_done"], ST)
            dve.wait_ge(s["nsum_done"], ST)
            dve.tensor_scalar(xq.rearrange("p i c -> p (i c)"), xl.rearrange("p i c -> p (i c)"), MAGIC, None, ALU.subtract
                              ).then_inc(s["fq"], 1)
            for k in range(2):
                dve.wait_ge(s["fqT_done"], k + 1)
                dve.tensor_copy(xqT[:, k, :], ps[:, k, :].bitcast(BF16)).then_inc(s["fqT_evac"], 1)
            FCH = 2

            def evac_T(i):
                dve.wait_ge(s["fT_done"], i + 1)
                if i >= 2:
                    dve.wait_ge(s["mm2_done"], i - 1)
                dve.tensor_copy(hT[i % 2].rearrange("p k t -> p (k t)"), ps[:, 2 + i % 2, :].bitcast(BF16)).then_inc(s["fT_evac"], 1)

            def x2(i):
                dve.wait_ge(s["mm2_done"], i + 1)
                dve.scalar_tensor_tensor(x[:, i, :], ps[:, i % 2, 0:DM], q8[:, 9, i:i + 1], x[:, i, :], ALU.mult, ALU.add
                                         ).then_inc(s["x2_done"], 1)

            for i in range(NT):
                i_ = slice(i, i + 1)
                c = FCH + 7 * i
                dve.wait_ge(s["fact"], 3 * i + 2)
                dve.tensor_reduce(q8[:, 2, i_], g2[i % 2], AX.X, ALU.max, apply_absolute_value=True).then_inc(s["famax"], 1)
                if i >= 1:
                    evac_T(i - 1)
                dve.wait_ge(s["fpow2"], i + 1)
                dve.tensor_scalar(q8[:, 8, i_], q8[:, 8, i_], 1e-12, None, ALU.max).then_inc(s["fch"], 1)
                dve.wait_ge(s["fch"], c + 1)
                dve.reciprocal(q8[:, 8, i_], q8[:, 8, i_]).then_inc(s["fch"], 1)
                dve.wait_ge(s["fch"], c + 2)
                dve.wait_ge(s["famax"], i + 1)
                dve.scalar_tensor_tensor(q8[:, 3, i_], q8[:, 2, i_], float(INNER) ** 0.5, q8[:, 8, i_], ALU.mult, ALU.mult
                                         ).then_inc(s["fch"], 1)
                dve.wait_ge(s["fch"], c + 3)
                dve.tensor_scalar(q8[:, 3, i_], q8[:, 3, i_], EPS, None, ALU.max).then_inc(s["fch"], 1)
                dve.wait_ge(s["fch"], c + 4)
                dve.reciprocal(q8[:, 4, i_], q8[:, 3, i_]).then_inc(s["fch"], 1)
                dve.wait_ge(s["fch"], c + 5)
                dve.scalar_tensor_tensor(q8[:, 5, i_], q8[:, 8, i_], 127.0 * float(INNER) ** 0.5, q8[:, 4, i_], ALU.mult, ALU.mult
                                         ).then_inc(s["fch"], 1)
                dve.tensor_tensor(q8[:, 9, i_], q8[:, 3, i_], k2[:, :], ALU.mult).then_inc(s["fch"], 1)
                dve.wait_ge(s["fch"], c + 7)
                dve.wait_ge(s["fact"], 3 * i + 3)
                dve.tensor_scalar(g2[i % 2], g2[i % 2], q8[:, 5, i_], MAGIC, ALU.mult, ALU.add).then_inc(s["fhq"], 1)
                dve.wait_ge(s["fhq"], 2 * i + 1)
                if i >= 2:
                    dve.wait_ge(s["fT_done"], i - 1)
                dve.tensor_scalar(hq[i % 2], g2[i % 2], MAGIC, None, ALU.subtract).then_inc(s["fhq"], 1)
                if i >= 1:
                    x2(i - 1)
            evac_T(NT - 1)
            x2(NT - 1)
            dve.wait_ge(s["ld_wk"], 16)
            dve.wait_ge(s["conv_done"], 4)
            dve.tensor_copy(WkH, Wkr).then_inc(s["wk_split"], 1)
            dve.wait_ge(s["wk_split"], 1)
            dve.tensor_tensor(WkL, Wkr, WkH.bitcast(F32), ALU.subtract).then_inc(s["wk_split"], 1)
            for n in range(4):
                k, c = divmod(n, 2)
                dve.wait_ge(s["wqh"], n + 1)
                dve.tensor_tensor(WqL[:, k, 1024 * c:1024 * c + 1024], Wqr[:, 1024 * n:1024 * n + 1024],
                                  WqH[:, k, 1024 * c:1024 * c + 1024].bitcast(F32), ALU.subtract).then_inc(s["wql"], 1)
            dve.tensor_scalar(gkq[:, :], gqk[:, 0:1], gqk[:, 1:2], float(P) ** -0.5, ALU.mult, ALU.mult).then_inc(s["gkq_done"], 1)
            dve.wait_ge(s["gkq_done"], 1)
            dve.wait_ge(s["x2_done"], NT)
            dve.wait_ge(s["fxl"], NT)

            def attn_ln(b):
                stats(range(2 * b, 2 * b + 2), "aln", 5 * b)
                dve.wait_ge(s["apow"], b + 1)
                if b >= 1:
                    dve.wait_ge(s["axT_done"], b)
                for i in range(2):
                    dve.tensor_scalar(xn[:, i, :], x[:, 2 * b + i, :], mv[:, 2 * b + i, 0:1], rstd[:, 2 * b + i:2 * b + i + 1],
                                      ALU.subtract, ALU.mult).then_inc(s["axn"], 1)

            def attn_lo(b):
                dve.wait_ge(s["axTH"], b + 1)
                if b >= 2:
                    dve.wait_ge(s["piece_done"], 16 * (b - 1))
                dve.tensor_tensor(xT[:, b % 2, 1, :, :].rearrange("p k t -> p (k t)"), ps[:, 7, :],
                                  xT[:, b % 2, 0, :, :].rearrange("p k t -> p (k t)").bitcast(F32), ALU.subtract
                                  ).then_inc(s["axTL"], 1)

            def piece_stats(p):
                dve.wait_ge(s["psq_done"], p + 1)
                if p >= 4:
                    dve.wait_ge(s["prv_done"], p - 3)
                dve.tensor_reduce(rr[:, p % 4, :], psq[p % 2].rearrange("p (a c) -> p a c", a=GRP), AX.X, ALU.add
                                  ).then_inc(s["prs"], 1)
                dve.wait_ge(s["prs"], 2 * p + 1)
                dve.tensor_scalar(rr[:, p % 4, :], rr[:, p % 4, :], 1.0 / P, EPS, ALU.mult, ALU.add).then_inc(s["prs"], 1)

            def piece_evac(p):
                G_, kind = divmod(p, 4)
                dst = (kT if kind < 2 else qT)[:, G_ % RING, :, (kind % 2) * P:(kind % 2) * P + P]
                src = ps[:, 7, :].rearrange("p (a t) -> p a t", a=GRP)
                dve.wait_ge(s["pT_done"], p + 1)
                if G_ >= RING:
                    dve.wait_ge(s["sc_done"], GRP * (G_ - RING + 1))
                if p == 0:
                    dve.wait_ge(s["wql"], 4)
                if kind < 2:
                    dve.tensor_scalar(dst, src, gkq[:, 0:1], None, ALU.mult).then_inc(s["pT_evac"], 1)
                else:
                    dve.tensor_copy(dst, src).then_inc(s["pT_evac"], 1)

            def head_max(n):
                dve.wait_ge(s["sc_done"], n + 1)
                if n >= 4:
                    dve.wait_ge(s["pnorm_done"], n - 3)
                dve.tensor_reduce(hs[:, n % 4, 0:2], ps[:, n % 2, :].rearrange("p (a k) -> p a k", a=2), AX.X, ALU.max
                                  ).then_inc(s["hmax"], 1)
                dve.wait_ge(s["hmax"], 2 * n + 1)
                if n % GRP == 0:
                    dve.wait_ge(s["prv_done"], 4 * (n // GRP) + 4)
                dve.scalar_tensor_tensor(hs[:, n % 4, 2:4], hs[:, n % 4, 0:2], -1.0, rq[:, (n // GRP) % RING, n % GRP, :],
                                         ALU.mult, ALU.mult).then_inc(s["hmax"], 1)

            def head_recip(n):
                dve.wait_ge(s["exps"], 2 * n + 2)
                dve.reciprocal(hs[:, n % 4, 6:8], hs[:, n % 4, 4:6]).then_inc(s["hrec"], 1)

            def U_out(n):
                dve.wait_ge(s["U_done"], n + 1)
                if n >= 3:
                    dve.wait_ge(s["y_done"], n - 2)
                dve.tensor_copy(Us[n % 3], ps[:, 4, 0:S]).then_inc(s["U_evac"], 1)

            def x3(b):
                dve.wait_ge(s["y_done"], H * (b + 1))
                x_ = x[:, 2 * b:2 * b + 2, :].rearrange("p i c -> p (i c)")
                dve.scalar_tensor_tensor(x_, ps[:, 5, :], tg[:, 2:3], x_, ALU.mult, ALU.add).then_inc(s["x3_done"], 1)

            attn_ln(0)
            for step in range(16 * B + FIRST_HEAD + U_LAG + 2):
                n = step - FIRST_HEAD
                if step % 16 == 0 and step < 16 * B:
                    attn_lo(step // 16)
                if 0 <= n < 16 * B:
                    head_max(n)
                if step < 16 * B:
                    piece_stats(step)
                if 0 <= n < 16 * B:
                    head_recip(n)
                if 0 <= step - PIECE_LAG < 16 * B:
                    piece_evac(step - PIECE_LAG)
                if 0 <= n - U_LAG < 16 * B:
                    U_out(n - U_LAG)
                m = n - U_LAG - 1
                if m >= 0 and m % H == H - 1:
                    x3(m // H)
                if step % 16 == 8 and step // 16 + 1 < B:
                    attn_ln(step // 16 + 1)
            dve.wait_ge(s["x3_done"], B)
            for b in range(B):
                stats(range(2 * b, 2 * b + 2), "mln", 5 * b)
                dve.wait_ge(s["mpow"], b + 1)
                if b >= 1:
                    dve.wait_ge(s["mxT_done"], b)
                for i in range(2):
                    dve.tensor_scalar(xm[:, i, :], x[:, 2 * b + i, :], mv[:, 2 * b + i, 0:1], rstd[:, 2 * b + i:2 * b + i + 1],
                                      ALU.subtract, ALU.mult).then_inc(s["mxn"], 1)
                dve.wait_ge(s["mxTH"], b + 1)
                dve.tensor_tensor(xmL[:, :, b * S:b * S + S], ps[:, 7, :].rearrange("p (k t) -> p k t", k=2),
                                  xmH[:, :, b * S:b * S + S].bitcast(F32), ALU.subtract).then_inc(s["mxTL"], 1)
            dve.wait_ge(s["rl_done"], NT)
            for i in range(NT):
                dve.tensor_reduce(rt[:, i, 4, 0:1], ps[:, 7, i * E:i * E + E], AX.X, ALU.max, negate=True).then_inc(s["rdve"], 1)
            dve.wait_ge(s["rexp"], NT)
            dve.reciprocal(rt[:, :, 4, 2:3], rt[:, :, 4, 1:2]).then_inc(s["rdve"], 1)
            dve.wait_ge(s["rdve"], NT + 1)
            dve.tensor_tensor(rt[:, :, 0, :], rt[:, :, 0, :], rt[:, :, 4, 2:3].to_broadcast([P, NT, E]), ALU.mult).then_inc(s["rdve"], 1)
            dve.wait_ge(s["rdve"], NT + 2)
            for i in range(NT):
                dve.max(rt[:, i, 1, :], rt[:, i, 0, :]).then_inc(s["rdve"], 1)
            dve.wait_ge(s["rdve"], 2 * NT + 2)
            for i in range(NT):
                dve.max_index(rti[:, i, :], rt[:, i, 1, :], rt[:, i, 0, :]).then_inc(s["rdve"], 1)
            dve.wait_ge(s["rdve"], 3 * NT + 2)
            dve.tensor_copy(rt[:, :, 2, :], rti[:, :, :]).then_inc(s["rdve"], 1)
            dve.tensor_tensor(rt[:, :, 4, 3:4], rt[:, :, 1, 0:1], rt[:, :, 1, 1:2], ALU.add).then_inc(s["rdve"], 1)
            dve.wait_ge(s["rdve"], 3 * NT + 4)
            dve.tensor_scalar(rt[:, :, 4, 3:4], rt[:, :, 4, 3:4], 1e-20, None, ALU.add).then_inc(s["rdve"], 1)
            dve.wait_ge(s["rdve"], 3 * NT + 5)
            dve.reciprocal(rt[:, :, 4, 4:5], rt[:, :, 4, 3:4]).then_inc(s["rdve"], 1)
            dve.wait_ge(s["rdve"], 3 * NT + 6)
            dve.tensor_tensor(rt[:, :, 3, 0:2], rt[:, :, 1, 0:2], rt[:, :, 4, 4:5].to_broadcast([P, NT, 2]), ALU.mult).then_inc(s["rdve"], 1)
            dve.wait_ge(s["rdve"], 3 * NT + 7)
            for i in range(NT):
                dve.tensor_scalar(rt[:, i, 5, :], iota8[:, :], rt[:, i, 2, 0:1], rt[:, i, 3, 0:1], ALU.is_equal, ALU.mult
                                  ).then_inc(s["rdve"], 1)
            for i in range(NT):
                dve.tensor_scalar(rt[:, i, 0, :], iota8[:, :], rt[:, i, 2, 1:2], rt[:, i, 3, 1:2], ALU.is_equal, ALU.mult
                                  ).then_inc(s["rdve"], 1)
            dve.wait_ge(s["rdve"], 5 * NT + 7)
            dve.tensor_tensor(rt[:, :, 5, :], rt[:, :, 5, :], rt[:, :, 0, :], ALU.add).then_inc(s["rdve"], 1)
            dve.wait_ge(s["rdve"], 5 * NT + 8)
            dve.tensor_copy(cwR[:, :, :], rt[:, :, 5, :]).then_inc(s["rdve"], 1)
            dve.wait_ge(s["rdve"], 5 * NT + 9)
            dve.wait_ge(s["gws"], 1)
            dve.tensor_copy(cwHL[:, :, 0:E], cwR[:, :, :].bitcast(F32)).then_inc(s["rdve"], 1)
            dve.tensor_tensor(cwHL[:, :, 32:32 + E], rt[:, :, 5, :], cwR[:, :, :].bitcast(F32), ALU.subtract).then_inc(s["rdve"], 1)
            assert RD_ALL == 5 * NT + 11

            def split_lo(ft):
                dve.wait_ge(s["wsplit"], ft + 1)
                dve.tensor_tensor(wL[ft % 2], wr[ft % 4], wH[ft % 2].bitcast(F32), ALU.subtract).then_inc(s["wsplitL"], 1)

            split_lo(0)
            split_lo(1)
            for a in range(2):
                dve.wait_ge(s["cwT_done"], a + 1)
                dve.tensor_copy(cwT[:, a * 512:a * 512 + 512], ps[0:64, 7, :]).then_inc(s["cwT_evac"], 1)
            for m in range(2 * FT):
                ft, c = divmod(m, 2)
                rows = min(P, FALL - ft * P)
                dve.wait_ge(s["silu_done"], m + 1)
                dve.wait_ge(s["up_mm"], m + 1)
                if m >= 2:
                    dve.wait_ge(s["hL_done"], m - 1)
                    dve.wait_ge(s["hH_done"], m - 1)
                if m == 0:
                    dve.wait_ge(s["PT_done"], 16 * B)
                hm_ = hm[m % 2][0:rows, :]
                if ft < FTR:
                    dve.tensor_tensor(hm_, ps[0:rows, 5, :], sg[m % 2][0:rows, :], ALU.mult).then_inc(s["m1_done"], 1)
                    dve.wait_ge(s["m1_done"], m + 1)
                    dve.wait_ge(s["cw_mm"], m + 1)
                    dve.tensor_tensor(hm_, ps[0:rows, 6, :], hm_, ALU.mult).then_inc(s["m2_done"], 1)
                else:
                    dve.tensor_tensor(hm_, ps[0:rows, 5, :], sg[m % 2][0:rows, :], ALU.mult).then_inc(s["m1_done"], 1)
                    dve.wait_ge(s["m1_done"], m + 1)
                    dve.tensor_copy(small[:, 1:2], tg[:, 0:1]).then_inc(s["m2_done"], 1)
                if c == 1 and ft >= 1 and ft + 1 < FT:
                    split_lo(ft + 1)
            dve.wait_ge(s["down_done"], 2 * FT)
            for b in range(B):
                for i in range(2):
                    dve.scalar_tensor_tensor(yo[b][:, i, :], ps[:, b, i * DM:i * DM + DM], tg[:, 3:4], x[:, 2 * b + i, :],
                                             ALU.mult, ALU.add).then_inc(s["out_done"], 1)

        @block.gpsimd
        def _(pool):
            pool.memset(ctxH[:, :, 0:PAD].bitcast(F32), 0.0).then_inc(s["pool_init"], 1)
            pool.memset(ctxL[:, :, 0:PAD].bitcast(F32), 0.0).then_inc(s["pool_init"], 1)
            pool.memset(phalf[:, :], 0.5).then_inc(s["pool_init"], 1)
            pool.memset(nhalf[:, :], -0.5).then_inc(s["pool_init"], 1)
            pool.memset(ones[:, :], 1.0).then_inc(s["pool_init"], 1)
            pool.wait_ge(s["pool_init"], 5)
            pool.wait_ge(s["zstat"], 2 * NT + 1)
            pool.tensor_tensor(rstd[:, :], ve[:, :], nhalf[:, 0:NT], ALU.pow).then_inc(s["zpow"], 1)
            pool.wait_ge(s["sel_ready"], 1)
            pool.wait_ge(s["ctx_split"], 2)
            for i in range(2):
                pool.memset(dA[i].rearrange("p (b l) -> p b l", b=B)[:, :, 0:1], 0.0).then_inc(s["pool_init"], 1)
            pool.wait_ge(s["bcd_evac"], 6)
            pool.wait_ge(s["wabs"], 2)
            for t in range(ST):
                pool.wait_ge(s["scan_done"], t + 1)
                if t >= 3:
                    pool.wait_ge(s["nsum_done"], t - 2)
                pool.tensor_tensor(hC[t % 3], hb[t % 2], Cs, ALU.mult).then_inc(s["hc_done"], 1)
            pool.wait_ge(s["fst"], 2 * NT + 1)
            pool.wait_ge(s["sz_done"], NT)
            pool.tensor_tensor(rstd[:, :], ve[:, :], nhalf[:, 0:NT], ALU.pow).then_inc(s["fpow"], 1)
            pool.wait_ge(s["fsc"], 2)
            pool.tensor_tensor(q8[:, 1, :], q8[:, 0, :], phalf[:, 0:NT], ALU.pow).then_inc(s["fpow"], 1)
            for i in range(NT):
                pool.wait_ge(s["fact"], 3 * i + 3)
                pool.tensor_tensor(q8[:, 8, i:i + 1], q8[:, 7, i:i + 1], phalf[:, 0:1], ALU.pow).then_inc(s["fpow2"], 1)

            def attn_pow(b):
                pool.wait_ge(s["aln"], 5 * b + 5)
                if b == 0:
                    pool.wait_ge(s["fxl"], NT)
                pool.tensor_tensor(rstd[:, 2 * b:2 * b + 2], ve[:, 2 * b:2 * b + 2], nhalf[:, 0:2], ALU.pow).then_inc(s["apow"], 1)

            def square(p):
                pool.wait_ge(s["raw_done"], p + 1)
                if p >= 2:
                    pool.wait_ge(s["prs"], 2 * (p - 2) + 1)
                pool.tensor_tensor(psq[p % 2], praw[p % 4], praw[p % 4], ALU.mult).then_inc(s["psq_done"], 1)

            def piece_pow(p):
                G_, kind = divmod(p, 4)
                pool.wait_ge(s["prs"], 2 * p + 2)
                if kind >= 2:
                    if G_ >= RING:
                        pool.wait_ge(s["exps"], 2 * GRP * (G_ - RING + 1))
                    dst = rq[:, G_ % RING, :, kind - 2]
                else:
                    dst = rv[:, p % 4, :]
                pool.tensor_tensor(dst, rr[:, p % 4, :], nhalf[:, 0:GRP], ALU.pow).then_inc(s["prv_done"], 1)
                if kind < 2:
                    pool.wait_ge(s["prv_done"], p + 1)
                    pr = praw[p % 4].rearrange("p (a c) -> p a c", a=GRP)
                    pool.tensor_tensor(pr, pr, rv[:, p % 4, :].unsqueeze(2).to_broadcast([P, GRP, P]), ALU.mult
                                       ).then_inc(s["pnorm"], 1)

            def normalise(n):
                pool.wait_ge(s["hrec"], n + 1)
                pool.tensor_tensor(Pb[n % 4], Pb[n % 4], hs[:, n % 4, 6:8].unsqueeze(2).to_broadcast([P, 2, S]), ALU.mult
                                   ).then_inc(s["pnorm_done"], 1)

            attn_pow(0)
            for step in range(16 * B + FIRST_HEAD):
                n = step - FIRST_HEAD
                if step < 16 * B:
                    square(step)
                    piece_pow(step)
                if step % 16 == 8 and step // 16 + 1 < B:
                    attn_pow(step // 16 + 1)
                if 0 <= n < 16 * B:
                    normalise(n)
            pool.wait_ge(s["piece_done"], 16 * B)
            pool.dma_start(esel[:, :], d["esel"]).then_inc(s["ld_esel"], 16)
            pool.memset(cwHL, 0.0).then_inc(s["gws"], 1)
            for b in range(B):
                pool.wait_ge(s["mln"], 5 * b + 5)
                pool.tensor_tensor(rstd[:, 2 * b:2 * b + 2], ve[:, 2 * b:2 * b + 2], nhalf[:, 0:2], ALU.pow).then_inc(s["mpow"], 1)
            pool.tensor_copy(gwH[:, :, :], gw[:, :, :]).then_inc(s["gws"], 1)
            pool.wait_ge(s["gws"], 2)
            pool.tensor_tensor(gwL[:, :, :], gw[:, :, :], gwH[:, :, :].bitcast(F32), ALU.subtract).then_inc(s["gws"], 1)
            for m in range(2 * FT):
                rows = min(P, FALL - (m // 2) * P)
                pool.wait_ge(s["hH_done"], m + 1)
                pool.tensor_tensor(hL[m % 3][0:rows, :], hm[m % 2][0:rows, :], hH[m % 3][0:rows, :].bitcast(F32), ALU.subtract
                                   ).then_inc(s["hL_done"], 1)


RD_ALL = 5 * NT + 11


def kernel(**inputs):
    import concourse.bacc as bacc
    from concourse.bass_utils import run_bass_kernel_spmd

    a = {k: np.asarray(v) for k, v in inputs.items()}
    c = np.ascontiguousarray

    def rows(w, n):
        return w.reshape(n, P, -1).transpose(1, 0, 2)

    p, m = np.arange(P)[:, None], np.arange(P)[None, :]
    sel = np.stack([(p % 64 == 8 * j + m // NS) for j in range(8)], 1).astype(np.float32)
    win = np.arange(2 * P - CH)[None, :]
    nwin = (win == P - CH + p // NS).astype(np.float32)
    f = np.arange(FTR * P)[None, :]
    r = np.arange(64)[:, None]
    esel = ((r % 32 == f // F) & (r % 32 < E)).astype(np.float32)

    gate = np.concatenate([a["L1_ffn_w_gate"].reshape(E * F, DM), a["L1_ffn_sw_gate"]])
    up = np.concatenate([a["L1_ffn_w_up"].reshape(E * F, DM), a["L1_ffn_sw_up"]])
    dn = np.concatenate([a["L1_ffn_w_down"].transpose(0, 2, 1).reshape(E * F, DM), a["L1_ffn_sw_down"].T])
    moe = np.zeros((FT, P, 768), np.float32)
    for i in range(FT):
        n = min(P, FALL - i * P)
        s_ = slice(i * P, i * P + n)
        for k in range(2):
            moe[i, :, k * P:k * P + n] = gate[s_, k * P:k * P + P].T
            moe[i, :, 256 + k * P:256 + k * P + n] = up[s_, k * P:k * P + P].T
        moe[i, :n, 512:768] = dn[s_]
    xpw = a["L0_xattn_x_proj_w"]
    reps = [DR + np.arange(P) % NS, DR + NS + np.arange(P) % NS, np.arange(DR)]
    xpT = rows(np.concatenate([xpw[i] for i in reps]).T, 2)
    alog = a["L0_xattn_A_log"].reshape(ST, P).T
    arrays = {
        "x": a["x"], "ctx": a["ctx_1024"],
        "ctxT": c(a["ctx_1024"].reshape(T, DC).T),
        "inT": c(a["L0_xattn_in_proj_w"].T),
        "cw": c(a["L0_xattn_conv_w"].T.reshape(-1)),
        "ec": c(np.stack([a["L0_xattn_conv_b"], a["L0_xattn_dt_proj_b"], a["L0_xattn_D"]], 1).reshape(2, P, 3).transpose(1, 0, 2)),
        "gates": c(np.array([a["g_xattn"][0], a["g_ffn"][0], a["g_xattn"][1], a["g_ffn"][1]])),
        "xp": c(xpT), "dtw": c(a["L0_xattn_dt_proj_w"].T), "acol": c(alog),
        "gqk": c(np.stack([a["L1_xattn_gq"], a["L1_xattn_gk"]], 1)),
        "sel": sel, "nwin": nwin, "ident": np.eye(P, dtype=np.float32),
        "w1": c(rows(a["L0_ffn_w1"].T, 2).reshape(P, -1)), "w2": c(rows(a["L0_ffn_w2"].T, FT0).reshape(P, -1)),
        "Wq": c(rows(a["L1_xattn_Wq"], 2).reshape(P, -1)), "Wk": a["L1_xattn_Wk"],
        "WvT": c(a["L1_xattn_Wv"].reshape(DC, H, P).transpose(2, 1, 0).reshape(P, -1)),
        "Wo": c(rows(a["L1_xattn_Wo"], H).reshape(P, -1)),
        "gw": c(rows(a["L1_ffn_gate_weight"].T, 2)), "iota8": np.tile(np.arange(E, dtype=np.float32), (P, 1)),
        "moe": moe, "esel": esel,
    }
    nc = bacc.Bacc("TRN2", target_bir_lowering=False, num_devices=1)
    d = {n: nc.dram_tensor("in_" + n, v.shape, mybir.dt.from_np(v.dtype), kind="ExternalInput").ap() for n, v in arrays.items()}
    d["out"] = nc.dram_tensor("out", (B, S, DM), F32, kind="ExternalOutput").ap()
    build(nc, d)
    r_ = run_bass_kernel_spmd(nc, [{"in_" + n: v for n, v in arrays.items()}], core_ids=[0])
    return r_.results[0]["out"]
```

```python
from contextlib import ExitStack

import numpy as np

import concourse.bass as bass
from concourse import mybir

F32 = mybir.dt.float32
F32R = mybir.dt.float32r
BF16 = mybir.dt.bfloat16
U32 = mybir.dt.uint32
ALU = mybir.AluOpType
ACT = mybir.ActivationFunctionType
AX = mybir.AxisListType

P = 128
B, S, DM = 4, 256, 256
DC = 128
T = B * S
NT = T // P
DI, NS, TAPS, DR = 256, 16, 4, 8
PAD = 4
CH = P // NS
ST = DI // CH
JT = P // CH
INNER = 1024
FT0 = INNER // P
H = 16
E, F, FS = 8, 176, 352
FALL = E * F + FS
FT = -(-FALL // P)
FTR = E * F // P
EPS = 1e-5
MAGIC = 12582912.0
NSUM_LAG = 3
GRP = 4
RING = 3
FIRST = 3
ORDER = [(ft, c) for c in range(2) for ft in range(FIRST)] + [(ft, c) for ft in range(FIRST, FT) for c in range(2)]

AT = {
    "piece": -0.12, "piece_T": 2.3, "key_norm": 0.82,
    "scores": 6.22, "head_max": 6.1, "probs_T": 8.7, "values": 9.81, "project_out": 10.37,
    "f_stat": 2.6, "f_norm": 3.1, "f_quant": 3.57, "f_xqT": 4.6, "f_up": 5.6, "f_square": 6.35, "f_peak": 7.23, "f_scale": 8.33, "f_scale2": 8.8, "f_round": 8.94,
    "f_hT": 9.72, "f_down": 10.48, "second": 3, "a_stat": 14.22, "a_xn": 14.22, "a_lnT": 16.59,
    "f_stat0": -13.28, "f_norm0": -12.9, "f_quant0": -12.4, "f_xqT0": -11.4, "f_up0": -10.4, "f_square0": -9.7, "f_peak0": -8.84, "f_scale0": -8.2, "f_scale20": -7.9,
    "f_round0": -7.2, "f_hT0": -6.4, "f_down0": -5.4, "second0": 1, "a_stat0": -3.28, "a_xn0": -3.03, "a_lnT0": -2.22,
    "G0": -9.15, "w_low0": -11.1, "keys0": -2.94,
    "m_stat": 10.53, "m_xn": 11.7, "m_T": 11.85, "m_route": 12.73, "m_pick": 13.31, "m_weight": 13.75, "m_spread": 14.515, "m_cwT": 14.97,
    "m_stat3": -0.05, "m_xn3": 0.25, "m_T3": 0.77, "m_route3": 1.65, "m_pick3": 2.05, "m_weight3": 2.15, "m_spread3": 2.25, "m_cwT3": 3.135,
    "x_split1": 1.5,
    "gate": 0, "up": 0.27, "cw": 0.42, "down": 1.83, "w_split": 1.75,
}
END = 16 * B + 10.2


def plan():
    def at(base, k, *names):
        return [(base + AT[name], name, k) for name in names]

    for k in range(16 * B):
        if k < 2:
            yield AT["keys0"] + k, "piece", k
        else:
            yield from at(k, k, "piece")
        yield from at(k, k, "piece_T", "key_norm", "scores", "head_max", "probs_T", "values", "project_out")
    for b in range(B):
        t, x0 = (0, "0") if b == 0 else (16 * (b - 1), "")
        for name in ("f_stat", "f_norm", "f_quant", "f_xqT", "a_stat", "a_xn", "a_lnT"):
            yield t + AT[name + x0], name, b
        for a in range(2):
            for name in ("f_up", "f_square", "f_peak", "f_scale", "f_scale2", "f_round", "f_hT", "f_down"):
                yield t + AT[name + x0] + AT["second" + x0] * a, name, 2 * b + a
        t = 16 * b + 15
        if b < B - 1:
            yield from at(t, b, "m_stat", "m_xn", "m_T", "m_route", "m_pick", "m_weight", "m_spread", "m_cwT")
    for name in ("m_stat", "m_xn", "m_T", "m_route", "m_pick", "m_weight", "m_spread", "m_cwT"):
        yield END + AT[name + "3"], name, B - 1
    for g in range(4):
        yield AT["G0"] + g, "G", g
    for b in range(B):
        yield AT["f_stat0"] + (-.1, .1, .8, .9)[b], "x1", b
    for n in range(5):
        yield AT["w_low0"] + .8 * n, "w_low", n
    yield END - 2, "w_split", 0
    yield END - 1.8, "w_split", 1
    yield END + .6, "w_split", 2
    yield END - 1.5, "x_split", 0
    yield END + AT["x_split1"], "x_split", 1
    for m, (ft, c) in enumerate(ORDER):
        yield from at(END + m, m, "gate", "up", "cw", "down")
        if c == 1 and ft + FIRST < FT:
            yield from at(END + m, ft + FIRST, "w_split")


AFTER = {
    "act": {"piece": 0.13, "scores": 0.46, "probs_T": 0.25, "f_up": 0.1, "f_stat": 0, "G": -0.02, "a_lnT": 0.1, "m_route": 0.2,
            "x_split": 0.06, "w_split": -0.06, "gate": 0.55, "cw": 0.65},
    "dve": {"piece": 0.65, "head_max": 0.23, "scores": 0.59, "piece_T": 0.13, "values": 0.2, "project_out": 0.08, "f_xqT": 0.1,
            "f_hT": -0.025, "f_down": 0.32, "a_lnT": 0, "m_T": 0.35, "m_route": 0.13, "m_cwT": -0.12, "x_split": 0.35, "w_split": 0.09,
            "up": 0.3, "cw": 0.22},
    "pool": {"piece_T": 0.315, "f_norm": 0.2, "piece": 0.43, "scores": 0.74, "cw": 0.68, "f_peak": -0.07, "f_stat": 0.2, "a_stat": 0.2, "m_stat": 0.325},
}


def in_order(engine, mine):
    after = AFTER.get(engine, {})
    for _, name, k in sorted(((t + after.get(name, 0), name, k) for t, name, k in plan() if name in mine), key=lambda e: e[0]):
        mine[name](k)


def build(nc, d):
    with ExitStack() as ctx:
        def sb(name, shape, dt=F32):
            return ctx.enter_context(nc.sbuf_tensor(name, shape, dt))

        def sem(name):
            return ctx.enter_context(nc.semaphore(name))

        ps = ctx.enter_context(nc.psum_tensor("ps", [P, 8, 512], F32))

        x = sb("x", [P, NT, DM])
        ctxn = sb("ctxn", [P, NT, DC])
        ctxH = sb("ctxH", [P, B, PAD + S], F32R)
        ctxL = sb("ctxL", [P, B, PAD + S], F32R)
        inT = sb("inT", [P, DI])
        cstage = sb("cstage", [P, 2048])
        u = sb("u", [P, 2, T])
        xp = sb("xp", [P, 2, 2 * P + DR])
        bcz = sb("bcz", [P, 4096])
        rA = sb("rA", [P, 8192], F32R)
        rK = sb("rK", [P, 4096], F32R)
        sel = sb("sel", [P, 8, P], F32R)
        nwin = sb("nwin", [P, 2 * P - CH])
        work = sb("work", [P, 9216])
        stage = sb("stage", [P, 6144])
        w12q = sb("w12q", [P, 2, 2048], BF16)
        G = sb("G", [P, H, DM])
        xT = sb("xT", [P, 2, 2, 2, S], F32R)
        ident = sb("ident", [P, P])
        identb = sb("identb", [P, P], BF16)
        ones = sb("ones", [P, P])
        acol = sb("acol", [P, ST])
        nacol = sb("nacol", [P, ST])
        dtw = sb("dtw", [DR, DI])
        ec = sb("ec", [P, 2, 3])
        gates = sb("gates", [P, 4])
        tg = sb("tg", [P, 4])
        gqk = sb("gqk", [P, 2])
        gkq = sb("gkq", [P, 1])
        st6 = sb("st6", [P, NT, 6])
        mv = sb("mv", [P, NT, 2])
        ve = sb("ve", [P, NT])
        rstd = sb("rstd", [P, NT])
        nb8 = sb("nb8", [P, NT])
        phalf = sb("phalf", [P, 32])
        nhalf = sb("nhalf", [P, 32])
        q8 = sb("q8", [P, 10, NT])
        wsum = sb("wsum", [P, 2])
        mw = sb("mw", [P, 2])
        iw = sb("iw", [P, 2])
        k2 = sb("k2", [P, 1])
        rr = sb("rr", [P, 4, GRP])
        rv = sb("rv", [P, 4, GRP])
        rq = sb("rq", [P, RING, GRP, 2])
        hs = sb("hs", [P, 4, 8])
        gw = sb("gw", [P, 2, E])
        iota8 = sb("iota8", [P, E])
        cwR = sb("cwR", [P, 2, E], F32R)
        rti = sb("rti", [P, NT, E], U32)

        cwb = cstage[:, 0:TAPS * DI].rearrange("p (j e) -> p j e", j=TAPS)
        wc = cstage[:, 1024:2048].rearrange("p (j e) -> p j e", j=TAPS)
        wcH = rK[:, 0:1024].rearrange("p (j e) -> p j e", j=TAPS)
        wcL = rK[:, 2048:3072].rearrange("p (j e) -> p j e", j=TAPS)
        Bs, Cs = bcz[:, 0:T], bcz[:, T:2 * T]
        sz = bcz[:, 2 * T:4 * T].rearrange("p (i l) -> p i l", i=NT)
        XD = rA[:, 0:4096].rearrange("p (s t) -> p s t", s=4)
        XU = rA[:, 4096:8192].rearrange("p (s t) -> p s t", s=4)
        ctxTr = work[:, 0:T]
        selr = work[:, T:2 * T].rearrange("p (j m) -> p j m", j=8)
        dab = [work[:, 2048:3072], cstage[:, 0:1024]]
        dex = [work[:, 3072:4096], cstage[:, 1024:2048]]
        dlt = [work[:, 4096:5120], stage[:, 4096:5120]]
        dre = [work[:, 5120:6144], stage[:, 5120:6144]]
        dtl = work[0:DR, 8192:9216]
        dA = [work[:, i * T:(i + 1) * T] for i in (0, 1)]
        dBu = [work[:, i * T:(i + 1) * T] for i in (2, 3)]
        hb = [work[:, i * T:(i + 1) * T] for i in (4, 5)]
        hC = [work[:, i * T:(i + 1) * T] for i in (6, 7, 8)]
        wraw = [stage[:, 0:2048], stage[:, 2048:4096]]
        yg = stage[:, 4096:6144].rearrange("p (t n) -> p t n", t=2)
        uf = u[:, :, :].rearrange("p a n -> p (a n)")
        g1 = bcz[:, 0:1024]
        g2 = [bcz[:, 1024:2048], bcz[:, 2048:3072]]
        hq = bcz[:, 3072:3584].bitcast(BF16)
        hT = bcz[:, 3584:4096].bitcast(BF16).rearrange("p (k t) -> p k t", k=FT0)
        xl = uf[:, 0:512].rearrange("p (i c) -> p i c", i=2)
        xq = uf[:, 512:768].bitcast(BF16).rearrange("p (i c) -> p i c", i=2)
        xqT = uf[:, 768:1024].bitcast(BF16).rearrange("p (k t) -> p k t", k=2)
        w1q = w12q[:, 0, :].rearrange("p (k f) -> p k f", k=2)
        w2q = w12q[:, 1, :].rearrange("p (k o) -> p k o", k=FT0)
        Wqr = stage[:, 0:4096]
        Wkr = cstage[:, 0:2048]
        WqH = rA[:, 0:4096].rearrange("p (k n) -> p k n", k=2)
        WqL = rA[:, 4096:8192].rearrange("p (k n) -> p k n", k=2)
        WkH, WkL = rK[:, 0:2048], rK[:, 2048:4096]
        WvT = stage[:, 4096:6144].rearrange("p (h c) -> p h c", c=DC)
        kT = stage[:, 0:3072].rearrange("p (g h t) -> p g h t", g=RING, h=GRP)
        qT = stage[:, 3072:6144].rearrange("p (g h t) -> p g h t", g=RING, h=GRP)
        praw = [work[:, 512 * i:512 * i + 512] for i in range(2)]
        psq = [work[:, 1024 + 512 * i:1536 + 512 * i] for i in range(4)]
        Pb = [work[:, 3072 + 512 * i:3584 + 512 * i].rearrange("p (q k) -> p q k", q=2) for i in range(4)]
        PT = [work[:, 5120 + 512 * i:5632 + 512 * i].rearrange("p (k q) -> p k q", k=2) for i in range(3)]
        Us = [work[:, 6656 + 256 * i:6912 + 256 * i] for i in range(3)]
        xn = work[:, 7424:7936].rearrange("p (i c) -> p i c", i=2)
        xmH = rA[:, 0:2048].rearrange("p (k t) -> p k t", k=2)
        xmL = rA[:, 2048:4096].rearrange("p (k t) -> p k t", k=2)
        wr = [bcz[:, 768 * i:768 * i + 768] for i in range(4)]
        wH = [rA[:, 4096:4864], rA[:, 5632:6400], rA[:, 7168:7936]]
        wL = [rA[:, 4864:5632], rA[:, 6400:7168], sel[:, :, :].rearrange("p j m -> p (j m)")[:, 0:768]]
        hH = [rK[:, 1024 * i:1024 * i + 512] for i in range(3)]
        hL = [rK[:, 1024 * i + 512:1024 * i + 1024] for i in range(3)]
        sg = [work[:, 512 * i:512 * i + 512] for i in range(2)]
        hm = [work[:, 1024 + 512 * i:1536 + 512 * i] for i in range(2)]
        yo = [work[:, 2048 + 512 * i:2560 + 512 * i].rearrange("p (i c) -> p i c", i=2) for i in range(4)]
        xm = work[:, 7936:8448].rearrange("p (i c) -> p i c", i=2)
        cwHL = work[:, 8448:8576].rearrange("p (i m) -> p i m", i=2)
        rt = work[:, 8576:8960].rearrange("p (i a e) -> p i a e", i=NT, a=6)
        xmf = cstage[:, :].rearrange("p (k t) -> p k t", k=2)
        cwTf = uf[0:64, 1024:2048]
        esel = xT[0:64].rearrange("p a b k t -> p (a b k t)")[:, 0:FTR * P]
        cwT = rK[0:64, 3072:4096]

        s = {}
        for name in ("ld_ctxT ld_wc ld_x ld_sel ld_xp ld_small ld_w ld_ctxn ld_wq ld_wk ld_wo ld_wv ld_moe0 ld_moe1 ld_moe2 "
                     "ld_moe3 ld_esel ld_out dve_chain "
                     "pool_init ctx_split conv_w sel_ready conv_done u_done zstat zpow znb sz_done xproj_done "
                     "dtl_evac bc_evac dpre_done dabs drelu dexp done_1p dln ddelta dhi_done dlo_done "
                     "wabs wsum_done wq_done nacol_done gate_done "
                     "dbc_done ubc_done exp_done dbu_done scan_done hc_done nsum_done yevac yg_done yT_done x1_done "
                     "fst fpow fnorm fxl fscale fq fqT_done fqT_evac mm1_done g1_done fact fpow2 fhq fT_done fT_evac mm2_done "
                     "x2_done kst kpow qsum_done qst qpow G_done G_evac wk_split wqh wql "
                     "aln apow axn axT_done axTH axTL piece_done raw_done psq_done pnorm pT_done pT_evac "
                     "sc_done hmax exps hrec pnorm_done PT_done PT_evac U_done U_evac y_done x3_done "
                     "mln mpow mxn mxT_done mxT_evac cwz rl_done rneg rexp cw_ready cwT_done cwT_evac cwc xmh xml wsplit wsplitL "
                     "gate_mm up_mm cw_mm silu_done m1_done m2_done hH_done hL_done down_done out_done").split():
            s[name] = sem(name)
        block = ctx.enter_context(nc.Block())

        @block.sync
        def _(sp):
            sp.dma_start(inT[:, :], d["inT"]).then_inc(s["ld_wc"], 16)
            sp.dma_start(cstage[:, 0:1024], d["cw"].partition_broadcast(P)).then_inc(s["ld_wc"], 16)
            sp.dma_start(ctxTr, d["ctxT"]).then_inc(s["ld_ctxT"], 16)
            sp.dma_start(ec[:, :, :], d["ec"]).then_inc(s["ld_small"], 16)
            sp.dma_start(gates[:, :], d["gates"].partition_broadcast(P)).then_inc(s["ld_small"], 16)
            sp.dma_start(x[:, :, :], d["x"].rearrange("b (h p) c -> p (b h) c", p=P)).then_inc(s["ld_x"], 16)
            sp.dma_start(xp[:, :, :], d["xp"]).then_inc(s["ld_xp"], 16)
            sp.dma_start(dtw[:, :], d["dtw"]).then_inc(s["ld_small"], 16)
            sp.dma_start(acol[:, :], d["acol"]).then_inc(s["ld_small"], 16)
            sp.dma_start(gqk[:, :], d["gqk"]).then_inc(s["ld_small"], 16)
            sp.dma_start(selr, d["sel"]).then_inc(s["ld_sel"], 16)
            sp.dma_start(nwin[:, :], d["nwin"]).then_inc(s["ld_sel"], 16)
            sp.dma_start(ident[:, :], d["ident"]).then_inc(s["ld_sel"], 16)
            sp.dma_start(wraw[0], d["w1"]).then_inc(s["ld_w"], 16)
            sp.dma_start(wraw[1], d["w2"]).then_inc(s["ld_w"], 16)
            sp.dma_start(ctxn[:, :, :], d["ctx"].rearrange("b (h p) c -> p (b h) c", p=P)).then_inc(s["ld_ctxn"], 16)
            sp.dma_start(gw[:, :, :], d["gw"]).then_inc(s["ld_ctxn"], 16)
            sp.dma_start(iota8[:, :], d["iota8"]).then_inc(s["ld_ctxn"], 16)
            sp.dma_start(G[:, :, :].rearrange("p h o -> p (h o)"), d["Wo"]).then_inc(s["ld_wo"], 16)
            sp.wait_ge(s["wq_done"], 6)
            sp.dma_start(Wqr, d["Wq"]).then_inc(s["ld_wq"], 16)
            sp.wait_ge(s["dlo_done"], 8)
            sp.dma_start(Wkr, d["Wk"]).then_inc(s["ld_wk"], 16)
            sp.wait_ge(s["yT_done"], 2 * B)
            sp.dma_start(stage[:, 4096:6144], d["WvT"]).then_inc(s["ld_wv"], 16)
            sp.wait_ge(s["x2_done"], NT)
            for i in range(FT):
                if i >= 4:
                    sp.wait_ge(s["wsplitL"], i - 3)
                sp.dma_start(wr[i % 4], d["moe"][i]).then_inc(s[f"ld_moe{i % 4}"], 16)
            for b in range(B):
                sp.wait_ge(s["out_done"], 2 * b + 2)
                sp.dma_start(d["out"][b].rearrange("(h p) c -> p h c", p=P), yo[b]).then_inc(s["ld_out"], 16)
            sp.wait_ge(s["ld_out"], 16 * B)

        def three(pe, out, pairs):
            terms = [(a, r) for aH, aL, rH, rL in pairs for a, r in ((aH, rH), (aH, rL), (aL, rH))]
            for n, (a, r) in enumerate(terms):
                last = pe.matmul(out, a, r, start=(n == 0), stop=(n == len(terms) - 1))
            return last

        @block.tensor
        def _(pe):
            pe.wait_ge(s["ctx_split"], 2)
            pe.wait_ge(s["pool_init"], 5)
            pe.wait_ge(s["conv_w"], 3)
            for et in range(2):
                if et == 1:
                    pe.wait_ge(s["wabs"], 2)
                    pe.matmul(ps[:, 7, 0:2], ones[:, :], wsum[:, :], start=True, stop=True).then_inc(s["wsum_done"], 1)
                for hf in range(2):
                    pairs = []
                    for j in range(TAPS):
                        c0 = PAD - (TAPS - 1) + j
                        w_ = slice(et * P, et * P + P)
                        pairs.append((wcH[:, j, w_], wcL[:, j, w_], ctxH[:, 2 * hf:2 * hf + 2, c0:c0 + S],
                                      ctxL[:, 2 * hf:2 * hf + 2, c0:c0 + S]))
                    three(pe, ps[:, 2 * et + hf, :], pairs).then_inc(s["conv_done"], 1)
            pe.wait_ge(s["ld_xp"], 16)
            pe.wait_ge(s["u_done"], 4)

            def xproj(c0, m, bank):
                for hf in range(2):
                    for k in range(2):
                        last = pe.matmul(ps[0:m, bank + hf, :], xp[:, k, c0:c0 + m], u[:, k, 512 * hf:512 * hf + 512],
                                         start=(k == 0), stop=(k == 1))
                last.then_inc(s["xproj_done"], 1)

            xproj(2 * P, DR, 0)
            pe.wait_ge(s["ld_small"], 80)
            pe.wait_ge(s["dtl_evac"], 1)
            for et in range(2):
                if et == 1:
                    pe.wait_ge(s["wq_done"], 1)
                    xproj(0, P, 6)
                for hf in range(2):
                    last = pe.matmul(ps[:, 2 + 2 * et + hf, :], dtw[:, et * P:et * P + P], dtl[:, 512 * hf:512 * hf + 512],
                                     start=True, stop=True)
                last.then_inc(s["dpre_done"], 1)
            xproj(P, P, 0)
            def nsum(t):
                et, jj = divmod(t, JT)
                pe.wait_ge(s["hc_done"], t + 1)
                if t == JT:
                    pe.wait_ge(s["yevac"], 1)
                for hf in range(2):
                    if t == ST - 1:
                        pe.wait_ge(s["hc_done"], t + 1 + hf)
                    last = pe.matmul(ps[:, 6 + hf, :], nwin[:, P - CH - CH * jj:2 * P - CH - CH * jj],
                                     hC[t % 3][:, 512 * hf:512 * hf + 512], start=(jj == 0), stop=(jj == JT - 1))
                    if t == ST - 1 or hf == 1:
                        last.then_inc(s["nsum_done"], 1)

            pe.wait_ge(s["sel_ready"], 1)
            pe.wait_ge(s["bc_evac"], 2)
            pe.wait_ge(s["drelu"], 2)
            for t in range(ST):
                g, j = divmod(t, 8)
                if j == 0:
                    pe.wait_ge(s["dlo_done"], 2 * g + 2)
                if t >= 1:
                    pe.wait_ge(s["exp_done"], t)
                for hf in range(2):
                    last = pe.matmul(ps[:, hf, :], sel[:, j, :], XD[:, g, 512 * hf:512 * hf + 512], start=True, stop=True)
                last.then_inc(s["dbc_done"], 1)
                if t >= 2:
                    pe.wait_ge(s["dbu_done"], t - 1)
                for hf in range(2):
                    last = pe.matmul(ps[:, 2 + 2 * (t % 2) + hf, :], sel[:, j, :], XU[:, g, 512 * hf:512 * hf + 512],
                                     start=True, stop=True)
                last.then_inc(s["ubc_done"], 1)
                if t >= NSUM_LAG:
                    nsum(t - NSUM_LAG)
            for t in range(ST - NSUM_LAG, ST):
                nsum(t)
            pe.wait_ge(s["exp_done"], ST)
            pe.wait_ge(s["dbu_done"], ST)
            pe.wait_ge(s["yg_done"], 1)
            for et in range(2):
                for b in range(B):
                    if et == 1:
                        pe.wait_ge(s["yg_done"], b + 2)
                    for lh in range(2):
                        last = pe.transpose(ps[:, b, lh * DM + et * P:lh * DM + et * P + P],
                                            yg[:, et, b * S + lh * P:b * S + lh * P + P], ident[:, :])
                    last.then_inc(s["yT_done"], 1)
            free = {6: ("yevac", 3), 7: ("yevac", 5)}

            def take(bank, sem_, value):
                pe.wait_ge(s[free[bank][0]], free[bank][1])
                free[bank] = (sem_, value)

            def f_xqT(b):
                pe.wait_ge(s["fq"], b + 1)
                take(7, "fqT_evac", b + 1)
                for k in range(2):
                    for i in range(2):
                        last = pe.transpose(ps[:, 7, :].bitcast(BF16)[:, k * S + i * P:k * S + i * P + P],
                                            xq[:, i, k * P:k * P + P], identb[:, :])
                last.then_inc(s["fqT_done"], 1)

            def f_up(i):
                pe.wait_ge(s["fqT_evac"], i // 2 + 1)
                pe.wait_ge(s["wq_done"], 6)
                for n in range(2):
                    take(6 + n, "g1_done", 2 * i + n + 1)
                    for k in range(2):
                        last = pe.matmul(ps[:, 6 + n, :], xqT[:, k, (i % 2) * P:(i % 2) * P + P],
                                         w1q[:, k, 512 * n:512 * n + 512], start=(k == 0), stop=(k == 1))
                    last.then_inc(s["mm1_done"], 1)

            def f_hT(i):
                pe.wait_ge(s["fhq"], i + 1)
                take(7, "fT_evac", i + 1)
                for k in range(FT0):
                    last = pe.transpose(ps[:, 7, :].bitcast(BF16)[:, k * P:k * P + P], hq[:, k * P:k * P + P], identb[:, :])
                last.then_inc(s["fT_done"], 1)

            def f_down(i):
                pe.wait_ge(s["fT_evac"], i + 1)
                take(6, "x2_done", i + 1)
                for k in range(FT0):
                    last = pe.matmul(ps[:, 6, 0:DM], hT[:, k, :], w2q[:, k, :], start=(k == 0), stop=(k == FT0 - 1))
                last.then_inc(s["mm2_done"], 1)

            def value_out(g):
                if g == 0:
                    pe.wait_ge(s["ld_wo"], 16)
                    pe.wait_ge(s["ld_wv"], 16)
                    pe.wait_ge(s["x1_done"], B)
                for n in (2 * g, 2 * g + 1):
                    if n >= 2:
                        pe.wait_ge(s["G_evac"], n - 1)
                    for a in range(2):
                        last = pe.matmul(ps[:, 4 + n % 2, a * DM:(a + 1) * DM], WvT[:, 2 * n + a, :], G[:, 2 * n + a, :],
                                         start=True, stop=True)
                    last.then_inc(s["G_done"], 1)

            def a_lnT(b):
                pe.wait_ge(s["axn"], 2 * b + 2)
                take(7, "axTL", b + 1)
                for k in range(2):
                    for i in range(2):
                        last = pe.transpose(ps[:, 7, k * S + i * P:k * S + i * P + P], xn[:, i, k * P:k * P + P], ident[:, :])
                last.then_inc(s["axT_done"], 1)

            def piece(p):
                b, r = divmod(p, 16)
                g, kind = divmod(r, 4)
                take(6, "raw_done", p + 1)
                if kind < 2:
                    if p == 0:
                        pe.wait_ge(s["wk_split"], 2)
                    n_ = slice(g * 512, g * 512 + 512)
                    a_ = slice(PAD + kind * P, PAD + kind * P + P)
                    last = three(pe, ps[:, 6, :], [(ctxH[:, b, a_], ctxL[:, b, a_], WkH[:, n_], WkL[:, n_])])
                else:
                    pe.wait_ge(s["axTH"], b + 1)
                    pe.wait_ge(s["axTL"], b + 1)
                    pe.wait_ge(s["wqh"], 4)
                    pe.wait_ge(s["wql"], 4)
                    for a in range(2):
                        h = GRP * g + 2 * (kind - 2) + a
                        n_ = slice(h * P, h * P + P)
                        last = three(pe, ps[:, 6, a * S:a * S + S],
                                     [(WqH[:, k, n_], WqL[:, k, n_], xT[:, b % 2, 0, k, :], xT[:, b % 2, 1, k, :]) for k in range(2)])
                last.then_inc(s["piece_done"], 1)

            def piece_T(p):
                G_, kind = divmod(p, 4)
                j = 2 * G_ + kind % 2
                if kind < 2:
                    pe.wait_ge(s["pnorm"], j + 1)
                    take(7, "pT_evac", j + 1)
                    for a in range(GRP):
                        last = pe.transpose(ps[:, 7, a * P:a * P + P], praw[kind][:, a * P:a * P + P], ident[:, :])
                    last.then_inc(s["pT_done"], 1)
                else:
                    pe.wait_ge(s["psq_done"], p + 1)
                    take(7, "qst", j + 1)
                    for a in range(4):
                        last = pe.matmul(ps[:, 7, a:a + 1], psq[kind][:, a * P:a * P + P], ones[:, 0:1], start=True, stop=True)
                    last.then_inc(s["qsum_done"], 1)

            def scores(n):
                G_, a = divmod(n, GRP)
                if a == 0:
                    pe.wait_ge(s["pT_evac"], 2 * G_ + 2)
                    pe.wait_ge(s["raw_done"], 4 * G_ + 4)
                if n >= 2:
                    pe.wait_ge(s["exps"], 2 * (n - 1))
                for qt in range(2):
                    last = pe.matmul(ps[:, n % 2, qt * S:qt * S + S], qT[:, G_ % RING, a, qt * P:qt * P + P],
                                     kT[:, G_ % RING, a, :], start=True, stop=True)
                last.then_inc(s["sc_done"], 1)

            def probs_T(n):
                pe.wait_ge(s["pnorm_done"], n + 1)
                if n >= 2:
                    pe.wait_ge(s["PT_evac"], n - 1)
                for kt in range(2):
                    for qt in range(2):
                        last = pe.transpose(ps[:, 2 + n % 2, kt * S + qt * P:kt * S + qt * P + P],
                                            Pb[n % 4][:, qt, kt * P:kt * P + P], ident[:, :])
                last.then_inc(s["PT_done"], 1)

            def values(n):
                b = n // H
                if n == 0:
                    pe.wait_ge(s["G_evac"], H // 2)
                    pe.wait_ge(s["ld_ctxn"], 48)
                pe.wait_ge(s["PT_evac"], n + 1)
                if n >= 1:
                    pe.wait_ge(s["U_evac"], n)
                for kt in range(2):
                    last = pe.matmul(ps[:, 4, 0:S], ctxn[:, 2 * b + kt, :], PT[n % 3][:, kt, :], start=(kt == 0), stop=(kt == 1))
                last.then_inc(s["U_done"], 1)

            def project_out(n):
                b, h = divmod(n, H)
                pe.wait_ge(s["U_evac"], n + 1)
                if h == 0 and b >= 1:
                    pe.wait_ge(s["x3_done"], b)
                for qt in range(2):
                    last = pe.matmul(ps[:, 5, qt * DM:qt * DM + DM], Us[n % 3][:, qt * P:qt * P + P], G[:, h, :],
                                     start=(h == 0 and qt == 0), stop=(h == H - 1), skip_group_check=True)
                last.then_inc(s["y_done"], 1)

            def m_T(b):
                pe.wait_ge(s["mxn"], 2 * b + 2)
                take(7, "mxT_evac", b + 1)
                for k in range(2):
                    for i in range(2):
                        last = pe.transpose(ps[:, 7, k * S + i * P:k * S + i * P + P], xm[:, i, k * P:k * P + P], ident[:, :])
                last.then_inc(s["mxT_done"], 1)

            def m_route(b):
                pe.wait_ge(s["mxT_evac"], b + 1)
                take(7, "rexp", 2 * b + 2)
                for i in range(2 * b, 2 * b + 2):
                    for k in range(2):
                        last = pe.matmul(ps[:, 7, i * E:i * E + E], xmf[:, k, i * P:i * P + P], gw[:, k, :],
                                         start=(k == 0), stop=(k == 1))
                last.then_inc(s["rl_done"], 1)

            def m_cwT(b):
                pe.wait_ge(s["cw_ready"], b + 1)
                take(7, "cwT_evac", b + 1)
                for i in range(2):
                    last = pe.transpose(ps[0:64, 7, i * P:i * P + P], cwHL[:, i, :], ident[:, :])
                last.then_inc(s["cwT_done"], 1)

            def product(m, which, bank):
                ft, c = ORDER[m]
                rows = min(P, FALL - ft * P)
                t_ = slice(c * 512, c * 512 + 512)
                return three(pe, ps[0:rows, bank, :],
                             [(wH[ft % FIRST][:, 256 * which + k * P:256 * which + k * P + rows],
                               wL[ft % FIRST][:, 256 * which + k * P:256 * which + k * P + rows],
                               xmH[:, k, t_], xmL[:, k, t_]) for k in range(2)])

            def gate(m):
                ft, c = ORDER[m]
                if m == 0:
                    pe.wait_ge(s["U_evac"], 16 * B)
                    pe.wait_ge(s["x3_done"], B)
                    pe.wait_ge(s["raw_done"], 16 * B)
                    pe.wait_ge(s["ld_esel"], 16)
                pe.wait_ge(s["xmh"], 2 * c + 2)
                pe.wait_ge(s["xml"], 2 * c + 2)
                pe.wait_ge(s["wsplit"], ft + 1)
                pe.wait_ge(s["wsplitL"], ft + 1)
                if m >= 1:
                    pe.wait_ge(s["silu_done"], m)
                product(m, 0, 4).then_inc(s["gate_mm"], 1)

            def up(m):
                if m >= 1:
                    pe.wait_ge(s["m1_done"], m)
                product(m, 1, 5).then_inc(s["up_mm"], 1)

            def cw(m):
                ft, c = ORDER[m]
                t_ = slice(c * 512, c * 512 + 512)
                if ft < FTR:
                    pe.wait_ge(s["cwc"], c + 1)
                    if m >= 1:
                        pe.wait_ge(s["m2_done"], m)
                    pe.matmul(ps[:, 6, :], esel[:, ft * P:ft * P + P], cwT[:, t_], start=True, stop=True).then_inc(s["cw_mm"], 1)

            def down(m):
                ft, c = ORDER[m]
                rows = min(P, FALL - ft * P)
                pe.wait_ge(s["hL_done"], m + 1)
                if m == 0:
                    pe.wait_ge(s["exps"], 2 * 16 * B)
                    pe.wait_ge(s["PT_evac"], 16 * B)
                for tt in range(4):
                    i = 4 * c + tt
                    a_ = slice(tt * P, tt * P + P)
                    terms = ((hH[m % 3], wH[ft % FIRST]), (hH[m % 3], wL[ft % FIRST]), (hL[m % 3], wH[ft % FIRST]))
                    for z, (a, w) in enumerate(terms):
                        last = pe.matmul(ps[:, i // 2, (i % 2) * DM:(i % 2) * DM + DM], a[0:rows, a_], w[0:rows, 512:768],
                                         start=(ft == 0 and z == 0 and i % 2 == 0), stop=(ft == FT - 1 and z == 2),
                                         skip_group_check=True)
                last.then_inc(s["down_done"], 1)

            mine = dict(piece=piece, scores=scores, piece_T=piece_T, probs_T=probs_T, project_out=project_out, values=values,
                        f_xqT=f_xqT, f_up=f_up, f_hT=f_hT, f_down=f_down, G=value_out, a_lnT=a_lnT, m_T=m_T, m_route=m_route,
                        m_cwT=m_cwT, gate=gate, up=up, cw=cw, down=down)
            in_order("pe", mine)

        @block.scalar
        def _(act):
            act.wait_ge(s["ld_small"], 80)
            act.activation(tg[:, :], gates[:, :], ACT.Tanh).then_inc(s["gate_done"], 1)
            act.wait_ge(s["ld_sel"], 48)
            act.copy(identb[:, :], ident[:, :]).then_inc(s["gate_done"], 1)
            gated_tiles = ((0, 1, 2), (3, 4), (5, 6, 7), ())
            for et in range(2):
                for hf in range(2):
                    act.wait_ge(s["conv_done"], 2 * et + hf + 1)
                    act.activation(u[:, et, 512 * hf:512 * hf + 512], ps[:, 2 * et + hf, :], ACT.Silu,
                                   bias=ec[:, et, 0:1]).then_inc(s["u_done"], 1)
                    act.wait_ge(s["znb"], 1)
                    for i in gated_tiles[2 * et + hf]:
                        act.activation(sz[:, i, :], x[:, i, :], ACT.Silu, bias=nb8[:, i:i + 1], scale=rstd[:, i:i + 1]
                                       ).then_inc(s["sz_done"], 1)
            act.wait_ge(s["xproj_done"], 1)
            act.copy(dtl, ps[0:DR, 0:2, :].rearrange("p a n -> p (a n)")).then_inc(s["dtl_evac"], 1)
            act.preload_act_table_set("natural_log_exp_and_others")
            act.activation(nacol[:, :], acol[:, :], ACT.Exp).then_inc(s["nacol_done"], 1)
            def soft_abs(et):
                act.wait_ge(s["dpre_done"], et + 1)
                act.activation(dab[et], ps[:, 2 + 2 * et:4 + 2 * et, :].rearrange("p a n -> p (a n)"), ACT.Abs,
                               bias=ec[:, et, 1:2]).then_inc(s["dabs"], 1)

            def soft_exp(et):
                act.wait_ge(s["dabs"], et + 1)
                act.activation(dex[et], dab[et], ACT.Exp, scale=-1.0).then_inc(s["dexp"], 1)

            def soft_1p(et):
                act.wait_ge(s["dexp"], et + 1)
                act.activation(dab[et], dex[et], ACT.Identity, bias=ones[:, 0:1]).then_inc(s["done_1p"], 1)

            def soft_ln(et):
                act.wait_ge(s["done_1p"], et + 1)
                act.activation(dlt[et], dab[et], ACT.Ln).then_inc(s["dln"], 1)

            def soft_hi(et, half):
                r_ = slice(64 * half, 64 * half + 64)
                act.wait_ge(s["ddelta"], 2 * et + 1)
                act.copy(XD[r_, 2 * et + half, :], dlt[et][r_]).then_inc(s["dhi_done"], 1)
                act.wait_ge(s["ddelta"], 2 * et + 2)
                act.copy(XU[r_, 2 * et + half, :], dab[et][r_]).then_inc(s["dhi_done"], 1)

            soft_abs(0)
            soft_exp(0)
            soft_1p(0)
            soft_ln(0)
            act.wait_ge(s["xproj_done"], 2)
            act.copy(Bs, ps[:, 6:8, :].rearrange("p a n -> p (a n)")).then_inc(s["bc_evac"], 1)
            soft_hi(0, 0)
            soft_hi(0, 1)
            soft_abs(1)
            act.wait_ge(s["xproj_done"], 3)
            act.copy(Cs, ps[:, 0:2, :].rearrange("p a n -> p (a n)")).then_inc(s["bc_evac"], 1)
            act.wait_ge(s["nacol_done"], 2)
            act.wait_ge(s["pool_init"], 7)
            for t in range(ST):
                act.wait_ge(s["dbc_done"], t + 1)
                if t >= 2:
                    act.wait_ge(s["scan_done"], t - 1)
                act.activation(dA[t % 2].rearrange("p (b l) -> p b l", b=B)[:, :, 1:S],
                               ps[:, 0:2, :].rearrange("p a (b l) -> p (a b) l", b=2)[:, :, 1:S], ACT.Exp,
                               scale=nacol[:, t:t + 1]).then_inc(s["exp_done"], 1)
                if t == 1:
                    soft_exp(1)
                if t == 2:
                    soft_1p(1)
                if t == 4:
                    soft_ln(1)
                if t in (9, 11):
                    soft_hi(1, (t - 9) // 2)

            def f_up(i):
                act.wait_ge(s["fscale"], i // 2 + 1)
                if i >= 1:
                    act.wait_ge(s["fact"], 2 * i)
                for n in range(2):
                    act.wait_ge(s["mm1_done"], 2 * i + n + 1)
                    act.activation(g1[:, 512 * n:512 * n + 512], ps[:, 6 + n, :], ACT.Gelu, scale=q8[:, 6, i:i + 1]
                                   ).then_inc(s["g1_done"], 1)
                act.wait_ge(s["g1_done"], 2 * i + 2)
                if i >= 2:
                    act.wait_ge(s["fhq"], i - 1)
                act.activation(g2[i % 2], g1, ACT.Gelu).then_inc(s["fact"], 1)

            def f_square(i):
                act.wait_ge(s["fact"], 2 * i + 1)
                act.activation(g1, g2[i % 2], ACT.Square, accum_out=q8[:, 7, i:i + 1]).then_inc(s["fact"], 1)

            def value_out(g):
                for n in (2 * g, 2 * g + 1):
                    act.wait_ge(s["G_done"], n + 1)
                    act.copy(G[:, 2 * n:2 * n + 2, :].rearrange("p a n -> p (a n)"), ps[:, 4 + n % 2, :]).then_inc(s["G_evac"], 1)

            def f_stat(b):
                if b == 0:
                    act.wait_ge(s["ld_wq"], 16)
                    act.wait_ge(s["ubc_done"], ST)
                    for n in range(4):
                        k, c = divmod(n, 2)
                        act.copy(WqH[:, k, 1024 * c:1024 * c + 1024], Wqr[:, 1024 * n:1024 * n + 1024]).then_inc(s["wqh"], 1)

            def a_lnT(b):
                act.wait_ge(s["axT_done"], b + 1)
                if b >= 2:
                    act.wait_ge(s["piece_done"], 16 * (b - 1))
                act.copy(xT[:, b % 2, 0, :, :].rearrange("p k t -> p (k t)"), ps[:, 7, :]).then_inc(s["axTH"], 1)

            def piece(p):
                G_, kind = divmod(p, 4)
                act.wait_ge(s["piece_done"], p + 1)
                if kind < 2:
                    if G_ >= 1:
                        act.wait_ge(s["pT_done"], 2 * G_ + kind - 1)
                        act.wait_ge(s["psq_done"], p - 3)
                    act.copy(praw[kind], ps[:, 6, :]).then_inc(s["raw_done"], 1)
                else:
                    if G_ == 0:
                        act.wait_ge(s["wql"], 4)
                        act.wait_ge(s["G_done"], H // 2)
                    if G_ >= RING:
                        act.wait_ge(s["sc_done"], GRP * (G_ - RING + 1))
                    a = 2 * (kind - 2)
                    act.copy(qT[:, G_ % RING, a:a + 2, :], ps[:, 6, :].rearrange("p (a t) -> p a t", a=2)).then_inc(s["raw_done"], 1)

            def softmax(n):
                act.wait_ge(s["hmax"], 2 * n + 2)
                if n >= 4:
                    act.wait_ge(s["PT_done"], n - 3)
                for qt in range(2):
                    act.activation(Pb[n % 4][:, qt, :], ps[:, n % 2, qt * S:qt * S + S], ACT.Exp,
                                   bias=hs[:, n % 4, 2 + qt:3 + qt], scale=rq[:, (n // GRP) % RING, n % GRP, qt:qt + 1],
                                   accum_out=hs[:, n % 4, 4 + qt:5 + qt]).then_inc(s["exps"], 1)

            def PT_half(n):
                act.wait_ge(s["PT_done"], n + 1)
                if n >= 3:
                    act.wait_ge(s["U_done"], n - 2)
                act.copy(PT[n % 3].rearrange("p k q -> p (k q)"), ps[:, 2 + n % 2, :]).then_inc(s["PT_evac"], 1)

            def m_route(b):
                act.wait_ge(s["rneg"], 2 * b + 2)
                for i in range(2 * b, 2 * b + 2):
                    act.activation(rt[:, i, 0, :], ps[:, 7, i * E:i * E + E], ACT.Exp, bias=rt[:, i, 4, 0:1],
                                   accum_out=rt[:, i, 4, 1:2]).then_inc(s["rexp"], 1)

            def x_split(c):
                act.wait_ge(s["mxT_evac"], 2 * c + 2)
                act.wait_ge(s["piece_done"], 16 * B)
                for k in range(2):
                    act.copy(xmH[:, k, c * 512:c * 512 + 512], xmf[:, k, c * 512:c * 512 + 512]).then_inc(s["xmh"], 1)

            def w_split(ft):
                act.wait_ge(s[f"ld_moe{ft % 4}"], 16 * (ft // 4 + 1))
                act.wait_ge(s["piece_done"], 16 * B)
                if ft >= FIRST:
                    act.wait_ge(s["down_done"], ORDER.index((ft - FIRST, 1)) + 1)
                act.copy(wH[ft % FIRST], wr[ft % 4]).then_inc(s["wsplit"], 1)

            def silu(m):
                rows = min(P, FALL - ORDER[m][0] * P)
                act.wait_ge(s["gate_mm"], m + 1)
                if m == 0:
                    act.wait_ge(s["pT_done"], 8 * B)
                    act.wait_ge(s["psq_done"], 16 * B)
                if m >= 2:
                    act.wait_ge(s["m1_done"], m - 1)
                act.activation(sg[m % 2][0:rows, :], ps[0:rows, 4, :], ACT.Silu).then_inc(s["silu_done"], 1)

            def hidden_hi(m):
                rows = min(P, FALL - ORDER[m][0] * P)
                if m < 2 * FTR:
                    act.wait_ge(s["m2_done"], m + 1)
                else:
                    act.wait_ge(s["m1_done"], m + 1)
                if m >= 3:
                    act.wait_ge(s["down_done"], m - 2)
                act.copy(hH[m % 3][0:rows, :], hm[m % 2][0:rows, :]).then_inc(s["hH_done"], 1)

            mine = dict(piece=piece, scores=softmax, probs_T=PT_half, f_stat=f_stat, f_up=f_up, f_square=f_square, G=value_out, a_lnT=a_lnT,
                        m_route=m_route, x_split=x_split, w_split=w_split, gate=silu, cw=hidden_hi)
            in_order("act", mine)

        @block.vector
        def _(dve):
            chain = [0]

            def link(ins):
                chain[0] += 1
                ins.then_inc(s["dve_chain"], 1)
                dve.wait_ge(s["dve_chain"], chain[0])

            dve.wait_ge(s["ld_ctxT"], 16)
            src = ctxTr.rearrange("p (b l) -> p b l", b=B)
            dve.tensor_copy(ctxH[:, :, PAD:], src).then_inc(s["ctx_split"], 1)
            dve.wait_ge(s["ld_wc"], 32)
            dve.tensor_tensor(wc, cwb, inT[:, :].unsqueeze(1).to_broadcast([P, TAPS, DI]), ALU.mult).then_inc(s["conv_w"], 1)
            dve.wait_ge(s["ctx_split"], 1)
            dve.tensor_tensor(ctxL[:, :, PAD:], src, ctxH[:, :, PAD:].bitcast(F32), ALU.subtract).then_inc(s["ctx_split"], 1)
            dve.wait_ge(s["conv_w"], 1)
            dve.tensor_copy(wcH, wc).then_inc(s["conv_w"], 1)
            dve.wait_ge(s["conv_w"], 2)
            dve.tensor_tensor(wcL, wc, wcH.bitcast(F32), ALU.subtract).then_inc(s["conv_w"], 1)
            dve.wait_ge(s["ld_x"], 16)
            dve.wait_ge(s["pool_init"], 5)

            def stats(tiles, name, base):
                for i in tiles:
                    dve.bn_stats(st6[:, i, :], x[:, i, :]).then_inc(s[name], 1)
                dve.wait_ge(s[name], base + len(tiles))
                for i in tiles:
                    dve.bn_aggr(mv[:, i, :], st6[:, i, :]).then_inc(s[name], 1)
                dve.wait_ge(s[name], base + 2 * len(tiles))
                a, z = tiles[0], tiles[-1] + 1
                dve.tensor_scalar(ve[:, a:z], mv[:, a:z, 1], EPS, None, ALU.add).then_inc(s[name], 1)

            stats(range(NT), "zstat", 0)
            dve.wait_ge(s["zpow"], 1)
            dve.scalar_tensor_tensor(nb8[:, :], mv[:, :, 0], -1.0, rstd[:, :], ALU.mult, ALU.mult).then_inc(s["znb"], 1)
            dve.wait_ge(s["ld_sel"], 48)
            dve.tensor_copy(sel[:, :, :], selr).then_inc(s["sel_ready"], 1)
            dve.wait_ge(s["ld_w"], 32)
            for w in range(2):
                dve.tensor_reduce(wsum[:, w:w + 1], wraw[w], AX.X, ALU.add, apply_absolute_value=True).then_inc(s["wabs"], 1)
            dve.wait_ge(s["wsum_done"], 1)
            dve.tensor_scalar(mw[:, :], ps[:, 7, 0:2], 1.0 / (INNER * DM), EPS, ALU.mult, ALU.max).then_inc(s["wq_done"], 1)
            dve.wait_ge(s["wq_done"], 1)
            link(dve.reciprocal(iw[:, :], mw[:, :]))

            def ternary(w, part):
                if part == 0:
                    link(dve.tensor_scalar(wraw[w], wraw[w], iw[:, w:w + 1], 1.0, ALU.mult, ALU.min))
                elif part == 1:
                    link(dve.tensor_scalar(wraw[w], wraw[w], -1.0, MAGIC, ALU.max, ALU.add))
                else:
                    dve.tensor_scalar(w12q[:, w, :], wraw[w], MAGIC, None, ALU.subtract).then_inc(s["wq_done"], 1 if w == 0 else 4)

            for part in range(3):
                for w in range(2):
                    ternary(w, part)

            dve.wait_ge(s["nacol_done"], 1)
            dve.tensor_scalar(nacol[:, :], nacol[:, :], -1.0, None, ALU.mult).then_inc(s["nacol_done"], 1)

            def soft_relu(et):
                dve.wait_ge(s["dpre_done"], et + 1)
                dve.wait_ge(s["dabs"], et + 1)
                pw = ps[:, 2 + 2 * et:4 + 2 * et, :].rearrange("p a n -> p (a n)")
                dve.tensor_scalar(dre[et], pw, ec[:, et, 1:2], 0.0, ALU.add, ALU.max).then_inc(s["drelu"], 1)

            def soft_1p(et):
                dve.wait_ge(s["done_1p"], et + 1)
                link(dve.scalar_tensor_tensor(dex[et], dab[et], 1.0, dex[et], ALU.subtract, ALU.subtract))
                dve.wait_ge(s["drelu"], et + 1)
                link(dve.tensor_tensor(dex[et], dre[et], dex[et], ALU.subtract))

            def soft_delta(et):
                dve.wait_ge(s["dln"], et + 1)
                dve.tensor_tensor(dlt[et], dlt[et], dex[et], ALU.add).then_inc(s["ddelta"], 1)
                dve.wait_ge(s["ddelta"], 2 * et + 1)
                dve.tensor_tensor(dab[et], dlt[et], u[:, et, :], ALU.mult).then_inc(s["ddelta"], 1)

            def soft_lo(et, half):
                r_ = slice(64 * half, 64 * half + 64)
                o_ = slice(64 - 64 * half, 128 - 64 * half)
                dve.wait_ge(s["dhi_done"], 4 * et + 2 * half + 1)
                dve.tensor_tensor(XD[o_, 2 * et + half, :], dlt[et][r_], XD[r_, 2 * et + half, :].bitcast(F32), ALU.subtract
                                  ).then_inc(s["dlo_done"], 1)
                dve.wait_ge(s["ddelta"], 2 * et + 2)
                dve.wait_ge(s["dhi_done"], 4 * et + 2 * half + 2)
                dve.tensor_tensor(XU[o_, 2 * et + half, :], dab[et][r_], XU[r_, 2 * et + half, :].bitcast(F32), ALU.subtract
                                  ).then_inc(s["dlo_done"], 1)

            soft_relu(0)
            soft_1p(0)
            soft_delta(0)
            soft_lo(0, 0)
            soft_lo(0, 1)
            soft_relu(1)

            def dbu(t):
                dve.wait_ge(s["ubc_done"], t + 1)
                if t >= 2:
                    dve.wait_ge(s["scan_done"], t - 1)
                if t == 0:
                    dve.wait_ge(s["dlo_done"], 4)
                    dve.wait_ge(s["bc_evac"], 1)
                pu = ps[:, 2 + 2 * (t % 2):4 + 2 * (t % 2), :].rearrange("p a n -> p (a n)")
                dve.tensor_tensor(dBu[t % 2], pu, Bs, ALU.mult).then_inc(s["dbu_done"], 1)

            def y_last(b):
                c_ = slice(b * S, b * S + S)
                dve.wait_ge(s["nsum_done"], ST + b // 2)
                dve.scalar_tensor_tensor(yg[:, 1, c_], u[:, 1, c_], ec[:, 1, 2:3], ps[:, 6 + b // 2, (b % 2) * S:(b % 2) * S + S],
                                         ALU.mult, ALU.add).then_inc(s["yevac"], 1)
                dve.wait_ge(s["yevac"], b + 2)
                ygv = yg[:, 1, c_]
                dve.tensor_tensor(ygv, ygv, sz[:, 2 * b + 1, :], ALU.mult).then_inc(s["yg_done"], 1)

            def y_out(et):
                dve.wait_ge(s["nsum_done"], JT * (et + 1))
                py = ps[:, 6:8, :].rearrange("p a n -> p (a n)")
                dve.scalar_tensor_tensor(yg[:, et, :], u[:, et, :], ec[:, et, 2:3], py, ALU.mult, ALU.add).then_inc(s["yevac"], 1)
                dve.wait_ge(s["yevac"], et + 1)
                dve.wait_ge(s["sz_done"], NT)
                ygv = yg[:, et, :].rearrange("p (b l) -> p b l", b=B)
                dve.tensor_tensor(ygv, ygv, sz.rearrange("p (b h) l -> p h b l", h=2)[:, et], ALU.mult).then_inc(s["yg_done"], 1)

            dbu(0)
            for t in range(ST):
                if t == JT + NSUM_LAG:
                    y_out(0)
                if t + 1 < ST:
                    dbu(t + 1)
                dve.wait_ge(s["exp_done"], t + 1)
                dve.wait_ge(s["dbu_done"], t + 1)
                if t >= 2:
                    dve.wait_ge(s["hc_done"], t - 1)
                dve.tensor_tensor_scan(hb[t % 2], dA[t % 2], dBu[t % 2], 0.0, ALU.mult, ALU.add).then_inc(s["scan_done"], 1)
                if t == 2:
                    soft_1p(1)
                if t == 6:
                    soft_delta(1)
                if t in (10, 12):
                    soft_lo(1, (t - 10) // 2)
            dve.wait_ge(s["gate_done"], 1)

            def x1(b):
                if b < 2:
                    y_last(2 * b)
                    y_last(2 * b + 1)
                dve.wait_ge(s["yT_done"], B + b + 1)
                x_ = x[:, 2 * b:2 * b + 2, :].rearrange("p i c -> p (i c)")
                dve.scalar_tensor_tensor(x_, ps[:, b, :], tg[:, 0:1], x_, ALU.mult, ALU.add).then_inc(s["x1_done"], 1)

            def f_stat(b):
                z = slice(2 * b, 2 * b + 2)
                dve.wait_ge(s["x1_done"], b + 1)
                stats(range(2 * b, 2 * b + 2), "fst", 5 * b)

            def f_norm(b):
                z = slice(2 * b, 2 * b + 2)
                dve.wait_ge(s["fpow"], 2 * b + 1)
                link(dve.scalar_tensor_tensor(q8[:, 0, z], mv[:, z, 1], float(DM), rstd[:, z], ALU.mult, ALU.mult))
                dve.tensor_tensor(q8[:, 0, z], q8[:, 0, z], rstd[:, z], ALU.mult).then_inc(s["fnorm"], 1)
                for i in range(2):
                    dve.tensor_scalar(xl[:, i, :], x[:, 2 * b + i, :], mv[:, 2 * b + i, 0:1], rstd[:, 2 * b + i:2 * b + i + 1],
                                      ALU.subtract, ALU.mult).then_inc(s["fxl"], 1)

            def row_scales(norm, peak, z, width):
                link(dve.tensor_scalar(norm, norm, 1e-12, None, ALU.max))
                link(dve.reciprocal(norm, norm))
                link(dve.scalar_tensor_tensor(q8[:, 3, z], peak, float(width) ** 0.5, norm, ALU.mult, ALU.mult))
                link(dve.tensor_scalar(q8[:, 3, z], q8[:, 3, z], EPS, None, ALU.max))

            def row_steps(norm, z, width):
                link(dve.reciprocal(q8[:, 4, z], q8[:, 3, z]))
                link(dve.scalar_tensor_tensor(q8[:, 5, z], norm, 127.0 * float(width) ** 0.5, q8[:, 4, z], ALU.mult, ALU.mult))

            def f_quant(b):
                z = slice(2 * b, 2 * b + 2)
                if b == 0:
                    link(dve.tensor_scalar(k2[:, :], mw[:, 1:2], tg[:, 1:2], 1.0 / 127.0, ALU.mult, ALU.mult))
                dve.wait_ge(s["fxl"], 2 * b + 2)
                link(dve.tensor_reduce(q8[:, 2, z], xl, AX.X, ALU.max, apply_absolute_value=True))
                dve.wait_ge(s["fpow"], 2 * b + 2)
                row_scales(q8[:, 1, z], q8[:, 2, z], z, DM)
                row_steps(q8[:, 1, z], z, DM)
                dve.tensor_scalar(q8[:, 6, z], q8[:, 3, z], mw[:, 0:1], 1.0 / 127.0, ALU.mult, ALU.mult).then_inc(s["fscale"], 1)
                for i in range(2):
                    link(dve.tensor_scalar(xl[:, i, :], xl[:, i, :], q8[:, 5, 2 * b + i:2 * b + i + 1], MAGIC, ALU.mult, ALU.add))
                dve.tensor_scalar(xq.rearrange("p i c -> p (i c)"), xl.rearrange("p i c -> p (i c)"), MAGIC, None, ALU.subtract
                                  ).then_inc(s["fq"], 1)

            def w_low(n):
                if n == 0:
                    dve.wait_ge(s["ld_wk"], 16)
                    link(dve.tensor_copy(WkH, Wkr))
                    dve.tensor_tensor(WkL, Wkr, WkH.bitcast(F32), ALU.subtract).then_inc(s["wk_split"], 2)
                    link(dve.tensor_scalar(gkq[:, :], gqk[:, 0:1], gqk[:, 1:2], float(P) ** -0.5, ALU.mult, ALU.mult))
                else:
                    k, c = divmod(n - 1, 2)
                    dve.wait_ge(s["wqh"], n)
                    dve.tensor_tensor(WqL[:, k, 1024 * c:1024 * c + 1024], Wqr[:, 1024 * (n - 1):1024 * n],
                                      WqH[:, k, 1024 * c:1024 * c + 1024].bitcast(F32), ALU.subtract).then_inc(s["wql"], 1)

            def f_xqT(b):
                dve.wait_ge(s["fqT_done"], b + 1)
                dve.tensor_copy(xqT.rearrange("p k t -> p (k t)"), ps[:, 7, :].bitcast(BF16)[:, 0:512]).then_inc(s["fqT_evac"], 1)

            def f_peak(i):
                dve.wait_ge(s["fact"], 2 * i + 1)
                link(dve.tensor_reduce(q8[:, 2, i:i + 1], g2[i % 2], AX.X, ALU.max, apply_absolute_value=True))

            def f_scale(i):
                i_ = slice(i, i + 1)
                dve.wait_ge(s["fpow2"], i + 1)
                row_scales(q8[:, 8, i_], q8[:, 2, i_], i_, INNER)

            def f_scale2(i):
                i_ = slice(i, i + 1)
                row_steps(q8[:, 8, i_], i_, INNER)
                link(dve.tensor_tensor(q8[:, 9, i_], q8[:, 3, i_], k2[:, :], ALU.mult))

            def f_round(i):
                i_ = slice(i, i + 1)
                dve.wait_ge(s["fact"], 2 * i + 2)
                link(dve.tensor_scalar(g2[i % 2], g2[i % 2], q8[:, 5, i_], MAGIC, ALU.mult, ALU.add))
                dve.tensor_scalar(hq, g2[i % 2], MAGIC, None, ALU.subtract).then_inc(s["fhq"], 1)

            def f_hT(i):
                dve.wait_ge(s["fT_done"], i + 1)
                dve.tensor_copy(hT.rearrange("p k t -> p (k t)"), ps[:, 7, :].bitcast(BF16)).then_inc(s["fT_evac"], 1)

            def f_down(i):
                dve.wait_ge(s["mm2_done"], i + 1)
                dve.scalar_tensor_tensor(x[:, i, :], ps[:, 6, 0:DM], q8[:, 9, i:i + 1], x[:, i, :], ALU.mult, ALU.add
                                         ).then_inc(s["x2_done"], 1)

            def a_ln(b):
                dve.wait_ge(s["x2_done"], 2 * b + 2)
                stats(range(2 * b, 2 * b + 2), "aln", 5 * b)

            def a_xn(b):
                dve.wait_ge(s["apow"], b + 1)
                for i in range(2):
                    dve.tensor_scalar(xn[:, i, :], x[:, 2 * b + i, :], mv[:, 2 * b + i, 0:1], rstd[:, 2 * b + i:2 * b + i + 1],
                                      ALU.subtract, ALU.mult).then_inc(s["axn"], 1)

            def a_lnT(b):
                dve.wait_ge(s["axTH"], b + 1)
                dve.tensor_tensor(xT[:, b % 2, 1, :, :].rearrange("p k t -> p (k t)"), ps[:, 7, :],
                                  xT[:, b % 2, 0, :, :].rearrange("p k t -> p (k t)").bitcast(F32), ALU.subtract
                                  ).then_inc(s["axTL"], 1)

            def piece_stats(p):
                G_, kind = divmod(p, 4)
                if kind >= 2:
                    return
                j = 2 * G_ + kind
                dve.wait_ge(s["psq_done"], p + 1)
                if G_ >= 1:
                    dve.wait_ge(s["kpow"], j - 1)
                dve.tensor_reduce(rr[:, kind, :], psq[kind].rearrange("p (a c) -> p a c", a=GRP), AX.X, ALU.add
                                  ).then_inc(s["kst"], 1)
                dve.wait_ge(s["kst"], 2 * j + 1)
                dve.tensor_scalar(rr[:, kind, :], rr[:, kind, :], 1.0 / P, EPS, ALU.mult, ALU.add).then_inc(s["kst"], 1)

            def piece_evac(p):
                G_, kind = divmod(p, 4)
                j = 2 * G_ + kind % 2
                if kind < 2:
                    dve.wait_ge(s["pT_done"], j + 1)
                    if G_ >= RING:
                        dve.wait_ge(s["sc_done"], GRP * (G_ - RING + 1))
                    if p == 0:
                        dve.wait_ge(s["wql"], 4)
                        dve.wait_ge(s["G_done"], H // 2)
                    dve.tensor_scalar(kT[:, G_ % RING, :, kind * P:kind * P + P], ps[:, 7, :].rearrange("p (a t) -> p a t", a=GRP),
                                      gkq[:, 0:1], None, ALU.mult).then_inc(s["pT_evac"], 1)
                else:
                    dve.wait_ge(s["qsum_done"], j + 1)
                    if G_ >= 1:
                        dve.wait_ge(s["qpow"], j - 1)
                    dve.tensor_scalar(rr[:, kind, :], ps[:, 7, 0:4], 1.0 / P, EPS, ALU.mult, ALU.add).then_inc(s["qst"], 1)

            def head_max(n):
                dve.wait_ge(s["sc_done"], n + 1)
                if n >= 4:
                    dve.wait_ge(s["pnorm_done"], n - 3)
                dve.tensor_reduce(hs[:, n % 4, 0:2], ps[:, n % 2, :].rearrange("p (a k) -> p a k", a=2), AX.X, ALU.max
                                  ).then_inc(s["hmax"], 1)
                dve.wait_ge(s["hmax"], 2 * n + 1)
                if n % GRP == 0:
                    dve.wait_ge(s["qpow"], 2 * (n // GRP) + 2)
                dve.scalar_tensor_tensor(hs[:, n % 4, 2:4], hs[:, n % 4, 0:2], -1.0, rq[:, (n // GRP) % RING, n % GRP, :],
                                         ALU.mult, ALU.mult).then_inc(s["hmax"], 1)

            def head_recip(n):
                dve.wait_ge(s["exps"], 2 * n + 2)
                dve.reciprocal(hs[:, n % 4, 6:8], hs[:, n % 4, 4:6]).then_inc(s["hrec"], 1)

            def U_out(n):
                dve.wait_ge(s["U_done"], n + 1)
                if n >= 3:
                    dve.wait_ge(s["y_done"], n - 2)
                dve.tensor_copy(Us[n % 3], ps[:, 4, 0:S]).then_inc(s["U_evac"], 1)

            def x3(b):
                dve.wait_ge(s["y_done"], H * (b + 1))
                x_ = x[:, 2 * b:2 * b + 2, :].rearrange("p i c -> p (i c)")
                dve.scalar_tensor_tensor(x_, ps[:, 5, :], tg[:, 2:3], x_, ALU.mult, ALU.add).then_inc(s["x3_done"], 1)

            def y_ready(n):
                if n % H == H - 1:
                    x3(n // H)

            def m_ln(b):
                dve.wait_ge(s["x3_done"], b + 1)
                stats(range(2 * b, 2 * b + 2), "mln", 5 * b)

            def m_xn(b):
                dve.wait_ge(s["mpow"], b + 1)
                for i in range(2):
                    dve.tensor_scalar(xm[:, i, :], x[:, 2 * b + i, :], mv[:, 2 * b + i, 0:1], rstd[:, 2 * b + i:2 * b + i + 1],
                                      ALU.subtract, ALU.mult).then_inc(s["mxn"], 1)

            def m_T(b):
                dve.wait_ge(s["mxT_done"], b + 1)
                dve.tensor_copy(xmf[:, :, b * S:b * S + S], ps[:, 7, :].rearrange("p (k t) -> p k t", k=2)).then_inc(s["mxT_evac"], 1)

            def m_route(b):
                z = slice(2 * b, 2 * b + 2)
                dve.wait_ge(s["rl_done"], b + 1)
                for i in range(2 * b, 2 * b + 2):
                    dve.tensor_reduce(rt[:, i, 4, 0:1], ps[:, 7, i * E:i * E + E], AX.X, ALU.max, negate=True).then_inc(s["rneg"], 1)

            def m_pick(b):
                z = slice(2 * b, 2 * b + 2)
                dve.wait_ge(s["rexp"], 2 * b + 2)
                link(dve.reciprocal(rt[:, z, 4, 2:3], rt[:, z, 4, 1:2]))
                link(dve.tensor_tensor(rt[:, z, 0, :], rt[:, z, 0, :], rt[:, z, 4, 2:3].to_broadcast([P, 2, E]), ALU.mult))
                for i in range(2 * b, 2 * b + 2):
                    link(dve.max(rt[:, i, 1, :], rt[:, i, 0, :]))
                for i in range(2 * b, 2 * b + 2):
                    link(dve.max_index(rti[:, i, :], rt[:, i, 1, :], rt[:, i, 0, :]))

            def m_weight(b):
                z = slice(2 * b, 2 * b + 2)
                link(dve.tensor_copy(rt[:, z, 2, :], rti[:, z, :]))
                link(dve.tensor_tensor(rt[:, z, 4, 3:4], rt[:, z, 1, 0:1], rt[:, z, 1, 1:2], ALU.add))
                link(dve.tensor_scalar(rt[:, z, 4, 3:4], rt[:, z, 4, 3:4], 1e-20, None, ALU.add))
                link(dve.reciprocal(rt[:, z, 4, 4:5], rt[:, z, 4, 3:4]))
                link(dve.tensor_tensor(rt[:, z, 3, 0:2], rt[:, z, 1, 0:2], rt[:, z, 4, 4:5].to_broadcast([P, 2, 2]), ALU.mult))

            def m_spread(b):
                z = slice(2 * b, 2 * b + 2)
                for i in range(2 * b, 2 * b + 2):
                    link(dve.tensor_scalar(rt[:, i, 5, :], iota8[:, :], rt[:, i, 2, 0:1], rt[:, i, 3, 0:1], ALU.is_equal, ALU.mult))
                    link(dve.tensor_scalar(rt[:, i, 0, :], iota8[:, :], rt[:, i, 2, 1:2], rt[:, i, 3, 1:2], ALU.is_equal, ALU.mult))
                link(dve.tensor_tensor(rt[:, z, 5, :], rt[:, z, 5, :], rt[:, z, 0, :], ALU.add))
                link(dve.tensor_copy(cwR[:, :, :], rt[:, z, 5, :]))
                dve.wait_ge(s["cwz"], 1)
                if b >= 1:
                    dve.wait_ge(s["cwT_done"], b)
                link(dve.tensor_copy(cwHL[:, :, 0:E], cwR[:, :, :].bitcast(F32)))
                dve.tensor_tensor(cwHL[:, :, 32:32 + E], rt[:, z, 5, :], cwR[:, :, :].bitcast(F32), ALU.subtract
                                  ).then_inc(s["cw_ready"], 1)

            def m_cwT(b):
                dve.wait_ge(s["cwT_done"], b + 1)
                dve.tensor_copy(cwTf[:, b * S:b * S + S], ps[0:64, 7, 0:S]).then_inc(s["cwT_evac"], 1)
                if b == 1:
                    dve.wait_ge(s["cwT_evac"], 2)
                if b == B - 1:
                    dve.wait_ge(s["cwT_evac"], B)
                    dve.tensor_copy(cwT[:, 512:1024], cwTf[:, 512:1024]).then_inc(s["cwc"], 1)

            def x_split(c):
                for k in range(2):
                    dve.wait_ge(s["xmh"], 2 * c + k + 1)
                    dve.tensor_tensor(xmL[:, k, c * 512:c * 512 + 512], xmf[:, k, c * 512:c * 512 + 512],
                                      xmH[:, k, c * 512:c * 512 + 512].bitcast(F32), ALU.subtract).then_inc(s["xml"], 1)
                if c == 0:
                    dve.wait_ge(s["piece_done"], 16 * B)
                    dve.tensor_copy(cwT[:, 0:512], cwTf[:, 0:512]).then_inc(s["cwc"], 1)

            def w_split(ft):
                dve.wait_ge(s["wsplit"], ft + 1)
                dve.tensor_tensor(wL[ft % FIRST], wr[ft % 4], wH[ft % FIRST].bitcast(F32), ALU.subtract).then_inc(s["wsplitL"], 1)

            def gated(m):
                rows = min(P, FALL - ORDER[m][0] * P)
                dve.wait_ge(s["silu_done"], m + 1)
                dve.wait_ge(s["up_mm"], m + 1)
                if m >= 2:
                    dve.wait_ge(s["hL_done"], m - 1)
                    dve.wait_ge(s["hH_done"], m - 1)
                ins = dve.tensor_tensor(hm[m % 2][0:rows, :], ps[0:rows, 5, :], sg[m % 2][0:rows, :], ALU.mult)
                ins.then_inc(s["m1_done"], 1)

            def weighted(m):
                rows = min(P, FALL - ORDER[m][0] * P)
                hm_ = hm[m % 2][0:rows, :]
                if m < 2 * FTR:
                    dve.wait_ge(s["m1_done"], m + 1)
                    dve.wait_ge(s["cw_mm"], m + 1)
                    dve.tensor_tensor(hm_, ps[0:rows, 6, :], hm_, ALU.mult).then_inc(s["m2_done"], 1)

            mine = dict(x1=x1, piece=piece_stats, head_max=head_max, scores=head_recip, piece_T=piece_evac, values=U_out,
                        project_out=y_ready, f_stat=f_stat, f_norm=f_norm, w_low=w_low, f_quant=f_quant, f_xqT=f_xqT, f_peak=f_peak,
                        f_scale=f_scale, f_scale2=f_scale2, f_round=f_round, f_hT=f_hT, f_down=f_down, a_stat=a_ln, a_xn=a_xn, a_lnT=a_lnT,
                        m_stat=m_ln, m_xn=m_xn, m_T=m_T, m_route=m_route, m_pick=m_pick, m_weight=m_weight, m_spread=m_spread, m_cwT=m_cwT, x_split=x_split,
                        w_split=w_split, up=gated, cw=weighted)
            in_order("dve", mine)
            for b in range(B):
                dve.wait_ge(s["down_done"], 2 * FT - 1 + b // 2)
                for i in range(2):
                    dve.scalar_tensor_tensor(yo[b][:, i, :], ps[:, b, i * DM:i * DM + DM], tg[:, 3:4], x[:, 2 * b + i, :],
                                             ALU.mult, ALU.add).then_inc(s["out_done"], 1)

        @block.gpsimd
        def _(pool):
            pool.memset(ctxH[:, :, 0:PAD].bitcast(F32), 0.0).then_inc(s["pool_init"], 1)
            pool.memset(ctxL[:, :, 0:PAD].bitcast(F32), 0.0).then_inc(s["pool_init"], 1)
            pool.memset(phalf[:, :], 0.5).then_inc(s["pool_init"], 1)
            pool.memset(nhalf[:, :], -0.5).then_inc(s["pool_init"], 1)
            pool.memset(ones[:, :], 1.0).then_inc(s["pool_init"], 1)
            pool.wait_ge(s["pool_init"], 5)
            pool.wait_ge(s["zstat"], 2 * NT + 1)
            pool.tensor_tensor(rstd[:, :], ve[:, :], nhalf[:, 0:NT], ALU.pow).then_inc(s["zpow"], 1)
            pool.wait_ge(s["sel_ready"], 1)
            pool.wait_ge(s["ctx_split"], 2)
            for i in range(2):
                pool.memset(dA[i].rearrange("p (b l) -> p b l", b=B)[:, :, 0:1], 0.0).then_inc(s["pool_init"], 1)
            pool.wait_ge(s["bc_evac"], 2)
            pool.wait_ge(s["dlo_done"], 4)
            for t in range(ST):
                pool.wait_ge(s["scan_done"], t + 1)
                if t >= 3:
                    pool.wait_ge(s["nsum_done"], t - 2)
                if t < ST - 1:
                    pool.tensor_tensor(hC[t % 3], hb[t % 2], Cs, ALU.mult).then_inc(s["hc_done"], 1)
                else:
                    for hf in range(2):
                        c_ = slice(512 * hf, 512 * hf + 512)
                        pool.tensor_tensor(hC[t % 3][:, c_], hb[t % 2][:, c_], Cs[:, c_], ALU.mult).then_inc(s["hc_done"], 1)
            pool.wait_ge(s["sz_done"], NT)

            def f_stat(b):
                z = slice(2 * b, 2 * b + 2)
                pool.wait_ge(s["fst"], 5 * b + 5)
                pool.tensor_tensor(rstd[:, z], ve[:, z], nhalf[:, 0:2], ALU.pow).then_inc(s["fpow"], 1)

            def f_norm2(b):
                z = slice(2 * b, 2 * b + 2)
                pool.wait_ge(s["fnorm"], b + 1)
                pool.tensor_tensor(q8[:, 1, z], q8[:, 0, z], phalf[:, 0:2], ALU.pow).then_inc(s["fpow"], 1)

            def f_chain(i):
                pool.wait_ge(s["fact"], 2 * i + 2)
                pool.tensor_tensor(q8[:, 8, i:i + 1], q8[:, 7, i:i + 1], phalf[:, 0:1], ALU.pow).then_inc(s["fpow2"], 1)

            def a_ln(b):
                pool.wait_ge(s["aln"], 5 * b + 5)
                pool.tensor_tensor(rstd[:, 2 * b:2 * b + 2], ve[:, 2 * b:2 * b + 2], nhalf[:, 0:2], ALU.pow).then_inc(s["apow"], 1)

            def m_ln(b):
                if b == 0:
                    pool.memset(cwHL, 0.0).then_inc(s["cwz"], 1)
                pool.wait_ge(s["mln"], 5 * b + 5)
                pool.tensor_tensor(rstd[:, 2 * b:2 * b + 2], ve[:, 2 * b:2 * b + 2], nhalf[:, 0:2], ALU.pow).then_inc(s["mpow"], 1)

            def square(p):
                G_, kind = divmod(p, 4)
                j = 2 * G_ + kind % 2
                pool.wait_ge(s["raw_done"], p + 1)
                if kind < 2:
                    if G_ >= 1:
                        pool.wait_ge(s["kst"], 2 * (j - 2) + 1)
                    src = praw[kind]
                else:
                    if G_ >= 1:
                        pool.wait_ge(s["qsum_done"], j - 1)
                    a = 2 * (kind - 2)
                    src = qT[:, G_ % RING, a:a + 2, :].rearrange("p a t -> p (a t)")
                pool.tensor_tensor(psq[kind], src, src, ALU.mult).then_inc(s["psq_done"], 1)

            def key_norm(p):
                G_, kind = divmod(p, 4)
                if kind < 2:
                    j = 2 * G_ + kind
                    pool.wait_ge(s["kst"], 2 * j + 2)
                    pool.tensor_tensor(rv[:, kind, :], rr[:, kind, :], nhalf[:, 0:GRP], ALU.pow).then_inc(s["kpow"], 1)
                    pool.wait_ge(s["kpow"], j + 1)
                    pr = praw[kind].rearrange("p (a c) -> p a c", a=GRP)
                    pool.tensor_tensor(pr, pr, rv[:, kind, :].unsqueeze(2).to_broadcast([P, GRP, P]), ALU.mult
                                       ).then_inc(s["pnorm"], 1)

            def query_norm(p):
                G_, kind = divmod(p, 4)
                if kind >= 2:
                    j = 2 * G_ + kind - 2
                    pool.wait_ge(s["qst"], j + 1)
                    if G_ >= RING:
                        pool.wait_ge(s["exps"], 2 * GRP * (G_ - RING + 1))
                    a = 2 * (kind - 2)
                    pool.tensor_tensor(rq[:, G_ % RING, a:a + 2, :].rearrange("p a q -> p (a q)"), rr[:, kind, :], nhalf[:, 0:GRP],
                                       ALU.pow).then_inc(s["qpow"], 1)

            def normalise(n):
                pool.wait_ge(s["hrec"], n + 1)
                pool.tensor_tensor(Pb[n % 4], Pb[n % 4], hs[:, n % 4, 6:8].unsqueeze(2).to_broadcast([P, 2, S]), ALU.mult
                                   ).then_inc(s["pnorm_done"], 1)

            def w_split(ft):
                if ft == 0:
                    pool.wait_ge(s["piece_done"], 16 * B)
                    pool.dma_start(esel, d["esel"]).then_inc(s["ld_esel"], 16)

            def expert(m):
                rows = min(P, FALL - ORDER[m][0] * P)
                pool.wait_ge(s["hH_done"], m + 1)
                pool.tensor_tensor(hL[m % 3][0:rows, :], hm[m % 2][0:rows, :], hH[m % 3][0:rows, :].bitcast(F32), ALU.subtract
                                   ).then_inc(s["hL_done"], 1)

            mine = dict(piece=square, key_norm=key_norm, piece_T=query_norm, scores=normalise, f_stat=f_stat, f_norm=f_norm2, f_peak=f_chain,
                        a_stat=a_ln, m_stat=m_ln, w_split=w_split, cw=expert)
            in_order("pool", mine)


def kernel(**inputs):
    import concourse.bacc as bacc
    from concourse.bass_utils import run_bass_kernel_spmd

    a = {k: np.asarray(v) for k, v in inputs.items()}
    c = np.ascontiguousarray

    def rows(w, n):
        return w.reshape(n, P, -1).transpose(1, 0, 2)

    p, m = np.arange(P)[:, None], np.arange(P)[None, :]
    sel = np.stack([(p % 64 == 8 * j + m // NS) for j in range(8)], 1).astype(np.float32)
    win = np.arange(2 * P - CH)[None, :]
    nwin = (win == P - CH + p // NS).astype(np.float32)
    f = np.arange(FTR * P)[None, :]
    r = np.arange(64)[:, None]
    esel = ((r % 32 == f // F) & (r % 32 < E)).astype(np.float32)

    gate = np.concatenate([a["L1_ffn_w_gate"].reshape(E * F, DM), a["L1_ffn_sw_gate"]])
    up = np.concatenate([a["L1_ffn_w_up"].reshape(E * F, DM), a["L1_ffn_sw_up"]])
    dn = np.concatenate([a["L1_ffn_w_down"].transpose(0, 2, 1).reshape(E * F, DM), a["L1_ffn_sw_down"].T])
    moe = np.zeros((FT, P, 768), np.float32)
    for i in range(FT):
        n = min(P, FALL - i * P)
        s_ = slice(i * P, i * P + n)
        for k in range(2):
            moe[i, :, k * P:k * P + n] = gate[s_, k * P:k * P + P].T
            moe[i, :, 256 + k * P:256 + k * P + n] = up[s_, k * P:k * P + P].T
        moe[i, :n, 512:768] = dn[s_]
    xpw = a["L0_xattn_x_proj_w"]
    reps = [DR + np.arange(P) % NS, DR + NS + np.arange(P) % NS, np.arange(DR)]
    xpT = rows(np.concatenate([xpw[i] for i in reps]).T, 2)
    alog = a["L0_xattn_A_log"].reshape(ST, P).T
    arrays = {
        "x": a["x"], "ctx": a["ctx_1024"],
        "ctxT": c(a["ctx_1024"].reshape(T, DC).T),
        "inT": c(a["L0_xattn_in_proj_w"].T),
        "cw": c(a["L0_xattn_conv_w"].T.reshape(-1)),
        "ec": c(np.stack([a["L0_xattn_conv_b"], a["L0_xattn_dt_proj_b"], a["L0_xattn_D"]], 1).reshape(2, P, 3).transpose(1, 0, 2)),
        "gates": c(np.array([a["g_xattn"][0], a["g_ffn"][0], a["g_xattn"][1], a["g_ffn"][1]])),
        "xp": c(xpT), "dtw": c(a["L0_xattn_dt_proj_w"].T), "acol": c(alog),
        "gqk": c(np.stack([a["L1_xattn_gq"], a["L1_xattn_gk"]], 1)),
        "sel": sel, "nwin": nwin, "ident": np.eye(P, dtype=np.float32),
        "w1": c(rows(a["L0_ffn_w1"].T, 2).reshape(P, -1)), "w2": c(rows(a["L0_ffn_w2"].T, FT0).reshape(P, -1)),
        "Wq": c(rows(a["L1_xattn_Wq"], 2).reshape(P, -1)), "Wk": a["L1_xattn_Wk"],
        "WvT": c(a["L1_xattn_Wv"].reshape(DC, H, P).transpose(2, 1, 0).reshape(P, -1)),
        "Wo": c(rows(a["L1_xattn_Wo"], H).reshape(P, -1)),
        "gw": c(rows(a["L1_ffn_gate_weight"].T, 2)), "iota8": np.tile(np.arange(E, dtype=np.float32), (P, 1)),
        "moe": moe, "esel": esel,
    }
    nc = bacc.Bacc("TRN2", target_bir_lowering=False, num_devices=1)
    d = {n: nc.dram_tensor("in_" + n, v.shape, mybir.dt.from_np(v.dtype), kind="ExternalInput").ap() for n, v in arrays.items()}
    d["out"] = nc.dram_tensor("out", (B, S, DM), F32, kind="ExternalOutput").ap()
    build(nc, d)
    r_ = run_bass_kernel_spmd(nc, [{"in_" + n: v for n, v in arrays.items()}], core_ids=[0])
    return r_.results[0]["out"]
```

```python
from contextlib import ExitStack

import numpy as np

import concourse.bass as bass
from concourse import mybir

F32 = mybir.dt.float32
F32R = mybir.dt.float32r
BF16 = mybir.dt.bfloat16
U32 = mybir.dt.uint32
ALU = mybir.AluOpType
ACT = mybir.ActivationFunctionType
AX = mybir.AxisListType

P = 128
B, S, DM = 4, 256, 256
DC = 128
T = B * S
NT = T // P
DI, NS, TAPS, DR = 256, 16, 4, 8
PAD = 4
CH = P // NS
ST = DI // CH
JT = P // CH
INNER = 1024
FT0 = INNER // P
H = 16
E, F, FS = 8, 176, 352
FALL = E * F + FS
FT = -(-FALL // P)
FTR = E * F // P
EPS = 1e-5
MAGIC = 12582912.0
SOFT = [(0, slice(0, 512)), (0, slice(512, 1024)), (1, slice(0, 1024))]
SPLIT = [(0, 0), (1, 0), (0, 1), (1, 1), (2, 0), (2, 1)]
NSUM_LAG = 3
GRP = 4
RING = 3
FIRST = 3
ORDER = [(ft, c) for c in range(2) for ft in range(FIRST)] + [(ft, c) for ft in range(FIRST, FT) for c in range(2)]

AT = {
    "piece": -0.12, "piece_T": 2.18, "piece_pow": 0.835,
    "scores": 6.1, "head_max": 6.1, "probs_T": 8.21, "values": 9.81, "project_out": 10.31,
    "f_stat": 2.29, "f_norm": 2.79, "f_quant": 3.26, "f_xqT": 4.35, "f_up": 5.35, "f_square": 6.13,
    "f_peak": 7.14, "f_scale": 7.8, "f_scale2": 8.55, "f_round": 9.19,
    "f_hT": 9.53, "f_down": 10.2, "second": 2.94, "a_stat": 14.22, "a_xn": 15.22, "a_lnT": 16.53,
    "f_stat0": -13.15, "f_norm0": -12.9, "f_quant0": -12.4, "f_xqT0": -11.15, "f_up0": -10.53, "f_square0": -9.48,
    "f_peak0": -9.18, "f_scale0": -8.2, "f_scale20": -8.15,
    "f_round0": -7.45, "f_hT0": -6.65, "f_down0": -5.68, "second0": 1, "a_stat0": -3.03, "a_xn0": -2.72, "a_lnT0": -1.44,
    "G0": -9.4, "w_low0": -11.04, "keys0": -3,
    "m_stat": 10.53, "m_xn": 11.7, "m_T": 11.91, "m_route": 12.73, "m_pick": 13.31, "m_weight": 13.75, "m_spread": 14.49, "m_cwT": 15.97,
    "m_stat3": 0.215, "m_xn3": 0.47, "m_T3": 1.05, "m_route3": 1.9, "m_pick3": 2.3, "m_weight3": 2.37, "m_spread3": 2.62, "m_cwT3": 3.22,
    "x_split1": 1.5,
    "gate": 0, "up": 0.27, "cw": 0.45, "down": 1.58, "w_split": 1.63,
}
END = 16 * B + 10.2


def plan():
    def at(base, k, *names):
        return [(base + AT[name], name, k) for name in names]

    for k in range(16 * B):
        if k < 2:
            yield AT["keys0"] + k, "piece", k
        else:
            yield from at(k, k, "piece")
        yield from at(k, k, "piece_T", "piece_pow", "scores", "head_max", "probs_T", "values", "project_out")
    for b in range(B):
        t, x0 = (0, "0") if b == 0 else (16 * (b - 1), "")
        for name in ("f_stat", "f_norm", "f_quant", "f_xqT", "a_stat", "a_xn", "a_lnT"):
            yield t + AT[name + x0], name, b
        for a in range(2):
            for name in ("f_up", "f_square", "f_peak", "f_scale", "f_scale2", "f_round", "f_hT", "f_down"):
                yield t + AT[name + x0] + AT["second" + x0] * a, name, 2 * b + a
        t = 16 * b + 15
        if b < B - 1:
            yield from at(t, b, "m_stat", "m_xn", "m_T", "m_route", "m_pick", "m_weight", "m_spread", "m_cwT")
    for name in ("m_stat", "m_xn", "m_T", "m_route", "m_pick", "m_weight", "m_spread", "m_cwT"):
        yield END + AT[name + "3"], name, B - 1
    for g in range(4):
        yield AT["G0"] + g, "G", g
    for b in range(B):
        yield AT["f_stat0"] + (-.1, .1, .8, .9)[b], "x1", b
    for n in range(5):
        yield AT["w_low0"] + .8 * n, "w_low", n
    yield END - 2, "w_split", 0
    yield END - 1.8, "w_split", 1
    yield END + .6, "w_split", 2
    yield END - 1.5, "x_split", 0
    yield END + AT["x_split1"], "x_split", 1
    for m, (ft, c) in enumerate(ORDER):
        yield from at(END + m, m, "gate", "up", "cw", "down")
        if c == 1 and ft + FIRST < FT:
            yield from at(END + m, ft + FIRST, "w_split")


AFTER = {
    "act": {"piece": 0.13, "scores": 0.4, "probs_T": 0.5, "f_up": 0.22, "f_stat": -0.28, "G": 0.69, "a_lnT": 0.35, "m_route": -0.17,
            "x_split": 0.06, "w_split": 0.25, "gate": 0.55, "cw": 0.4},
    "dve": {"piece": 0.65, "head_max": 0.2, "scores": 0.715, "piece_T": 0.13, "values": 0.39, "project_out": 0.08, "f_xqT": 0.1,
            "f_hT": 0.16, "f_down": 0.32, "a_lnT": 0, "m_T": 0.23, "m_route": 0.38, "m_cwT": -0.15, "x_split": 0.6, "w_split": 0.03,
            "up": 0.315, "cw": 0.16},
    "pool": {"f_norm": 0.02, "piece": 0.19, "scores": 1.24, "cw": 0.5, "f_peak": 0.12, "f_stat": -0.05, "a_stat": 0.14, "m_stat": 0.58},
}


def in_order(engine, mine):
    after = AFTER.get(engine, {})
    for _, name, k in sorted(((t + after.get(name, 0), name, k) for t, name, k in plan() if name in mine), key=lambda e: e[0]):
        mine[name](k)


def build(nc, d):
    with ExitStack() as ctx:
        def sb(name, shape, dt=F32):
            return ctx.enter_context(nc.sbuf_tensor(name, shape, dt))

        def sem(name):
            return ctx.enter_context(nc.semaphore(name))

        ps = ctx.enter_context(nc.psum_tensor("ps", [P, 8, 512], F32))

        x = sb("x", [P, NT, DM])
        ctxn = sb("ctxn", [P, NT, DC])
        ctxH = sb("ctxH", [P, B, PAD + S], F32R)
        ctxL = sb("ctxL", [P, B, PAD + S], F32R)
        inT = sb("inT", [P, DI])
        cstage = sb("cstage", [P, 2048])
        u = sb("u", [P, 2, T])
        xp = sb("xp", [P, 2, 2 * P + DR])
        bcz = sb("bcz", [P, 4096])
        rA = sb("rA", [P, 8192], F32R)
        rK = sb("rK", [P, 4096], F32R)
        sel = sb("sel", [P, 8, P], F32R)
        nwin = sb("nwin", [P, 2 * P - CH])
        work = sb("work", [P, 9216])
        stage = sb("stage", [P, 6144])
        w12q = sb("w12q", [P, 2, 2048], BF16)
        G = sb("G", [P, H, DM])
        xT = sb("xT", [P, 2, 2, 2, S], F32R)
        ident = sb("ident", [P, P])
        identb = sb("identb", [P, P], BF16)
        ones = sb("ones", [P, P])
        acol = sb("acol", [P, ST])
        nacol = sb("nacol", [P, ST])
        dtw = sb("dtw", [DR, DI])
        ec = sb("ec", [P, 2, 3])
        gates = sb("gates", [P, 4])
        tg = sb("tg", [P, 4])
        gqk = sb("gqk", [P, 2])
        gkq = sb("gkq", [P, 1])
        st6 = sb("st6", [P, NT, 6])
        mv = sb("mv", [P, NT, 2])
        ve = sb("ve", [P, NT])
        rstd = sb("rstd", [P, NT])
        nb8 = sb("nb8", [P, NT])
        nmagic = sb("nmagic", [P, 1])
        phalf = sb("phalf", [P, 32])
        nhalf = sb("nhalf", [P, 32])
        q8 = sb("q8", [P, 10, NT])
        wsum = sb("wsum", [P, 2])
        mw = sb("mw", [P, 2])
        iw = sb("iw", [P, 2])
        k2 = sb("k2", [P, 1])
        rr = sb("rr", [P, 4, GRP])
        rv = sb("rv", [P, 4, GRP])
        rq = sb("rq", [P, RING, GRP, 2])
        hs = sb("hs", [P, 4, 8])
        gw = sb("gw", [P, 2, E])
        iota8 = sb("iota8", [P, E])
        cwR = sb("cwR", [P, 2, E], F32R)
        rti = sb("rti", [P, NT, E], U32)

        cwb = cstage[:, 0:TAPS * DI].rearrange("p (j e) -> p j e", j=TAPS)
        wc = cstage[:, 1024:2048].rearrange("p (j e) -> p j e", j=TAPS)
        wcH = rK[:, 0:1024].rearrange("p (j e) -> p j e", j=TAPS)
        wcL = rK[:, 2048:3072].rearrange("p (j e) -> p j e", j=TAPS)
        Bs, Cs = bcz[:, 0:T], bcz[:, T:2 * T]
        sz = bcz[:, 2 * T:4 * T].rearrange("p (i l) -> p i l", i=NT)
        XD = rA[:, 0:4096].rearrange("p (s t) -> p s t", s=4)
        XU = rA[:, 4096:8192].rearrange("p (s t) -> p s t", s=4)
        ctxTr = work[:, 0:T]
        selr = work[:, T:2 * T].rearrange("p (j m) -> p j m", j=8)
        dab = [work[:, 2048:3072], cstage[:, 0:1024]]
        dex = [work[:, 3072:4096], cstage[:, 1024:2048]]
        dlt = [work[:, 4096:5120], stage[:, 4096:5120]]
        dre = [work[:, 5120:6144], stage[:, 5120:6144]]
        dtl = work[0:DR, 8192:9216]
        dA = [work[:, i * T:(i + 1) * T] for i in (0, 1)]
        dBu = [work[:, i * T:(i + 1) * T] for i in (2, 3)]
        hb = [work[:, i * T:(i + 1) * T] for i in (4, 5)]
        hC = [work[:, i * T:(i + 1) * T] for i in (6, 7, 8)]
        wraw = [stage[:, 0:2048], stage[:, 2048:4096]]
        yg = stage[:, 4096:6144].rearrange("p (t n) -> p t n", t=2)
        uf = u[:, :, :].rearrange("p a n -> p (a n)")
        g1 = bcz[:, 0:1024]
        g2 = [bcz[:, 1024:2048], bcz[:, 2048:3072]]
        hq = bcz[:, 3072:3584].bitcast(BF16)
        hT = bcz[:, 3584:4096].bitcast(BF16).rearrange("p (k t) -> p k t", k=FT0)
        xl = uf[:, 0:512].rearrange("p (i c) -> p i c", i=2)
        xq = uf[:, 512:768].bitcast(BF16).rearrange("p (i c) -> p i c", i=2)
        xqT = uf[:, 768:1024].bitcast(BF16).rearrange("p (k t) -> p k t", k=2)
        w1q = w12q[:, 0, :].rearrange("p (k f) -> p k f", k=2)
        w2q = w12q[:, 1, :].rearrange("p (k o) -> p k o", k=FT0)
        Wqr = stage[:, 0:4096]
        Wkr = cstage[:, 0:2048]
        WqH = rA[:, 0:4096].rearrange("p (k n) -> p k n", k=2)
        WqL = rA[:, 4096:8192].rearrange("p (k n) -> p k n", k=2)
        WkH, WkL = rK[:, 0:2048], rK[:, 2048:4096]
        WvT = stage[:, 4096:6144].rearrange("p (h c) -> p h c", c=DC)
        kT = stage[:, 0:3072].rearrange("p (g h t) -> p g h t", g=RING, h=GRP)
        qT = stage[:, 3072:6144].rearrange("p (g h t) -> p g h t", g=RING, h=GRP)
        praw = [work[:, 512 * i:512 * i + 512] for i in range(4)]
        psq = [work[:, 2048 + 512 * i:2560 + 512 * i] for i in range(2)]
        Pb = [work[:, 3072 + 512 * i:3584 + 512 * i].rearrange("p (q k) -> p q k", q=2) for i in range(4)]
        PT = [work[:, 5120 + 512 * i:5632 + 512 * i].rearrange("p (k q) -> p k q", k=2) for i in range(3)]
        Us = [work[:, 6656 + 256 * i:6912 + 256 * i] for i in range(3)]
        xn = work[:, 7424:7936].rearrange("p (i c) -> p i c", i=2)
        xmH = rA[:, 0:2048].rearrange("p (k t) -> p k t", k=2)
        xmL = rA[:, 2048:4096].rearrange("p (k t) -> p k t", k=2)
        wr = [bcz[:, 768 * i:768 * i + 768] for i in range(4)]
        wH = [rA[:, 4096:4864], rA[:, 5632:6400], rA[:, 7168:7936]]
        wL = [rA[:, 4864:5632], rA[:, 6400:7168], sel[:, :, :].rearrange("p j m -> p (j m)")[:, 0:768]]
        hH = [rK[:, 1024 * i:1024 * i + 512] for i in range(3)]
        hL = [rK[:, 1024 * i + 512:1024 * i + 1024] for i in range(3)]
        sg = [work[:, 512 * i:512 * i + 512] for i in range(2)]
        hm = [work[:, 1024 + 512 * i:1536 + 512 * i] for i in range(2)]
        yo = [work[:, 2048 + 512 * i:2560 + 512 * i].rearrange("p (i c) -> p i c", i=2) for i in range(4)]
        xm = work[:, 7936:8448].rearrange("p (i c) -> p i c", i=2)
        cwHL = work[:, 8448:8576].rearrange("p (i m) -> p i m", i=2)
        rt = work[:, 8576:8960].rearrange("p (i a e) -> p i a e", i=NT, a=6)
        xmf = cstage[:, :].rearrange("p (k t) -> p k t", k=2)
        cwTf = uf[0:64, 1024:2048]
        esel = xT[0:64].rearrange("p a b k t -> p (a b k t)")[:, 0:FTR * P]
        cwT = rK[0:64, 3072:4096]

        s = {}
        for name in ("ld_ctxT ld_wc ld_x ld_sel ld_xp ld_small ld_w ld_ctxn ld_wq ld_wk ld_wo ld_wv ld_moe0 ld_moe1 ld_moe2 "
                     "ld_moe3 ld_esel ld_out dve_chain "
                     "pool_init ctx_split conv_w sel_ready conv_done u_done zstat zpow znb sz_done xproj_done "
                     "dtl_evac bc_evac dpre_done dabs drelu dexp done_1p dln ddelta dhi_done dlo_done "
                     "wabs wsum_done iw_done round0 round1 wq_done nacol_done gate_done "
                     "dbc_done ubc_done exp_done dbu_done scan_done hc_done nsum_done yevac yg_done yT_done x1_done "
                     "fst fpow fnorm fxl fscale fq fqT_done fqT_evac mm1_done g1_done fact fpow2 fhq fT_done fT_evac mm2_done "
                     "x2_done prs prv_done G_done G_evac wk_split wqh wql "
                     "aln apow axn axT_done axTH axTL piece_done raw_done psq_done pnorm pT_done pT_evac "
                     "sc_done hmax exps hrec pnorm_done PT_done PT_evac U_done U_evac y_done x3_done "
                     "mln mpow mxn mxT_done mxT_evac cwz rl_done rneg rexp cw_ready cwT_done cwT_evac cwc xmh xml wsplit wsplitL "
                     "gate_mm up_mm cw_mm silu_done m1_done m2_done hH_done hL_done down_done out_done").split():
            s[name] = sem(name)
        block = ctx.enter_context(nc.Block())

        @block.sync
        def _(sp):
            sp.dma_start(inT[:, :], d["inT"]).then_inc(s["ld_wc"], 16)
            sp.dma_start(cstage[:, 0:1024], d["cw"].partition_broadcast(P)).then_inc(s["ld_wc"], 16)
            sp.dma_start(ctxTr, d["ctxT"]).then_inc(s["ld_ctxT"], 16)
            sp.dma_start(ec[:, :, :], d["ec"]).then_inc(s["ld_small"], 16)
            sp.dma_start(gates[:, :], d["gates"].partition_broadcast(P)).then_inc(s["ld_small"], 16)
            sp.dma_start(x[:, :, :], d["x"].rearrange("b (h p) c -> p (b h) c", p=P)).then_inc(s["ld_x"], 16)
            sp.dma_start(xp[:, :, :], d["xp"]).then_inc(s["ld_xp"], 16)
            sp.dma_start(dtw[:, :], d["dtw"]).then_inc(s["ld_small"], 16)
            sp.dma_start(acol[:, :], d["acol"]).then_inc(s["ld_small"], 16)
            sp.dma_start(gqk[:, :], d["gqk"]).then_inc(s["ld_small"], 16)
            sp.dma_start(selr, d["sel"]).then_inc(s["ld_sel"], 16)
            sp.dma_start(nwin[:, :], d["nwin"]).then_inc(s["ld_sel"], 16)
            sp.dma_start(ident[:, :], d["ident"]).then_inc(s["ld_sel"], 16)
            sp.dma_start(wraw[0], d["w1"]).then_inc(s["ld_w"], 16)
            sp.dma_start(wraw[1], d["w2"]).then_inc(s["ld_w"], 16)
            sp.dma_start(ctxn[:, :, :], d["ctx"].rearrange("b (h p) c -> p (b h) c", p=P)).then_inc(s["ld_ctxn"], 16)
            sp.dma_start(gw[:, :, :], d["gw"]).then_inc(s["ld_ctxn"], 16)
            sp.dma_start(iota8[:, :], d["iota8"]).then_inc(s["ld_ctxn"], 16)
            sp.dma_start(G[:, :, :].rearrange("p h o -> p (h o)"), d["Wo"]).then_inc(s["ld_wo"], 16)
            sp.wait_ge(s["wq_done"], 6)
            sp.dma_start(Wqr, d["Wq"]).then_inc(s["ld_wq"], 16)
            sp.wait_ge(s["dlo_done"], 12)
            sp.dma_start(Wkr, d["Wk"]).then_inc(s["ld_wk"], 16)
            sp.wait_ge(s["yT_done"], 2 * B)
            sp.dma_start(stage[:, 4096:6144], d["WvT"]).then_inc(s["ld_wv"], 16)
            sp.wait_ge(s["x2_done"], NT)
            for i in range(FT):
                if i >= 4:
                    sp.wait_ge(s["wsplitL"], i - 3)
                sp.dma_start(wr[i % 4], d["moe"][i]).then_inc(s[f"ld_moe{i % 4}"], 16)
            for b in range(B):
                sp.wait_ge(s["out_done"], 2 * b + 2)
                sp.dma_start(d["out"][b].rearrange("(h p) c -> p h c", p=P), yo[b]).then_inc(s["ld_out"], 16)
            sp.wait_ge(s["ld_out"], 16 * B)

        def clip_round(engine, w, done):
            engine.tensor_scalar(wraw[w], wraw[w], iw[:, w:w + 1], 1.0, ALU.mult, ALU.min).then_inc(s[done], 1)
            engine.wait_ge(s[done], 1)
            engine.tensor_scalar(wraw[w], wraw[w], -1.0, MAGIC, ALU.max, ALU.add).then_inc(s[done], 1)

        def three(pe, out, pairs):
            terms = [(a, r) for aH, aL, rH, rL in pairs for a, r in ((aH, rH), (aH, rL), (aL, rH))]
            for n, (a, r) in enumerate(terms):
                last = pe.matmul(out, a, r, start=(n == 0), stop=(n == len(terms) - 1))
            return last

        @block.tensor
        def _(pe):
            pe.wait_ge(s["ctx_split"], 1)
            pe.wait_ge(s["pool_init"], 6)
            pe.wait_ge(s["conv_w"], 2)
            for et in range(2):
                for hf in range(2):
                    w_ = slice(et * P, et * P + P)
                    for z, (aw, r) in enumerate(((wcH, ctxH), (wcH, ctxL), (wcL, ctxH))):
                        if z == 1:
                            pe.wait_ge(s["ctx_split"], 2)
                        if z == 2:
                            pe.wait_ge(s["conv_w"], 3)
                        for j in range(TAPS):
                            c0 = PAD - (TAPS - 1) + j
                            last = pe.matmul(ps[:, 2 * et + hf, :], aw[:, j, w_], r[:, 2 * hf:2 * hf + 2, c0:c0 + S],
                                             start=(z == 0 and j == 0), stop=(z == 2 and j == TAPS - 1))
                    last.then_inc(s["conv_done"], 1)
            pe.wait_ge(s["ld_xp"], 16)
            pe.wait_ge(s["u_done"], 4)

            def xproj(c0, m, bank):
                for hf in range(2):
                    for k in range(2):
                        last = pe.matmul(ps[0:m, bank + hf, :], xp[:, k, c0:c0 + m], u[:, k, 512 * hf:512 * hf + 512],
                                         start=(k == 0), stop=(k == 1))
                last.then_inc(s["xproj_done"], 1)

            xproj(2 * P, DR, 0)
            pe.wait_ge(s["wabs"], 2)
            pe.matmul(ps[:, 7, 0:2], ones[:, :], wsum[:, :], start=True, stop=True).then_inc(s["wsum_done"], 1)
            pe.wait_ge(s["ld_small"], 80)
            pe.wait_ge(s["dtl_evac"], 1)
            for et in range(2):
                if et == 1:
                    pe.wait_ge(s["wq_done"], 1)
                    xproj(0, P, 6)
                for hf in range(2):
                    last = pe.matmul(ps[:, 2 + 2 * et + hf, :], dtw[:, et * P:et * P + P], dtl[:, 512 * hf:512 * hf + 512],
                                     start=True, stop=True)
                    if et == 0 or hf == 1:
                        last.then_inc(s["dpre_done"], 1)
            pe.wait_ge(s["bc_evac"], 1)
            xproj(P, P, 6)
            def nsum(t):
                et, jj = divmod(t, JT)
                pe.wait_ge(s["hc_done"], t + 1)
                if t == JT:
                    pe.wait_ge(s["yevac"], 1)
                for hf in range(2):
                    if t == ST - 1:
                        pe.wait_ge(s["hc_done"], t + 1 + hf)
                    last = pe.matmul(ps[:, 6 + hf, :], nwin[:, P - CH - CH * jj:2 * P - CH - CH * jj],
                                     hC[t % 3][:, 512 * hf:512 * hf + 512], start=(jj == 0), stop=(jj == JT - 1))
                    if t == ST - 1 or hf == 1:
                        last.then_inc(s["nsum_done"], 1)

            pe.wait_ge(s["sel_ready"], 1)
            for t in range(ST):
                g, j = divmod(t, 8)
                if j == 0:
                    pe.wait_ge(s["dlo_done"], (4, 8, 10, 12)[g])
                if t >= 1:
                    pe.wait_ge(s["exp_done"], t)
                for hf in range(2):
                    last = pe.matmul(ps[:, hf, :], sel[:, j, :], XD[:, g, 512 * hf:512 * hf + 512], start=True, stop=True)
                last.then_inc(s["dbc_done"], 1)
                if t < 2:
                    pe.wait_ge(s["drelu"], t + 2)
                if t >= 2:
                    pe.wait_ge(s["dbu_done"], t - 1)
                for hf in range(2):
                    last = pe.matmul(ps[:, 2 + 2 * (t % 2) + hf, :], sel[:, j, :], XU[:, g, 512 * hf:512 * hf + 512],
                                     start=True, stop=True)
                last.then_inc(s["ubc_done"], 1)
                if t >= NSUM_LAG:
                    nsum(t - NSUM_LAG)
            for t in range(ST - NSUM_LAG, ST):
                nsum(t)
            pe.wait_ge(s["exp_done"], ST)
            pe.wait_ge(s["dbu_done"], ST)
            pe.wait_ge(s["yg_done"], 1)
            for et in range(2):
                for b in range(B):
                    if et == 1:
                        pe.wait_ge(s["yg_done"], b + 2)
                    for lh in range(2):
                        last = pe.transpose(ps[:, b, lh * DM + et * P:lh * DM + et * P + P],
                                            yg[:, et, b * S + lh * P:b * S + lh * P + P], ident[:, :])
                    last.then_inc(s["yT_done"], 1)
            free = {6: ("yevac", 3), 7: ("yevac", 5)}

            def take(bank, sem_, value):
                pe.wait_ge(s[free[bank][0]], free[bank][1])
                free[bank] = (sem_, value)

            def f_xqT(b):
                pe.wait_ge(s["fq"], b + 1)
                take(7, "fqT_evac", b + 1)
                for k in range(2):
                    for i in range(2):
                        last = pe.transpose(ps[:, 7, :].bitcast(BF16)[:, k * S + i * P:k * S + i * P + P],
                                            xq[:, i, k * P:k * P + P], identb[:, :])
                last.then_inc(s["fqT_done"], 1)

            def f_up(i):
                pe.wait_ge(s["fqT_evac"], i // 2 + 1)
                pe.wait_ge(s["wq_done"], 6)
                for n in range(2):
                    take(6 + n, "g1_done", 2 * i + n + 1)
                    for k in range(2):
                        last = pe.matmul(ps[:, 6 + n, :], xqT[:, k, (i % 2) * P:(i % 2) * P + P],
                                         w1q[:, k, 512 * n:512 * n + 512], start=(k == 0), stop=(k == 1))
                    last.then_inc(s["mm1_done"], 1)

            def f_hT(i):
                pe.wait_ge(s["fhq"], i + 1)
                take(7, "fT_evac", i + 1)
                for k in range(FT0):
                    last = pe.transpose(ps[:, 7, :].bitcast(BF16)[:, k * P:k * P + P], hq[:, k * P:k * P + P], identb[:, :])
                last.then_inc(s["fT_done"], 1)

            def f_down(i):
                pe.wait_ge(s["fT_evac"], i + 1)
                take(6, "x2_done", i + 1)
                for k in range(FT0):
                    last = pe.matmul(ps[:, 6, 0:DM], hT[:, k, :], w2q[:, k, :], start=(k == 0), stop=(k == FT0 - 1))
                last.then_inc(s["mm2_done"], 1)

            def value_out(g):
                if g == 0:
                    pe.wait_ge(s["ld_wo"], 16)
                    pe.wait_ge(s["ld_wv"], 16)
                    pe.wait_ge(s["x1_done"], B)
                for n in (2 * g, 2 * g + 1):
                    if n >= 2:
                        pe.wait_ge(s["G_evac"], n - 1)
                    for a in range(2):
                        last = pe.matmul(ps[:, 4 + n % 2, a * DM:(a + 1) * DM], WvT[:, 2 * n + a, :], G[:, 2 * n + a, :],
                                         start=True, stop=True)
                    last.then_inc(s["G_done"], 1)

            def a_lnT(b):
                pe.wait_ge(s["axn"], 2 * b + 2)
                take(7, "axTL", b + 1)
                for k in range(2):
                    for i in range(2):
                        last = pe.transpose(ps[:, 7, k * S + i * P:k * S + i * P + P], xn[:, i, k * P:k * P + P], ident[:, :])
                last.then_inc(s["axT_done"], 1)

            def piece(p):
                b, r = divmod(p, 16)
                g, kind = divmod(r, 4)
                tt = kind % 2
                take(6, "raw_done", p + 1)
                n_ = slice(g * 512, g * 512 + 512)
                if kind < 2:
                    if p == 0:
                        pe.wait_ge(s["wk_split"], 2)
                    a_ = slice(PAD + tt * P, PAD + tt * P + P)
                    pairs = [(ctxH[:, b, a_], ctxL[:, b, a_], WkH[:, n_], WkL[:, n_])]
                else:
                    pe.wait_ge(s["axTH"], b + 1)
                    pe.wait_ge(s["axTL"], b + 1)
                    pe.wait_ge(s["wqh"], 4)
                    pe.wait_ge(s["wql"], 4)
                    a_ = slice(tt * P, tt * P + P)
                    pairs = [(xT[:, b % 2, 0, k, a_], xT[:, b % 2, 1, k, a_], WqH[:, k, n_], WqL[:, k, n_]) for k in range(2)]
                three(pe, ps[:, 6, :], pairs).then_inc(s["piece_done"], 1)

            def piece_T(p):
                if p % 4 < 2:
                    pe.wait_ge(s["pnorm"], 2 * (p // 4) + p % 4 + 1)
                else:
                    pe.wait_ge(s["raw_done"], p + 1)
                take(7, "pT_evac", p + 1)
                for a in range(GRP):
                    last = pe.transpose(ps[:, 7, a * P:a * P + P], praw[p % 4][:, a * P:a * P + P], ident[:, :])
                last.then_inc(s["pT_done"], 1)

            def scores(n):
                G_, a = divmod(n, GRP)
                if a == 0:
                    pe.wait_ge(s["pT_evac"], 4 * G_ + 4)
                if n >= 2:
                    pe.wait_ge(s["exps"], 2 * (n - 1))
                for qt in range(2):
                    last = pe.matmul(ps[:, n % 2, qt * S:qt * S + S], qT[:, G_ % RING, a, qt * P:qt * P + P],
                                     kT[:, G_ % RING, a, :], start=True, stop=True)
                last.then_inc(s["sc_done"], 1)

            def probs_T(n):
                pe.wait_ge(s["pnorm_done"], n + 1)
                if n >= 2:
                    pe.wait_ge(s["PT_evac"], n - 1)
                for kt in range(2):
                    for qt in range(2):
                        last = pe.transpose(ps[:, 2 + n % 2, kt * S + qt * P:kt * S + qt * P + P],
                                            Pb[n % 4][:, qt, kt * P:kt * P + P], ident[:, :])
                last.then_inc(s["PT_done"], 1)

            def values(n):
                b = n // H
                if n == 0:
                    pe.wait_ge(s["G_evac"], H // 2)
                    pe.wait_ge(s["ld_ctxn"], 48)
                pe.wait_ge(s["PT_evac"], n + 1)
                if n >= 1:
                    pe.wait_ge(s["U_evac"], n)
                for kt in range(2):
                    last = pe.matmul(ps[:, 4, 0:S], ctxn[:, 2 * b + kt, :], PT[n % 3][:, kt, :], start=(kt == 0), stop=(kt == 1))
                last.then_inc(s["U_done"], 1)

            def project_out(n):
                b, h = divmod(n, H)
                pe.wait_ge(s["U_evac"], n + 1)
                if h == 0 and b >= 1:
                    pe.wait_ge(s["x3_done"], b)
                for qt in range(2):
                    last = pe.matmul(ps[:, 5, qt * DM:qt * DM + DM], Us[n % 3][:, qt * P:qt * P + P], G[:, h, :],
                                     start=(h == 0 and qt == 0), stop=(h == H - 1), skip_group_check=True)
                last.then_inc(s["y_done"], 1)

            def m_T(b):
                pe.wait_ge(s["mxn"], 2 * b + 2)
                take(7, "mxT_evac", b + 1)
                for k in range(2):
                    for i in range(2):
                        last = pe.transpose(ps[:, 7, k * S + i * P:k * S + i * P + P], xm[:, i, k * P:k * P + P], ident[:, :])
                last.then_inc(s["mxT_done"], 1)

            def m_route(b):
                pe.wait_ge(s["mxT_evac"], b + 1)
                take(7, "rexp", 2 * b + 2)
                for i in range(2 * b, 2 * b + 2):
                    for k in range(2):
                        last = pe.matmul(ps[:, 7, i * E:i * E + E], xmf[:, k, i * P:i * P + P], gw[:, k, :],
                                         start=(k == 0), stop=(k == 1))
                last.then_inc(s["rl_done"], 1)

            def m_cwT(b):
                pe.wait_ge(s["cw_ready"], b + 1)
                take(7, "cwT_evac", b + 1)
                for i in range(2):
                    last = pe.transpose(ps[0:64, 7, i * P:i * P + P], cwHL[:, i, :], ident[:, :])
                last.then_inc(s["cwT_done"], 1)

            def product(m, which, bank):
                ft, c = ORDER[m]
                rows = min(P, FALL - ft * P)
                t_ = slice(c * 512, c * 512 + 512)
                return three(pe, ps[0:rows, bank, :],
                             [(wH[ft % FIRST][:, 256 * which + k * P:256 * which + k * P + rows],
                               wL[ft % FIRST][:, 256 * which + k * P:256 * which + k * P + rows],
                               xmH[:, k, t_], xmL[:, k, t_]) for k in range(2)])

            def gate(m):
                ft, c = ORDER[m]
                if m == 0:
                    pe.wait_ge(s["U_evac"], 16 * B)
                    pe.wait_ge(s["x3_done"], B)
                    pe.wait_ge(s["raw_done"], 16 * B)
                    pe.wait_ge(s["ld_esel"], 16)
                pe.wait_ge(s["xmh"], 2 * c + 2)
                pe.wait_ge(s["xml"], 2 * c + 2)
                pe.wait_ge(s["wsplit"], ft + 1)
                pe.wait_ge(s["wsplitL"], ft + 1)
                if m >= 1:
                    pe.wait_ge(s["silu_done"], m)
                product(m, 0, 4).then_inc(s["gate_mm"], 1)

            def up(m):
                if m >= 1:
                    pe.wait_ge(s["m1_done"], m)
                product(m, 1, 5).then_inc(s["up_mm"], 1)

            def cw(m):
                ft, c = ORDER[m]
                t_ = slice(c * 512, c * 512 + 512)
                if ft < FTR:
                    pe.wait_ge(s["cwc"], c + 1)
                    if m >= 1:
                        pe.wait_ge(s["m2_done"], m)
                    pe.matmul(ps[:, 6, :], esel[:, ft * P:ft * P + P], cwT[:, t_], start=True, stop=True).then_inc(s["cw_mm"], 1)

            def down(m):
                ft, c = ORDER[m]
                rows = min(P, FALL - ft * P)
                pe.wait_ge(s["hL_done"], m + 1)
                if m == 0:
                    pe.wait_ge(s["exps"], 2 * 16 * B)
                    pe.wait_ge(s["PT_evac"], 16 * B)
                for tt in range(4):
                    i = 4 * c + tt
                    a_ = slice(tt * P, tt * P + P)
                    terms = ((hH[m % 3], wH[ft % FIRST]), (hH[m % 3], wL[ft % FIRST]), (hL[m % 3], wH[ft % FIRST]))
                    for z, (a, w) in enumerate(terms):
                        last = pe.matmul(ps[:, i // 2, (i % 2) * DM:(i % 2) * DM + DM], a[0:rows, a_], w[0:rows, 512:768],
                                         start=(ft == 0 and z == 0 and i % 2 == 0), stop=(ft == FT - 1 and z == 2),
                                         skip_group_check=True)
                last.then_inc(s["down_done"], 1)

            mine = dict(piece=piece, scores=scores, piece_T=piece_T, probs_T=probs_T, project_out=project_out, values=values,
                        f_xqT=f_xqT, f_up=f_up, f_hT=f_hT, f_down=f_down, G=value_out, a_lnT=a_lnT, m_T=m_T, m_route=m_route,
                        m_cwT=m_cwT, gate=gate, up=up, cw=cw, down=down)
            in_order("pe", mine)

        @block.scalar
        def _(act):
            act.wait_ge(s["ld_ctxT"], 16)
            act.copy(ctxH[:, :, PAD:], ctxTr.rearrange("p (b l) -> p b l", b=B)).then_inc(s["ctx_split"], 1)
            act.wait_ge(s["ld_small"], 80)
            act.activation(tg[:, :], gates[:, :], ACT.Tanh).then_inc(s["gate_done"], 1)
            act.wait_ge(s["ld_sel"], 48)
            act.copy(identb[:, :], ident[:, :]).then_inc(s["gate_done"], 1)
            gated_tiles = ((0, 1, 2), (3, 4), (5, 6, 7), ())
            for et in range(2):
                for hf in range(2):
                    act.wait_ge(s["conv_done"], 2 * et + hf + 1)
                    act.activation(u[:, et, 512 * hf:512 * hf + 512], ps[:, 2 * et + hf, :], ACT.Silu,
                                   bias=ec[:, et, 0:1]).then_inc(s["u_done"], 1)
                    act.wait_ge(s["znb"], 1)
                    for i in gated_tiles[2 * et + hf]:
                        act.activation(sz[:, i, :], x[:, i, :], ACT.Silu, bias=nb8[:, i:i + 1], scale=rstd[:, i:i + 1]
                                       ).then_inc(s["sz_done"], 1)
            act.wait_ge(s["xproj_done"], 1)
            act.copy(dtl, ps[0:DR, 0:2, :].rearrange("p a n -> p (a n)")).then_inc(s["dtl_evac"], 1)
            act.preload_act_table_set("natural_log_exp_and_others")
            act.activation(nacol[:, :], acol[:, :], ACT.Exp).then_inc(s["nacol_done"], 1)
            def soft_abs(c):
                et, c_ = SOFT[c]
                act.wait_ge(s["dpre_done"], c + 1)
                act.activation(dab[et][:, c_], ps[:, 2 + 2 * et:4 + 2 * et, :].rearrange("p a n -> p (a n)")[:, c_], ACT.Abs,
                               bias=ec[:, et, 1:2]).then_inc(s["dabs"], 1)

            def soft_exp(c):
                et, c_ = SOFT[c]
                act.wait_ge(s["dabs"], c + 1)
                act.activation(dex[et][:, c_], dab[et][:, c_], ACT.Exp, scale=-1.0).then_inc(s["dexp"], 1)

            def soft_1p(c):
                et, c_ = SOFT[c]
                act.wait_ge(s["dexp"], c + 1)
                act.activation(dab[et][:, c_], dex[et][:, c_], ACT.Identity, bias=ones[:, 0:1]).then_inc(s["done_1p"], 1)

            def soft_ln(c):
                et, c_ = SOFT[c]
                act.wait_ge(s["done_1p"], c + 1)
                act.activation(dlt[et][:, c_], dab[et][:, c_], ACT.Ln).then_inc(s["dln"], 1)

            def soft_hi(part):
                c, half = SPLIT[part]
                et, c_ = SOFT[c]
                r_ = slice(64 * half, 64 * half + 64)
                act.wait_ge(s["ddelta"], 2 * c + 1)
                act.copy(XD[r_, 2 * et + half, c_], dlt[et][r_, c_]).then_inc(s["dhi_done"], 1)
                act.wait_ge(s["ddelta"], 2 * c + 2)
                act.copy(XU[r_, 2 * et + half, c_], dab[et][r_, c_]).then_inc(s["dhi_done"], 1)

            for c in range(2):
                soft_abs(c)
                soft_exp(c)
                soft_1p(c)
                soft_ln(c)
            act.wait_ge(s["xproj_done"], 2)
            act.copy(Bs, ps[:, 6:8, :].rearrange("p a n -> p (a n)")).then_inc(s["bc_evac"], 1)
            for part in range(4):
                soft_hi(part)
            act.wait_ge(s["xproj_done"], 3)
            act.copy(Cs, ps[:, 6:8, :].rearrange("p a n -> p (a n)")).then_inc(s["bc_evac"], 1)
            soft_abs(2)
            act.wait_ge(s["nacol_done"], 2)
            act.wait_ge(s["pool_init"], 8)
            for t in range(ST):
                act.wait_ge(s["dbc_done"], t + 1)
                if t >= 2:
                    act.wait_ge(s["scan_done"], t - 1)
                act.activation(dA[t % 2].rearrange("p (b l) -> p b l", b=B)[:, :, 1:S],
                               ps[:, 0:2, :].rearrange("p a (b l) -> p (a b) l", b=2)[:, :, 1:S], ACT.Exp,
                               scale=nacol[:, t:t + 1]).then_inc(s["exp_done"], 1)
                if t in (13, 15):
                    w = (t - 13) // 2
                    act.wait_ge(s[f"round{w}"], 2)
                    act.activation(w12q[:, w, :], wraw[w], ACT.Identity, bias=nmagic[:, :]).then_inc(s["wq_done"], 1 + 3 * w)
                if t == 1:
                    soft_exp(2)
                if t == 2:
                    soft_1p(2)
                if t == 4:
                    soft_ln(2)
                if t in (9, 11):
                    soft_hi(4 + (t - 9) // 2)

            def f_up(i):
                act.wait_ge(s["fscale"], i // 2 + 1)
                if i >= 1:
                    act.wait_ge(s["fact"], 2 * i)
                for n in range(2):
                    act.wait_ge(s["mm1_done"], 2 * i + n + 1)
                    act.activation(g1[:, 512 * n:512 * n + 512], ps[:, 6 + n, :], ACT.Gelu, scale=q8[:, 6, i:i + 1]
                                   ).then_inc(s["g1_done"], 1)
                act.wait_ge(s["g1_done"], 2 * i + 2)
                if i >= 2:
                    act.wait_ge(s["fhq"], i - 1)
                act.activation(g2[i % 2], g1, ACT.Gelu).then_inc(s["fact"], 1)

            def f_square(i):
                act.wait_ge(s["fact"], 2 * i + 1)
                act.activation(g1, g2[i % 2], ACT.Square, accum_out=q8[:, 7, i:i + 1]).then_inc(s["fact"], 1)

            def value_out(g):
                for n in (2 * g, 2 * g + 1):
                    act.wait_ge(s["G_done"], n + 1)
                    act.copy(G[:, 2 * n:2 * n + 2, :].rearrange("p a n -> p (a n)"), ps[:, 4 + n % 2, :]).then_inc(s["G_evac"], 1)

            def f_stat(b):
                if b == 0:
                    act.wait_ge(s["ld_wq"], 16)
                    act.wait_ge(s["ubc_done"], ST)
                    for n in range(4):
                        k, c = divmod(n, 2)
                        act.copy(WqH[:, k, 1024 * c:1024 * c + 1024], Wqr[:, 1024 * n:1024 * n + 1024]).then_inc(s["wqh"], 1)

            def a_lnT(b):
                act.wait_ge(s["axT_done"], b + 1)
                if b >= 2:
                    act.wait_ge(s["piece_done"], 16 * (b - 1))
                act.copy(xT[:, b % 2, 0, :, :].rearrange("p k t -> p (k t)"), ps[:, 7, :]).then_inc(s["axTH"], 1)

            def piece(p):
                act.wait_ge(s["piece_done"], p + 1)
                if p >= 4:
                    act.wait_ge(s["pT_done"], p - 3)
                    act.wait_ge(s["psq_done"], p - 3)
                act.copy(praw[p % 4], ps[:, 6, :]).then_inc(s["raw_done"], 1)

            def softmax(n):
                act.wait_ge(s["hmax"], 2 * n + 2)
                if n >= 4:
                    act.wait_ge(s["PT_done"], n - 3)
                for qt in range(2):
                    act.activation(Pb[n % 4][:, qt, :], ps[:, n % 2, qt * S:qt * S + S], ACT.Exp,
                                   bias=hs[:, n % 4, 2 + qt:3 + qt], scale=rq[:, (n // GRP) % RING, n % GRP, qt:qt + 1],
                                   accum_out=hs[:, n % 4, 4 + qt:5 + qt]).then_inc(s["exps"], 1)

            def PT_half(n):
                act.wait_ge(s["PT_done"], n + 1)
                if n >= 3:
                    act.wait_ge(s["U_done"], n - 2)
                act.copy(PT[n % 3].rearrange("p k q -> p (k q)"), ps[:, 2 + n % 2, :]).then_inc(s["PT_evac"], 1)

            def m_route(b):
                act.wait_ge(s["rneg"], 2 * b + 2)
                for i in range(2 * b, 2 * b + 2):
                    act.activation(rt[:, i, 0, :], ps[:, 7, i * E:i * E + E], ACT.Exp, bias=rt[:, i, 4, 0:1],
                                   accum_out=rt[:, i, 4, 1:2]).then_inc(s["rexp"], 1)

            def x_split(c):
                act.wait_ge(s["mxT_evac"], 2 * c + 2)
                act.wait_ge(s["piece_done"], 16 * B)
                for k in range(2):
                    act.copy(xmH[:, k, c * 512:c * 512 + 512], xmf[:, k, c * 512:c * 512 + 512]).then_inc(s["xmh"], 1)

            def w_split(ft):
                act.wait_ge(s[f"ld_moe{ft % 4}"], 16 * (ft // 4 + 1))
                act.wait_ge(s["piece_done"], 16 * B)
                if ft >= FIRST:
                    act.wait_ge(s["down_done"], ORDER.index((ft - FIRST, 1)) + 1)
                act.copy(wH[ft % FIRST], wr[ft % 4]).then_inc(s["wsplit"], 1)

            def silu(m):
                rows = min(P, FALL - ORDER[m][0] * P)
                act.wait_ge(s["gate_mm"], m + 1)
                if m == 0:
                    act.wait_ge(s["pT_done"], 16 * B)
                    act.wait_ge(s["psq_done"], 16 * B)
                if m >= 2:
                    act.wait_ge(s["m1_done"], m - 1)
                act.activation(sg[m % 2][0:rows, :], ps[0:rows, 4, :], ACT.Silu).then_inc(s["silu_done"], 1)

            def hidden_hi(m):
                rows = min(P, FALL - ORDER[m][0] * P)
                if m < 2 * FTR:
                    act.wait_ge(s["m2_done"], m + 1)
                else:
                    act.wait_ge(s["m1_done"], m + 1)
                if m >= 3:
                    act.wait_ge(s["down_done"], m - 2)
                act.copy(hH[m % 3][0:rows, :], hm[m % 2][0:rows, :]).then_inc(s["hH_done"], 1)

            mine = dict(piece=piece, scores=softmax, probs_T=PT_half, f_stat=f_stat, f_up=f_up, f_square=f_square, G=value_out, a_lnT=a_lnT,
                        m_route=m_route, x_split=x_split, w_split=w_split, gate=silu, cw=hidden_hi)
            in_order("act", mine)

        @block.vector
        def _(dve):
            chain = [0]

            def link(ins):
                chain[0] += 1
                ins.then_inc(s["dve_chain"], 1)
                dve.wait_ge(s["dve_chain"], chain[0])

            dve.wait_ge(s["ld_wc"], 32)
            dve.tensor_tensor(wc, cwb, inT[:, :].unsqueeze(1).to_broadcast([P, TAPS, DI]), ALU.mult).then_inc(s["conv_w"], 1)
            dve.wait_ge(s["conv_w"], 1)
            dve.tensor_copy(wcH, wc).then_inc(s["conv_w"], 1)
            dve.wait_ge(s["ctx_split"], 1)
            dve.tensor_tensor(ctxL[:, :, PAD:], ctxTr.rearrange("p (b l) -> p b l", b=B), ctxH[:, :, PAD:].bitcast(F32), ALU.subtract
                              ).then_inc(s["ctx_split"], 1)
            dve.wait_ge(s["conv_w"], 2)
            dve.tensor_tensor(wcL, wc, wcH.bitcast(F32), ALU.subtract).then_inc(s["conv_w"], 1)
            dve.wait_ge(s["ld_x"], 16)
            dve.wait_ge(s["pool_init"], 6)

            def stats(tiles, name, base):
                for i in tiles:
                    dve.bn_stats(st6[:, i, :], x[:, i, :]).then_inc(s[name], 1)
                dve.wait_ge(s[name], base + len(tiles))
                for i in tiles:
                    dve.bn_aggr(mv[:, i, :], st6[:, i, :]).then_inc(s[name], 1)
                dve.wait_ge(s[name], base + 2 * len(tiles))
                a, z = tiles[0], tiles[-1] + 1
                dve.tensor_scalar(ve[:, a:z], mv[:, a:z, 1], EPS, None, ALU.add).then_inc(s[name], 1)

            stats(range(NT), "zstat", 0)
            dve.wait_ge(s["zpow"], 1)
            dve.scalar_tensor_tensor(nb8[:, :], mv[:, :, 0], -1.0, rstd[:, :], ALU.mult, ALU.mult).then_inc(s["znb"], 1)
            dve.wait_ge(s["ld_sel"], 48)
            dve.tensor_copy(sel[:, :, :], selr).then_inc(s["sel_ready"], 1)
            dve.wait_ge(s["ld_w"], 32)
            for w in range(2):
                dve.tensor_reduce(wsum[:, w:w + 1], wraw[w], AX.X, ALU.add, apply_absolute_value=True).then_inc(s["wabs"], 1)
            dve.wait_ge(s["wsum_done"], 1)
            dve.tensor_scalar(mw[:, :], ps[:, 7, 0:2], 1.0 / (INNER * DM), EPS, ALU.mult, ALU.max).then_inc(s["wq_done"], 1)
            dve.wait_ge(s["wq_done"], 1)
            dve.reciprocal(iw[:, :], mw[:, :]).then_inc(s["iw_done"], 1)
            dve.wait_ge(s["iw_done"], 1)
            clip_round(dve, 0, "round0")

            dve.wait_ge(s["nacol_done"], 1)
            dve.tensor_scalar(nacol[:, :], nacol[:, :], -1.0, None, ALU.mult).then_inc(s["nacol_done"], 1)

            def soft_relu(c):
                et, c_ = SOFT[c]
                dve.wait_ge(s["dpre_done"], c + 1)
                dve.wait_ge(s["dabs"], c + 1)
                pw = ps[:, 2 + 2 * et:4 + 2 * et, :].rearrange("p a n -> p (a n)")[:, c_]
                dve.tensor_scalar(dre[et][:, c_], pw, ec[:, et, 1:2], 0.0, ALU.add, ALU.max).then_inc(s["drelu"], 1)

            def soft_1p(c):
                et, c_ = SOFT[c]
                dve.wait_ge(s["done_1p"], c + 1)
                link(dve.scalar_tensor_tensor(dex[et][:, c_], dab[et][:, c_], 1.0, dex[et][:, c_], ALU.subtract, ALU.subtract))
                dve.wait_ge(s["drelu"], c + 1)
                link(dve.tensor_tensor(dex[et][:, c_], dre[et][:, c_], dex[et][:, c_], ALU.subtract))

            def soft_delta(c):
                et, c_ = SOFT[c]
                dve.wait_ge(s["dln"], c + 1)
                dve.tensor_tensor(dlt[et][:, c_], dlt[et][:, c_], dex[et][:, c_], ALU.add).then_inc(s["ddelta"], 1)
                dve.wait_ge(s["ddelta"], 2 * c + 1)
                dve.tensor_tensor(dab[et][:, c_], dlt[et][:, c_], u[:, et, c_], ALU.mult).then_inc(s["ddelta"], 1)

            def soft_lo(part):
                c, half = SPLIT[part]
                et, c_ = SOFT[c]
                r_ = slice(64 * half, 64 * half + 64)
                o_ = slice(64 - 64 * half, 128 - 64 * half)
                dve.wait_ge(s["dhi_done"], 2 * part + 1)
                dve.tensor_tensor(XD[o_, 2 * et + half, c_], dlt[et][r_, c_], XD[r_, 2 * et + half, c_].bitcast(F32),
                                  ALU.subtract).then_inc(s["dlo_done"], 1)
                dve.wait_ge(s["ddelta"], 2 * c + 2)
                dve.wait_ge(s["dhi_done"], 2 * part + 2)
                dve.tensor_tensor(XU[o_, 2 * et + half, c_], dab[et][r_, c_], XU[r_, 2 * et + half, c_].bitcast(F32),
                                  ALU.subtract).then_inc(s["dlo_done"], 1)

            soft_relu(0)
            soft_1p(0)
            soft_relu(1)
            soft_delta(0)
            soft_1p(1)
            soft_delta(1)
            for part in range(4):
                soft_lo(part)
            soft_relu(2)

            def dbu(t):
                dve.wait_ge(s["ubc_done"], t + 1)
                if t >= 2:
                    dve.wait_ge(s["scan_done"], t - 1)
                if t == 0:
                    dve.wait_ge(s["dlo_done"], 8)
                    dve.wait_ge(s["bc_evac"], 1)
                pu = ps[:, 2 + 2 * (t % 2):4 + 2 * (t % 2), :].rearrange("p a n -> p (a n)")
                dve.tensor_tensor(dBu[t % 2], pu, Bs, ALU.mult).then_inc(s["dbu_done"], 1)

            def y_last(b):
                c_ = slice(b * S, b * S + S)
                dve.wait_ge(s["nsum_done"], ST + b // 2)
                dve.scalar_tensor_tensor(yg[:, 1, c_], u[:, 1, c_], ec[:, 1, 2:3], ps[:, 6 + b // 2, (b % 2) * S:(b % 2) * S + S],
                                         ALU.mult, ALU.add).then_inc(s["yevac"], 1)
                dve.wait_ge(s["yevac"], b + 2)
                ygv = yg[:, 1, c_]
                dve.tensor_tensor(ygv, ygv, sz[:, 2 * b + 1, :], ALU.mult).then_inc(s["yg_done"], 1)

            def y_out(et):
                dve.wait_ge(s["nsum_done"], JT * (et + 1))
                py = ps[:, 6:8, :].rearrange("p a n -> p (a n)")
                dve.scalar_tensor_tensor(yg[:, et, :], u[:, et, :], ec[:, et, 2:3], py, ALU.mult, ALU.add).then_inc(s["yevac"], 1)

            def y_gate(et):
                dve.wait_ge(s["yevac"], et + 1)
                dve.wait_ge(s["sz_done"], NT)
                ygv = yg[:, et, :].rearrange("p (b l) -> p b l", b=B)
                dve.tensor_tensor(ygv, ygv, sz.rearrange("p (b h) l -> p h b l", h=2)[:, et], ALU.mult).then_inc(s["yg_done"], 1)

            dbu(0)
            for t in range(ST):
                if t + 1 < ST:
                    dbu(t + 1)
                if t == JT + NSUM_LAG - 1:
                    y_out(0)
                dve.wait_ge(s["exp_done"], t + 1)
                dve.wait_ge(s["dbu_done"], t + 1)
                if t >= 2:
                    dve.wait_ge(s["hc_done"], t - 1)
                dve.tensor_tensor_scan(hb[t % 2], dA[t % 2], dBu[t % 2], 0.0, ALU.mult, ALU.add).then_inc(s["scan_done"], 1)
                if t == 2:
                    soft_1p(2)
                if t == 6:
                    soft_delta(2)
                if t == JT + NSUM_LAG + 1:
                    y_gate(0)
                if t in (10, 12):
                    soft_lo(4 + (t - 10) // 2)
            dve.wait_ge(s["gate_done"], 1)

            def x1(b):
                if b < 2:
                    y_last(2 * b)
                    y_last(2 * b + 1)
                dve.wait_ge(s["yT_done"], B + b + 1)
                x_ = x[:, 2 * b:2 * b + 2, :].rearrange("p i c -> p (i c)")
                dve.scalar_tensor_tensor(x_, ps[:, b, :], tg[:, 0:1], x_, ALU.mult, ALU.add).then_inc(s["x1_done"], 1)

            def f_stat(b):
                z = slice(2 * b, 2 * b + 2)
                dve.wait_ge(s["x1_done"], b + 1)
                stats(range(2 * b, 2 * b + 2), "fst", 5 * b)

            def f_norm(b):
                z = slice(2 * b, 2 * b + 2)
                dve.wait_ge(s["fpow"], 2 * b + 1)
                link(dve.scalar_tensor_tensor(q8[:, 0, z], mv[:, z, 1], float(DM), rstd[:, z], ALU.mult, ALU.mult))
                dve.tensor_tensor(q8[:, 0, z], q8[:, 0, z], rstd[:, z], ALU.mult).then_inc(s["fnorm"], 1)
                for i in range(2):
                    dve.tensor_scalar(xl[:, i, :], x[:, 2 * b + i, :], mv[:, 2 * b + i, 0:1], rstd[:, 2 * b + i:2 * b + i + 1],
                                      ALU.subtract, ALU.mult).then_inc(s["fxl"], 1)

            def row_scales(norm, peak, z, width):
                link(dve.tensor_scalar(norm, norm, 1e-12, None, ALU.max))
                link(dve.reciprocal(norm, norm))
                link(dve.scalar_tensor_tensor(q8[:, 3, z], peak, float(width) ** 0.5, norm, ALU.mult, ALU.mult))
                link(dve.tensor_scalar(q8[:, 3, z], q8[:, 3, z], EPS, None, ALU.max))

            def row_steps(norm, z, width):
                link(dve.reciprocal(q8[:, 4, z], q8[:, 3, z]))
                link(dve.scalar_tensor_tensor(q8[:, 5, z], norm, 127.0 * float(width) ** 0.5, q8[:, 4, z], ALU.mult, ALU.mult))

            def f_quant(b):
                z = slice(2 * b, 2 * b + 2)
                if b == 0:
                    link(dve.tensor_scalar(k2[:, :], mw[:, 1:2], tg[:, 1:2], 1.0 / 127.0, ALU.mult, ALU.mult))
                dve.wait_ge(s["fxl"], 2 * b + 2)
                link(dve.tensor_reduce(q8[:, 2, z], xl, AX.X, ALU.max, apply_absolute_value=True))
                dve.wait_ge(s["fpow"], 2 * b + 2)
                row_scales(q8[:, 1, z], q8[:, 2, z], z, DM)
                row_steps(q8[:, 1, z], z, DM)
                dve.tensor_scalar(q8[:, 6, z], q8[:, 3, z], mw[:, 0:1], 1.0 / 127.0, ALU.mult, ALU.mult).then_inc(s["fscale"], 1)
                for i in range(2):
                    link(dve.tensor_scalar(xl[:, i, :], xl[:, i, :], q8[:, 5, 2 * b + i:2 * b + i + 1], MAGIC, ALU.mult, ALU.add))
                dve.tensor_scalar(xq.rearrange("p i c -> p (i c)"), xl.rearrange("p i c -> p (i c)"), MAGIC, None, ALU.subtract
                                  ).then_inc(s["fq"], 1)

            def w_low(n):
                if n == 0:
                    dve.wait_ge(s["ld_wk"], 16)
                    link(dve.tensor_copy(WkH, Wkr))
                    dve.tensor_tensor(WkL, Wkr, WkH.bitcast(F32), ALU.subtract).then_inc(s["wk_split"], 2)
                    link(dve.tensor_scalar(gkq[:, :], gqk[:, 0:1], gqk[:, 1:2], float(P) ** -0.5, ALU.mult, ALU.mult))
                else:
                    k, c = divmod(n - 1, 2)
                    dve.wait_ge(s["wqh"], n)
                    dve.tensor_tensor(WqL[:, k, 1024 * c:1024 * c + 1024], Wqr[:, 1024 * (n - 1):1024 * n],
                                      WqH[:, k, 1024 * c:1024 * c + 1024].bitcast(F32), ALU.subtract).then_inc(s["wql"], 1)

            def f_xqT(b):
                dve.wait_ge(s["fqT_done"], b + 1)
                dve.tensor_copy(xqT.rearrange("p k t -> p (k t)"), ps[:, 7, :].bitcast(BF16)[:, 0:512]).then_inc(s["fqT_evac"], 1)

            def f_peak(i):
                dve.wait_ge(s["fact"], 2 * i + 1)
                link(dve.tensor_reduce(q8[:, 2, i:i + 1], g2[i % 2], AX.X, ALU.max, apply_absolute_value=True))

            def f_scale(i):
                i_ = slice(i, i + 1)
                dve.wait_ge(s["fpow2"], i + 1)
                row_scales(q8[:, 8, i_], q8[:, 2, i_], i_, INNER)

            def f_scale2(i):
                i_ = slice(i, i + 1)
                row_steps(q8[:, 8, i_], i_, INNER)
                link(dve.tensor_tensor(q8[:, 9, i_], q8[:, 3, i_], k2[:, :], ALU.mult))

            def f_round(i):
                i_ = slice(i, i + 1)
                dve.wait_ge(s["fact"], 2 * i + 2)
                link(dve.tensor_scalar(g2[i % 2], g2[i % 2], q8[:, 5, i_], MAGIC, ALU.mult, ALU.add))
                dve.tensor_scalar(hq, g2[i % 2], MAGIC, None, ALU.subtract).then_inc(s["fhq"], 1)

            def f_hT(i):
                dve.wait_ge(s["fT_done"], i + 1)
                dve.tensor_copy(hT.rearrange("p k t -> p (k t)"), ps[:, 7, :].bitcast(BF16)).then_inc(s["fT_evac"], 1)

            def f_down(i):
                dve.wait_ge(s["mm2_done"], i + 1)
                dve.scalar_tensor_tensor(x[:, i, :], ps[:, 6, 0:DM], q8[:, 9, i:i + 1], x[:, i, :], ALU.mult, ALU.add
                                         ).then_inc(s["x2_done"], 1)

            def a_ln(b):
                dve.wait_ge(s["x2_done"], 2 * b + 2)
                stats(range(2 * b, 2 * b + 2), "aln", 5 * b)

            def a_xn(b):
                dve.wait_ge(s["apow"], b + 1)
                for i in range(2):
                    dve.tensor_scalar(xn[:, i, :], x[:, 2 * b + i, :], mv[:, 2 * b + i, 0:1], rstd[:, 2 * b + i:2 * b + i + 1],
                                      ALU.subtract, ALU.mult).then_inc(s["axn"], 1)

            def a_lnT(b):
                dve.wait_ge(s["axTH"], b + 1)
                dve.tensor_tensor(xT[:, b % 2, 1, :, :].rearrange("p k t -> p (k t)"), ps[:, 7, :],
                                  xT[:, b % 2, 0, :, :].rearrange("p k t -> p (k t)").bitcast(F32), ALU.subtract
                                  ).then_inc(s["axTL"], 1)

            def piece_stats(p):
                dve.wait_ge(s["psq_done"], p + 1)
                if p >= 4:
                    dve.wait_ge(s["prv_done"], p - 3)
                dve.tensor_reduce(rr[:, p % 4, :], psq[p % 2].rearrange("p (a c) -> p a c", a=GRP), AX.X, ALU.add
                                  ).then_inc(s["prs"], 1)
                dve.wait_ge(s["prs"], 2 * p + 1)
                dve.tensor_scalar(rr[:, p % 4, :], rr[:, p % 4, :], 1.0 / P, EPS, ALU.mult, ALU.add).then_inc(s["prs"], 1)

            def piece_evac(p):
                G_, kind = divmod(p, 4)
                dst = (kT if kind < 2 else qT)[:, G_ % RING, :, (kind % 2) * P:(kind % 2) * P + P]
                src = ps[:, 7, :].rearrange("p (a t) -> p a t", a=GRP)
                dve.wait_ge(s["pT_done"], p + 1)
                if G_ >= RING:
                    dve.wait_ge(s["sc_done"], GRP * (G_ - RING + 1))
                if p == 0:
                    dve.wait_ge(s["wql"], 4)
                if p == GRP + 2:
                    dve.wait_ge(s["G_done"], H // 2)
                if kind < 2:
                    dve.tensor_scalar(dst, src, gkq[:, 0:1], None, ALU.mult).then_inc(s["pT_evac"], 1)
                else:
                    dve.tensor_copy(dst, src).then_inc(s["pT_evac"], 1)

            def head_max(n):
                dve.wait_ge(s["sc_done"], n + 1)
                if n >= 4:
                    dve.wait_ge(s["pnorm_done"], n - 3)
                dve.tensor_reduce(hs[:, n % 4, 0:2], ps[:, n % 2, :].rearrange("p (a k) -> p a k", a=2), AX.X, ALU.max
                                  ).then_inc(s["hmax"], 1)
                dve.wait_ge(s["hmax"], 2 * n + 1)
                if n % GRP == 0:
                    dve.wait_ge(s["prv_done"], 4 * (n // GRP) + 4)
                dve.scalar_tensor_tensor(hs[:, n % 4, 2:4], hs[:, n % 4, 0:2], -1.0, rq[:, (n // GRP) % RING, n % GRP, :],
                                         ALU.mult, ALU.mult).then_inc(s["hmax"], 1)

            def head_recip(n):
                dve.wait_ge(s["exps"], 2 * n + 2)
                dve.reciprocal(hs[:, n % 4, 6:8], hs[:, n % 4, 4:6]).then_inc(s["hrec"], 1)

            def U_out(n):
                dve.wait_ge(s["U_done"], n + 1)
                if n >= 3:
                    dve.wait_ge(s["y_done"], n - 2)
                dve.tensor_copy(Us[n % 3], ps[:, 4, 0:S]).then_inc(s["U_evac"], 1)

            def x3(b):
                dve.wait_ge(s["y_done"], H * (b + 1))
                x_ = x[:, 2 * b:2 * b + 2, :].rearrange("p i c -> p (i c)")
                dve.scalar_tensor_tensor(x_, ps[:, 5, :], tg[:, 2:3], x_, ALU.mult, ALU.add).then_inc(s["x3_done"], 1)

            def y_ready(n):
                if n % H == H - 1:
                    x3(n // H)

            def m_ln(b):
                dve.wait_ge(s["x3_done"], b + 1)
                stats(range(2 * b, 2 * b + 2), "mln", 5 * b)

            def m_xn(b):
                dve.wait_ge(s["mpow"], b + 1)
                for i in range(2):
                    dve.tensor_scalar(xm[:, i, :], x[:, 2 * b + i, :], mv[:, 2 * b + i, 0:1], rstd[:, 2 * b + i:2 * b + i + 1],
                                      ALU.subtract, ALU.mult).then_inc(s["mxn"], 1)

            def m_T(b):
                dve.wait_ge(s["mxT_done"], b + 1)
                dve.tensor_copy(xmf[:, :, b * S:b * S + S], ps[:, 7, :].rearrange("p (k t) -> p k t", k=2)).then_inc(s["mxT_evac"], 1)

            def m_route(b):
                z = slice(2 * b, 2 * b + 2)
                dve.wait_ge(s["rl_done"], b + 1)
                for i in range(2 * b, 2 * b + 2):
                    dve.tensor_reduce(rt[:, i, 4, 0:1], ps[:, 7, i * E:i * E + E], AX.X, ALU.max, negate=True).then_inc(s["rneg"], 1)

            def m_pick(b):
                z = slice(2 * b, 2 * b + 2)
                dve.wait_ge(s["rexp"], 2 * b + 2)
                link(dve.reciprocal(rt[:, z, 4, 2:3], rt[:, z, 4, 1:2]))
                link(dve.tensor_tensor(rt[:, z, 0, :], rt[:, z, 0, :], rt[:, z, 4, 2:3].to_broadcast([P, 2, E]), ALU.mult))
                for i in range(2 * b, 2 * b + 2):
                    link(dve.max(rt[:, i, 1, :], rt[:, i, 0, :]))
                for i in range(2 * b, 2 * b + 2):
                    link(dve.max_index(rti[:, i, :], rt[:, i, 1, :], rt[:, i, 0, :]))

            def m_weight(b):
                z = slice(2 * b, 2 * b + 2)
                link(dve.tensor_copy(rt[:, z, 2, :], rti[:, z, :]))
                link(dve.tensor_tensor(rt[:, z, 4, 3:4], rt[:, z, 1, 0:1], rt[:, z, 1, 1:2], ALU.add))
                link(dve.tensor_scalar(rt[:, z, 4, 3:4], rt[:, z, 4, 3:4], 1e-20, None, ALU.add))
                link(dve.reciprocal(rt[:, z, 4, 4:5], rt[:, z, 4, 3:4]))
                link(dve.tensor_tensor(rt[:, z, 3, 0:2], rt[:, z, 1, 0:2], rt[:, z, 4, 4:5].to_broadcast([P, 2, 2]), ALU.mult))

            def m_spread(b):
                z = slice(2 * b, 2 * b + 2)
                for i in range(2 * b, 2 * b + 2):
                    link(dve.tensor_scalar(rt[:, i, 5, :], iota8[:, :], rt[:, i, 2, 0:1], rt[:, i, 3, 0:1], ALU.is_equal, ALU.mult))
                    link(dve.tensor_scalar(rt[:, i, 0, :], iota8[:, :], rt[:, i, 2, 1:2], rt[:, i, 3, 1:2], ALU.is_equal, ALU.mult))
                link(dve.tensor_tensor(rt[:, z, 5, :], rt[:, z, 5, :], rt[:, z, 0, :], ALU.add))
                link(dve.tensor_copy(cwR[:, :, :], rt[:, z, 5, :]))
                dve.wait_ge(s["cwz"], 1)
                if b >= 1:
                    dve.wait_ge(s["cwT_done"], b)
                link(dve.tensor_copy(cwHL[:, :, 0:E], cwR[:, :, :].bitcast(F32)))
                dve.tensor_tensor(cwHL[:, :, 32:32 + E], rt[:, z, 5, :], cwR[:, :, :].bitcast(F32), ALU.subtract
                                  ).then_inc(s["cw_ready"], 1)

            def m_cwT(b):
                dve.wait_ge(s["cwT_done"], b + 1)
                dve.tensor_copy(cwTf[:, b * S:b * S + S], ps[0:64, 7, 0:S]).then_inc(s["cwT_evac"], 1)
                if b == 1:
                    dve.wait_ge(s["cwT_evac"], 2)
                if b == B - 1:
                    dve.wait_ge(s["cwT_evac"], B)
                    dve.tensor_copy(cwT[:, 512:1024], cwTf[:, 512:1024]).then_inc(s["cwc"], 1)

            def x_split(c):
                for k in range(2):
                    dve.wait_ge(s["xmh"], 2 * c + k + 1)
                    dve.tensor_tensor(xmL[:, k, c * 512:c * 512 + 512], xmf[:, k, c * 512:c * 512 + 512],
                                      xmH[:, k, c * 512:c * 512 + 512].bitcast(F32), ALU.subtract).then_inc(s["xml"], 1)
                if c == 0:
                    dve.wait_ge(s["piece_done"], 16 * B)
                    dve.tensor_copy(cwT[:, 0:512], cwTf[:, 0:512]).then_inc(s["cwc"], 1)

            def w_split(ft):
                dve.wait_ge(s["wsplit"], ft + 1)
                dve.tensor_tensor(wL[ft % FIRST], wr[ft % 4], wH[ft % FIRST].bitcast(F32), ALU.subtract).then_inc(s["wsplitL"], 1)

            def gated(m):
                rows = min(P, FALL - ORDER[m][0] * P)
                dve.wait_ge(s["silu_done"], m + 1)
                dve.wait_ge(s["up_mm"], m + 1)
                if m >= 2:
                    dve.wait_ge(s["hL_done"], m - 1)
                    dve.wait_ge(s["hH_done"], m - 1)
                ins = dve.tensor_tensor(hm[m % 2][0:rows, :], ps[0:rows, 5, :], sg[m % 2][0:rows, :], ALU.mult)
                ins.then_inc(s["m1_done"], 1)

            def weighted(m):
                rows = min(P, FALL - ORDER[m][0] * P)
                hm_ = hm[m % 2][0:rows, :]
                if m < 2 * FTR:
                    dve.wait_ge(s["m1_done"], m + 1)
                    dve.wait_ge(s["cw_mm"], m + 1)
                    dve.tensor_tensor(hm_, ps[0:rows, 6, :], hm_, ALU.mult).then_inc(s["m2_done"], 1)

            mine = dict(x1=x1, piece=piece_stats, head_max=head_max, scores=head_recip, piece_T=piece_evac, values=U_out,
                        project_out=y_ready, f_stat=f_stat, f_norm=f_norm, w_low=w_low, f_quant=f_quant, f_xqT=f_xqT, f_peak=f_peak,
                        f_scale=f_scale, f_scale2=f_scale2, f_round=f_round, f_hT=f_hT, f_down=f_down, a_stat=a_ln, a_xn=a_xn, a_lnT=a_lnT,
                        m_stat=m_ln, m_xn=m_xn, m_T=m_T, m_route=m_route, m_pick=m_pick, m_weight=m_weight, m_spread=m_spread, m_cwT=m_cwT, x_split=x_split,
                        w_split=w_split, up=gated, cw=weighted)
            in_order("dve", mine)
            for b in range(B):
                dve.wait_ge(s["down_done"], 2 * FT - 1 + b // 2)
                for i in range(2):
                    dve.scalar_tensor_tensor(yo[b][:, i, :], ps[:, b, i * DM:i * DM + DM], tg[:, 3:4], x[:, 2 * b + i, :],
                                             ALU.mult, ALU.add).then_inc(s["out_done"], 1)

        @block.gpsimd
        def _(pool):
            pool.memset(ctxH[:, :, 0:PAD].bitcast(F32), 0.0).then_inc(s["pool_init"], 1)
            pool.memset(ctxL[:, :, 0:PAD].bitcast(F32), 0.0).then_inc(s["pool_init"], 1)
            pool.memset(phalf[:, :], 0.5).then_inc(s["pool_init"], 1)
            pool.memset(nhalf[:, :], -0.5).then_inc(s["pool_init"], 1)
            pool.memset(nmagic[:, :], -MAGIC).then_inc(s["pool_init"], 1)
            pool.memset(ones[:, :], 1.0).then_inc(s["pool_init"], 1)
            pool.wait_ge(s["pool_init"], 6)
            pool.wait_ge(s["zstat"], 2 * NT + 1)
            pool.tensor_tensor(rstd[:, :], ve[:, :], nhalf[:, 0:NT], ALU.pow).then_inc(s["zpow"], 1)
            pool.wait_ge(s["sel_ready"], 1)
            pool.wait_ge(s["ctx_split"], 2)
            for i in range(2):
                pool.memset(dA[i].rearrange("p (b l) -> p b l", b=B)[:, :, 0:1], 0.0).then_inc(s["pool_init"], 1)
            pool.wait_ge(s["iw_done"], 1)
            clip_round(pool, 1, "round1")
            pool.wait_ge(s["bc_evac"], 2)
            pool.wait_ge(s["dlo_done"], 8)
            for t in range(ST):
                pool.wait_ge(s["scan_done"], t + 1)
                if t >= 3:
                    pool.wait_ge(s["nsum_done"], t - 2)
                if t < ST - 1:
                    pool.tensor_tensor(hC[t % 3], hb[t % 2], Cs, ALU.mult).then_inc(s["hc_done"], 1)
                else:
                    for hf in range(2):
                        c_ = slice(512 * hf, 512 * hf + 512)
                        pool.tensor_tensor(hC[t % 3][:, c_], hb[t % 2][:, c_], Cs[:, c_], ALU.mult).then_inc(s["hc_done"], 1)
            pool.wait_ge(s["sz_done"], NT)

            def f_stat(b):
                z = slice(2 * b, 2 * b + 2)
                pool.wait_ge(s["fst"], 5 * b + 5)
                pool.tensor_tensor(rstd[:, z], ve[:, z], nhalf[:, 0:2], ALU.pow).then_inc(s["fpow"], 1)

            def f_norm2(b):
                z = slice(2 * b, 2 * b + 2)
                pool.wait_ge(s["fnorm"], b + 1)
                pool.tensor_tensor(q8[:, 1, z], q8[:, 0, z], phalf[:, 0:2], ALU.pow).then_inc(s["fpow"], 1)

            def f_chain(i):
                pool.wait_ge(s["fact"], 2 * i + 2)
                pool.tensor_tensor(q8[:, 8, i:i + 1], q8[:, 7, i:i + 1], phalf[:, 0:1], ALU.pow).then_inc(s["fpow2"], 1)

            def a_ln(b):
                pool.wait_ge(s["aln"], 5 * b + 5)
                pool.tensor_tensor(rstd[:, 2 * b:2 * b + 2], ve[:, 2 * b:2 * b + 2], nhalf[:, 0:2], ALU.pow).then_inc(s["apow"], 1)

            def m_ln(b):
                if b == 0:
                    pool.memset(cwHL, 0.0).then_inc(s["cwz"], 1)
                pool.wait_ge(s["mln"], 5 * b + 5)
                pool.tensor_tensor(rstd[:, 2 * b:2 * b + 2], ve[:, 2 * b:2 * b + 2], nhalf[:, 0:2], ALU.pow).then_inc(s["mpow"], 1)

            def square(p):
                pool.wait_ge(s["raw_done"], p + 1)
                if p >= 2:
                    pool.wait_ge(s["prs"], 2 * (p - 2) + 1)
                pool.tensor_tensor(psq[p % 2], praw[p % 4], praw[p % 4], ALU.mult).then_inc(s["psq_done"], 1)

            def piece_pow(p):
                G_, kind = divmod(p, 4)
                pool.wait_ge(s["prs"], 2 * p + 2)
                if kind >= 2:
                    if G_ >= RING:
                        pool.wait_ge(s["exps"], 2 * GRP * (G_ - RING + 1))
                    dst = rq[:, G_ % RING, :, kind - 2]
                else:
                    dst = rv[:, p % 4, :]
                pool.tensor_tensor(dst, rr[:, p % 4, :], nhalf[:, 0:GRP], ALU.pow).then_inc(s["prv_done"], 1)
                if kind < 2:
                    pool.wait_ge(s["prv_done"], p + 1)
                    pr = praw[p % 4].rearrange("p (a c) -> p a c", a=GRP)
                    pool.tensor_tensor(pr, pr, rv[:, p % 4, :].unsqueeze(2).to_broadcast([P, GRP, P]), ALU.mult
                                       ).then_inc(s["pnorm"], 1)

            def normalise(n):
                pool.wait_ge(s["hrec"], n + 1)
                pool.tensor_tensor(Pb[n % 4], Pb[n % 4], hs[:, n % 4, 6:8].unsqueeze(2).to_broadcast([P, 2, S]), ALU.mult
                                   ).then_inc(s["pnorm_done"], 1)

            def w_split(ft):
                if ft == 0:
                    pool.wait_ge(s["piece_done"], 16 * B)
                    pool.dma_start(esel, d["esel"]).then_inc(s["ld_esel"], 16)

            def expert(m):
                rows = min(P, FALL - ORDER[m][0] * P)
                pool.wait_ge(s["hH_done"], m + 1)
                pool.tensor_tensor(hL[m % 3][0:rows, :], hm[m % 2][0:rows, :], hH[m % 3][0:rows, :].bitcast(F32), ALU.subtract
                                   ).then_inc(s["hL_done"], 1)

            mine = dict(piece=square, piece_pow=piece_pow, scores=normalise, f_stat=f_stat, f_norm=f_norm2, f_peak=f_chain,
                        a_stat=a_ln, m_stat=m_ln, w_split=w_split, cw=expert)
            in_order("pool", mine)


def kernel(**inputs):
    import concourse.bacc as bacc
    from concourse.bass_utils import run_bass_kernel_spmd

    a = {k: np.asarray(v) for k, v in inputs.items()}
    c = np.ascontiguousarray

    def rows(w, n):
        return w.reshape(n, P, -1).transpose(1, 0, 2)

    p, m = np.arange(P)[:, None], np.arange(P)[None, :]
    sel = np.stack([(p % 64 == 8 * j + m // NS) for j in range(8)], 1).astype(np.float32)
    win = np.arange(2 * P - CH)[None, :]
    nwin = (win == P - CH + p // NS).astype(np.float32)
    f = np.arange(FTR * P)[None, :]
    r = np.arange(64)[:, None]
    esel = ((r % 32 == f // F) & (r % 32 < E)).astype(np.float32)

    gate = np.concatenate([a["L1_ffn_w_gate"].reshape(E * F, DM), a["L1_ffn_sw_gate"]])
    up = np.concatenate([a["L1_ffn_w_up"].reshape(E * F, DM), a["L1_ffn_sw_up"]])
    dn = np.concatenate([a["L1_ffn_w_down"].transpose(0, 2, 1).reshape(E * F, DM), a["L1_ffn_sw_down"].T])
    moe = np.zeros((FT, P, 768), np.float32)
    for i in range(FT):
        n = min(P, FALL - i * P)
        s_ = slice(i * P, i * P + n)
        for k in range(2):
            moe[i, :, k * P:k * P + n] = gate[s_, k * P:k * P + P].T
            moe[i, :, 256 + k * P:256 + k * P + n] = up[s_, k * P:k * P + P].T
        moe[i, :n, 512:768] = dn[s_]
    xpw = a["L0_xattn_x_proj_w"]
    reps = [DR + np.arange(P) % NS, DR + NS + np.arange(P) % NS, np.arange(DR)]
    xpT = rows(np.concatenate([xpw[i] for i in reps]).T, 2)
    alog = a["L0_xattn_A_log"].reshape(ST, P).T
    arrays = {
        "x": a["x"], "ctx": a["ctx_1024"],
        "ctxT": c(a["ctx_1024"].reshape(T, DC).T),
        "inT": c(a["L0_xattn_in_proj_w"].T),
        "cw": c(a["L0_xattn_conv_w"].T.reshape(-1)),
        "ec": c(np.stack([a["L0_xattn_conv_b"], a["L0_xattn_dt_proj_b"], a["L0_xattn_D"]], 1).reshape(2, P, 3).transpose(1, 0, 2)),
        "gates": c(np.array([a["g_xattn"][0], a["g_ffn"][0], a["g_xattn"][1], a["g_ffn"][1]])),
        "xp": c(xpT), "dtw": c(a["L0_xattn_dt_proj_w"].T), "acol": c(alog),
        "gqk": c(np.stack([a["L1_xattn_gq"], a["L1_xattn_gk"]], 1)),
        "sel": sel, "nwin": nwin, "ident": np.eye(P, dtype=np.float32),
        "w1": c(rows(a["L0_ffn_w1"].T, 2).reshape(P, -1)), "w2": c(rows(a["L0_ffn_w2"].T, FT0).reshape(P, -1)),
        "Wq": c(rows(a["L1_xattn_Wq"], 2).reshape(P, -1)), "Wk": a["L1_xattn_Wk"],
        "WvT": c(a["L1_xattn_Wv"].reshape(DC, H, P).transpose(2, 1, 0).reshape(P, -1)),
        "Wo": c(rows(a["L1_xattn_Wo"], H).reshape(P, -1)),
        "gw": c(rows(a["L1_ffn_gate_weight"].T, 2)), "iota8": np.tile(np.arange(E, dtype=np.float32), (P, 1)),
        "moe": moe, "esel": esel,
    }
    nc = bacc.Bacc("TRN2", target_bir_lowering=False, num_devices=1)
    d = {n: nc.dram_tensor("in_" + n, v.shape, mybir.dt.from_np(v.dtype), kind="ExternalInput").ap() for n, v in arrays.items()}
    d["out"] = nc.dram_tensor("out", (B, S, DM), F32, kind="ExternalOutput").ap()
    build(nc, d)
    r_ = run_bass_kernel_spmd(nc, [{"in_" + n: v for n, v in arrays.items()}], core_ids=[0])
    return r_.results[0]["out"]
```
